# Optimizing a Trainium2 kernel written in Bass

```python
import numpy as np
import jax
import jax.numpy as jnp

def _softmax(x, axis=-1):
    return jax.nn.softmax(x, axis=axis)

def _gelu(x):
    return jax.nn.gelu(x, approximate=True)

def _silu(x):
    return jax.nn.silu(x)

def _sigmoid(x):
    return jax.nn.sigmoid(x)

def _layernorm(x, axis=-1, eps=1e-05):
    m = jnp.mean(x, axis=axis, keepdims=True)
    v = jnp.var(x, axis=axis, keepdims=True)
    return (x - m) / jnp.sqrt(v + eps)

def _scatter_add(tgt, idx, src, axis=0):
    return tgt.at[idx].add(src)

def _segment_sum(src, seg, n):
    return jax.ops.segment_sum(src, seg, n)
kernel_name = 'mk_adaln_d1_jaxref_r4_9a39cb'

def setup_inputs(seed: int=0):
    np.random.seed(seed)
    _w = jnp.asarray

    def _L0_attn_setup():
        import jax, jax.numpy as jnp
        import numpy as np
        B, S, D = (2, 512, 1024)
        H = 32
        HD = D // H
        THETA = 10000.0

        def _rope_cos_sin(seq_len, head_dim, theta=THETA):
            inv = 1.0 / theta ** (np.arange(0, head_dim, 2)[:head_dim // 2].astype(np.float32) / head_dim)
            t = np.arange(seq_len)
            f = np.outer(t, inv).astype(np.float32)
            return (jnp.asarray(np.cos(f)), jnp.asarray(np.sin(f)))

        def _apply_rotary(x, cos, sin):
            xr = x.astype(jnp.float32).reshape(*x.shape[:-1], HD // 2, 2)
            x0, x1 = (xr[..., 0], xr[..., 1])
            c = cos[None, :, None, :]
            s = sin[None, :, None, :]
            o0 = x0 * c - x1 * s
            o1 = x0 * s + x1 * c
            return jnp.stack((o0, o1), axis=-1).reshape(*x.shape[:-1], HD)
        key = jax.random.key(seed)
        ks = jax.random.split(key, 5)
        std = 0.02
        return {'x': jax.random.normal(ks[0], (B, S, D), dtype=jnp.float32), 'wq': jax.random.normal(ks[1], (D, D), dtype=jnp.float32) * std, 'wk': jax.random.normal(ks[2], (D, D), dtype=jnp.float32) * std, 'wv': jax.random.normal(ks[3], (D, D), dtype=jnp.float32) * std, 'wo': jax.random.normal(ks[4], (D, D), dtype=jnp.float32) * std}
    _L0_attn_in = _L0_attn_setup()

    def _L0_ffn_setup():
        import jax, jax.numpy as jnp
        import numpy as np
        B, S, D, O, E, R = (4, 512, 1024, 1024, 8, 16)
        SCALING = 32.0 / 16.0
        MAX_THRESHOLD = 0.125
        key = jax.random.key(seed)
        ks = jax.random.split(key, 8)
        return {'x': jax.random.normal(ks[0], (B, S, D), jnp.float32), 'W_base': jax.random.normal(ks[1], (O, D), jnp.float32) * (1.0 / np.sqrt(D)), 'b_base': jax.random.normal(ks[2], (O,), jnp.float32) * 0.02, 'W_gate': jax.random.normal(ks[3], (E, D), jnp.float32) * (1.0 / np.sqrt(D)), 'W_thr': jax.random.normal(ks[4], (D,), jnp.float32) * (1.0 / np.sqrt(D)), 'b_thr': jax.random.normal(ks[5], (1,), jnp.float32) * 0.02, 'A_w': jax.random.normal(ks[6], (E, R, D), jnp.float32) * (1.0 / np.sqrt(D)), 'B_w': jax.random.normal(ks[7], (E, O, R), jnp.float32) * (1.0 / np.sqrt(R))}
    _L0_ffn_in = _L0_ffn_setup()
    _L0_c = _w((lambda *s: np.random.randn(*s).astype(np.float32) * 0.05)(2, 1024))
    _L0_wmod = _w((lambda *s: np.random.randn(*s).astype(np.float32) * 0.05)(1024, 6 * 1024) * 1024 ** (-0.5))
    _d = {'L0_attn_x': _L0_attn_in['x'], 'L0_attn_wq': _L0_attn_in['wq'], 'L0_attn_wk': _L0_attn_in['wk'], 'L0_attn_wv': _L0_attn_in['wv'], 'L0_attn_wo': _L0_attn_in['wo'], 'L0_ffn_W_base': _L0_ffn_in['W_base'], 'L0_ffn_b_base': _L0_ffn_in['b_base'], 'L0_ffn_W_gate': _L0_ffn_in['W_gate'], 'L0_ffn_W_thr': _L0_ffn_in['W_thr'], 'L0_ffn_b_thr': _L0_ffn_in['b_thr'], 'L0_ffn_A_w': _L0_ffn_in['A_w'], 'L0_ffn_B_w': _L0_ffn_in['B_w'], 'L0_c': _L0_c, 'L0_wmod': _L0_wmod}
    _x0 = _d['L0_attn_x']
    _d['L0_attn_x'] = jax.random.normal(jax.random.fold_in(jax.random.key(seed), 1), (2, 1024, 1024), dtype=_x0.dtype)
    del _x0
    return _d

def reference(L0_attn_x, L0_attn_wq, L0_attn_wk, L0_attn_wv, L0_attn_wo, L0_ffn_W_base, L0_ffn_b_base, L0_ffn_W_gate, L0_ffn_W_thr, L0_ffn_b_thr, L0_ffn_A_w, L0_ffn_B_w, L0_c, L0_wmod):

    def _L0_attn_ref(x, wq, wk, wv, wo):
        import jax, jax.numpy as jnp
        import numpy as np
        B, S, D = (2, 512, 1024)
        H = 32
        HD = D // H
        THETA = 10000.0

        def _rope_cos_sin(seq_len, head_dim, theta=THETA):
            inv = 1.0 / theta ** (np.arange(0, head_dim, 2)[:head_dim // 2].astype(np.float32) / head_dim)
            t = np.arange(seq_len)
            f = np.outer(t, inv).astype(np.float32)
            return (jnp.asarray(np.cos(f)), jnp.asarray(np.sin(f)))

        def _apply_rotary(x, cos, sin):
            xr = x.astype(jnp.float32).reshape(*x.shape[:-1], HD // 2, 2)
            x0, x1 = (xr[..., 0], xr[..., 1])
            c = cos[None, :, None, :]
            s = sin[None, :, None, :]
            o0 = x0 * c - x1 * s
            o1 = x0 * s + x1 * c
            return jnp.stack((o0, o1), axis=-1).reshape(*x.shape[:-1], HD)
        b, s, d = x.shape
        q = (x @ wq).reshape(b, s, H, HD)
        k = (x @ wk).reshape(b, s, H, HD)
        v = (x @ wv).reshape(b, s, H, HD)
        cos, sin = _rope_cos_sin(s, HD)
        q = _apply_rotary(q, cos, sin)
        k = _apply_rotary(k, cos, sin)
        scale = 1.0 / jnp.sqrt(jnp.float32(HD))
        scores = jnp.einsum('bqhd,bkhd->bhqk', q, k) * scale
        causal = jnp.tril(jnp.ones((s, s), dtype=bool))
        scores = jnp.where(causal[None, None], scores, jnp.finfo(scores.dtype).min)
        probs = jax.nn.softmax(scores, axis=-1)
        out = jnp.einsum('bhqk,bkhd->bqhd', probs, v).reshape(b, s, d)
        return out @ wo

    def _L0_ffn_ref(x, W_base, b_base, W_gate, W_thr, b_thr, A_w, B_w):
        import jax, jax.numpy as jnp
        import numpy as np
        B, S, D, O, E, R = (4, 512, 1024, 1024, 8, 16)
        SCALING = 32.0 / 16.0
        MAX_THRESHOLD = 0.125
        base = jnp.einsum('bsd,od->bso', x, W_base) + b_base
        xf = x.reshape(-1, D)
        gate = jax.nn.softmax(xf @ W_gate.T, axis=-1)
        thr = jax.nn.sigmoid(xf @ W_thr + b_thr[0]) * MAX_THRESHOLD
        adapted = gate - thr[:, None]
        selected = (adapted >= 0).astype(x.dtype)
        w = adapted * selected
        wsum = jnp.sum(w, axis=-1, keepdims=True)
        wsum = jnp.where(wsum == 0, jnp.ones_like(wsum), wsum)
        w = w / wsum
        h = jnp.einsum('nd,erd->ner', xf, A_w)
        moe = jnp.einsum('ner,ne,eor->no', h, w, B_w) * SCALING
        return base + moe.reshape(base.shape)
    x = L0_attn_x
    mod = (_silu(L0_c) @ L0_wmod).reshape(L0_c.shape[0], 6, 1, -1)
    sa, ca, ga, sb, cb, gb = (mod[:, 0], mod[:, 1], mod[:, 2], mod[:, 3], mod[:, 4], mod[:, 5])
    ga = (2 * (ga >= 0) - 1) * jnp.maximum(jnp.abs(ga), 0.25)
    gb = (2 * (gb >= 0) - 1) * jnp.maximum(jnp.abs(gb), 0.25)
    h = _layernorm(x, axis=-1) * (1 + ca) + sa
    x = x + ga * _L0_attn_ref(h, L0_attn_wq, L0_attn_wk, L0_attn_wv, L0_attn_wo)
    h = _layernorm(x, axis=-1) * (1 + cb) + sb
    x = x + gb * _L0_ffn_ref(h, L0_ffn_W_base, L0_ffn_b_base, L0_ffn_W_gate, L0_ffn_W_thr, L0_ffn_b_thr, L0_ffn_A_w, L0_ffn_B_w)
    return x

_drawn_inputs = setup_inputs


def setup_inputs(seed=0):
    import zlib

    import numpy as np

    out = dict(_drawn_inputs(seed))
    spreads = {}
    factors = {'L0_attn_wq': 8.0,
     'L0_attn_wk': 8.0,
     'L0_attn_wv': 5.878,
     'L0_attn_wo': 5.886,
     'L0_ffn_b_base': 38.988,
     'L0_ffn_W_thr': 4.677}
    for name, (base, spread) in spreads.items():
        noise = np.random.default_rng([zlib.crc32(name.encode()), seed]).standard_normal(out[name].shape)
        drawn = base * np.exp(spread * noise) if base else spread * noise
        out[name] = jnp.asarray(drawn.astype(out[name].dtype))
    for name, factor in factors.items():
        out[name] = (out[name] * factor).astype(out[name].dtype)
    return out
```

```python
from contextlib import ExitStack

import concourse.bass as bass
from concourse import mybir

F32 = mybir.dt.float32
F32R = mybir.dt.float32r
BF16 = mybir.dt.bfloat16
ALU = mybir.AluOpType
ACT = mybir.ActivationFunctionType
AX_X = mybir.AxisListType.X

P = 128
B, S, D = 2, 1024, 1024
H, HD = 32, 32
GH = P // HD
G = H // GH
NT = S // P
KT = D // P
BANK = 512
E_, R_ = 8, 16
ER = E_ * R_
EPS = 1e-5
SCALING = 2.0
MAX_THRESHOLD = 0.125
MASKED = -1e30
AGW = ER + 10
MODC = 6 * D // BANK
HU = GH * NT
LAST_STEP = HU + 4


def chunks_of(n):
    kts = n // GH + 1
    return [(k0, min(4, kts - k0)) for k0 in range(0, kts, 4)]


def attention_plan():
    plan, count = {}, {"dve": 0, "act": 0}
    at = 0
    for n in range(HU):
        for c, (k0, m) in enumerate(chunks_of(n)):
            eng = ("dve", "act")[(n + c) % 2] if n < HU // 2 else ("dve", "act")[c]
            plan[n, c] = (eng, count[eng], at, k0, m)
            count[eng] += 1
            at += 1
    return plan, count, at


PLAN, EVAC, TCHUNKS = attention_plan()


def ring_order(with_attention, with_qkv):
    order = []
    for n in range(LAST_STEP):
        if with_qkv and n >= 6 and (n - 6) % 4 == 0:
            order.append(("qk", (n - 6) // 4))
        if with_attention and 0 <= n - 2 < HU:
            order += [("t", n - 2, c) for c in range(len(chunks_of(n - 2)))]
    return order


def adaln_block(nc, x_in, wq, wk, wv, wo, W_base, b_base, W_gate, W_thr, b_thr, A_w, B_w, c_in, wmod,
                rope_c, ident_c, mask_c, sel_c, out):
    attn_dram = nc.dram_tensor("attn_scratch", [D, B * S], F32, kind="Internal").ap()
    mod_dram = nc.dram_tensor("mod_scratch", [B, 6 * D], F32, kind="Internal").ap()
    x_rows = x_in.rearrange("b s d -> (b s) d")
    out_rows = out.rearrange("b s d -> (b s) d")

    outer = ExitStack()
    with outer:
        def sem(name):
            return outer.enter_context(nc.semaphore(name))

        def keep(name, shape, dt):
            return outer.enter_context(nc.sbuf_tensor(name, shape, dt))

        def psum(name, cols):
            return outer.enter_context(nc.psum_tensor(name, [P, cols], F32))

        ps_s = [psum("ps_s0", 2 * BANK), psum("ps_s1", 2 * BANK)]
        ps_t = [psum("ps_t0", BANK), psum("ps_t1", BANK)]
        ps_qkv = psum("ps_qkv", BANK)
        ps_pv = psum("ps_pv", BANK)

        ident = keep("ident", [P, P], F32)
        modcol = keep("modcol", [P, 4 * KT], F32)
        modcol1 = keep("modcol1", [P, 4 * KT], F32)
        mcol_rows = keep("mcol_rows", [4 * KT, P], F32)
        stats = keep("stats", [P, 2, 6], F32)
        mv = keep("mv", [P, 2], F32)
        vareps = keep("vareps", [P, 1], F32)
        minus_half = keep("minus_half", [P, 1], F32)
        eps = keep("eps", [P, 1], F32)
        rstd = keep("rstd", [P, 1], F32)

        phase_a = ExitStack()

        def sb(name, shape, dt):
            return phase_a.enter_context(nc.sbuf_tensor(name, shape, dt))

        hT_hi = sb("hT_hi", [P, KT, S], F32R)
        hT_lo = sb("hT_lo", [P, KT, S], F32R)
        w_raw = sb("w_raw", [P, KT, 3, P], F32)
        w_hi = sb("w_hi", [P, KT, 3 * P], F32R)
        w_lo = sb("w_lo", [P, KT, 3 * P], F32R)
        qkv_sb = sb("qkv_sb", [P, 2, 3 * P], F32)
        qk_rot = sb("qk_rot", [P, 2, 2 * P], F32)
        rope_a = sb("rope_a", [P, 2 * P], F32)
        rope_b = sb("rope_b", [P, 2 * P], F32)
        rope_tab = sb("rope_tab", [P, 2, NT, 2, HD], F32)
        qkT = sb("qkT", [P, 2, 2, S], F32)
        q_stack = sb("q_stack", [3 * HD, GH, S], F32R)
        k_stack = sb("k_stack", [3 * HD, GH, S], F32R)
        v_next = sb("v_next", [P, NT, P], F32)
        v_now = sb("v_now", [P, NT, P], F32)
        probs = sb("probs", [P, GH, S], F32)
        probsT = sb("probsT", [P, NT, GH, P], F32)
        nmax = sb("nmax", [P, HU], F32)
        sums = sb("sums", [P, HU], F32)
        rinv = sb("rinv", [P, GH], F32)
        rinv_wide = sb("rinv_wide", [P, GH, HD], F32)
        rinvT = sb("rinvT", [P, P], F32)
        attnT = sb("attnT", [P, S], F32)
        mask = sb("mask", [P, P], BF16)
        ident16 = sb("ident16", [P, P], BF16)
        sel = sb("sel", [P, B], F32)
        c_rows = sb("c_rows", [B * KT, P], F32)
        c_e = sb("c_e", [P, B * KT], F32)
        c_e1 = sb("c_e1", [P, B * KT], F32)
        c_sig = sb("c_sig", [P, B * KT], F32)
        c_pad = v_now[:, 0:2, :].rearrange("p a (k b) -> p (a k) b", b=HD)
        xb = qkT[:, 0, :, :]
        ht = qkT[:, 1, 0, :].rearrange("p (a n) -> p a n", a=2)
        wm_buf = [probs[:, :, :].rearrange("p h s -> p (h s)").rearrange("p (k n) -> p k n", k=KT),
                  probsT[:, :, :, :].rearrange("p k h q -> p k (h q)")]
        mod_part = attnT[:, 0:BANK]
        mod_row = attnT[0:B, BANK:2 * BANK]
        phase_a.close()

        phase_b = ExitStack()

        def sb2(name, shape, dt):
            return phase_b.enter_context(nc.sbuf_tensor(name, shape, dt))

        wo_hi = sb2("wo_hi", [P, KT, D], F32R)
        wo_lo = sb2("wo_lo", [P, KT, D], F32R)
        wb_hi = sb2("wb_hi", [P, KT, D], F32R)
        wb_lo = sb2("wb_lo", [P, KT, D], F32R)
        ag_hi = sb2("ag_hi", [P, KT, AGW], F32R)
        ag_lo = sb2("ag_lo", [P, KT, AGW], F32R)
        bt_hi = sb2("bt_hi", [P, D], F32R)
        bt_lo = sb2("bt_lo", [P, D], F32R)
        ga = sb2("ga", [P, B, D], F32)
        gb = sb2("gb", [P, B, D], F32)
        bias = sb2("bias", [P, D], F32)
        a_raw = sb2("a_raw", [P, KT, P], F32)
        a_hi = sb2("a_hi", [P, KT, P], F32R)
        a_lo = sb2("a_lo", [P, KT, P], F32R)
        x1 = sb2("x1", [P, 2, D], F32)
        xn = sb2("xn", [P, D], F32)
        h2t = sb2("h2t", [P, BANK], F32)
        h2_hi = sb2("h2_hi", [P, KT, P], F32R)
        h2_lo = sb2("h2_lo", [P, KT, P], F32R)
        gsm = sb2("gsm", [P, 48], F32)
        bthr = sb2("bthr", [P, 2], F32)
        ag_out = sb2("ag_out", [P, AGW], F32)
        hw = sb2("hw", [P, E_, R_], F32)
        hwT_hi = sb2("hwT_hi", [P, P], F32R)
        hwT_lo = sb2("hwT_lo", [P, P], F32R)
        stage = [x1[:, 0, :], x1[:, 1, :], xn[:, :]]
        phase_b.close()

        const_ld = sem("const_ld")
        rope_ld = sem("rope_ld")
        c_t = sem("c_t")
        c_ex = sem("c_ex")
        c_done = sem("c_done")
        wm_ld = [sem("wm_ld0"), sem("wm_ld1")]
        mod_mm = sem("mod_mm")
        mod_ev = sem("mod_ev")
        mod_sum = sem("mod_sum")
        mod_rw = sem("mod_rw")
        mod_st = sem("mod_st")
        mcol_ld = sem("mcol_ld")
        mcol_t = sem("mcol_t")
        mcol = sem("mcol")
        ln_x = [sem("ln_x0"), sem("ln_x1")]
        ln_st = sem("ln_st")
        ln_rs = sem("ln_rs")
        ln_xn = sem("ln_xn")
        ln_tr = sem("ln_tr")
        ln_tt = sem("ln_tt")
        ln_hi = sem("ln_hi")
        ln_lo = sem("ln_lo")
        w_ld = sem("w_ld")
        w_hi_ok = sem("w_hi_ok")
        w_lo_ok = sem("w_lo_ok")
        qkv_mm = sem("qkv_mm")
        qkv_cp = sem("qkv_cp")
        roped = sem("roped")
        qk_t = sem("qk_t")
        qk_hi = sem("qk_hi")
        qk_lo = sem("qk_lo")
        stacked = [sem("stacked0"), sem("stacked1")]
        v_ok = sem("v_ok")
        s_ok = sem("s_ok")
        max_ok = sem("max_ok")
        exp_ok = sem("exp_ok")
        t_ok = sem("t_ok")
        ev = {"dve": sem("ev_dve"), "act": sem("ev_act")}
        rinv_ok = sem("rinv_ok")
        pv_ok = sem("pv_ok")
        rinvT_ok = sem("rinvT_ok")
        at_ok = sem("at_ok")
        at_st = sem("at_st")
        pool_seq = sem("pool_seq")
        dve_seq = sem("dve_seq")
        inv_ok = sem("inv_ok")
        pool_half = sem("pool_half")
        pool_ve = sem("pool_ve")
        st_ld = [sem(f"st_ld{i}") for i in range(3)]
        st_t = sem("st_t")
        st_hi = sem("st_hi")
        st_lo = sem("st_lo")
        rows_ld = sem("rows_ld")
        gate_tmp = sem("gate_tmp")
        rows_ok = sem("rows_ok")
        mcol2_ld = sem("mcol2_ld")
        mcol2_t = sem("mcol2_t")
        a_ld = sem("a_ld")
        a_hi_ok = sem("a_hi_ok")
        a_lo_ok = sem("a_lo_ok")
        x_ld = [sem("x_ld0"), sem("x_ld1")]
        wo_ok = sem("wo_ok")
        gated = sem("gated")
        x1_ok = sem("x1_ok")
        bn_ok = sem("bn_ok")
        b_st = sem("b_st")
        b_ve = sem("b_ve")
        b_rs = sem("b_rs")
        xn_ok = sem("xn_ok")
        xt_ok = sem("xt_ok")
        h2t_ok = sem("h2t_ok")
        h2_hi_ok = sem("h2_hi_ok")
        h2_lo_ok = sem("h2_lo_ok")
        ag_ok = sem("ag_ok")
        ag_cp = sem("ag_cp")
        gate_max = sem("gate_max")
        gate_exp = sem("gate_exp")
        gate_seq = sem("gate_seq")
        hw_ok = sem("hw_ok")
        hwT_ok = sem("hwT_ok")
        hwT_hi_ok = sem("hwT_hi_ok")
        hwT_lo_ok = sem("hwT_lo_ok")
        y_ok = sem("y_ok")
        y_ev = sem("y_ev")
        y_gated = sem("y_gated")
        out_ok = sem("out_ok")
        out_st = sem("out_st")
        stack_groups = 6 * GH * 16

        seq = {"dve": 0, "pool": 0}

        items = [("wo", k) for k in range(KT)] + [("ag", 0), ("ag", 1), ("bt", 0)] + [("wb", o) for o in range(KT)]
        n_dma = {"bt": E_}
        loaded, units_to, unit = [], [], 0
        for kind, k in items:
            n = 1 + AGW - ER - E_ if (kind, k) == ("ag", 1) else n_dma.get(kind, 1)
            loaded.append((loaded[-len(stage)] if len(loaded) >= len(stage) else 0) + 16 * n)
            unit += 1 if kind == "wo" else 2
            units_to.append(unit)
        UNITS = unit
        GATE_STEPS = 8

        def piece(kind, k, half):
            ks = slice(4 * half, 4 * half + 4)
            if kind == "wb":
                return tuple(w[:, ks, k * P:(k + 1) * P] for w in (wb_hi, wb_lo))
            if kind == "bt":
                return tuple(w[:, half * BANK:(half + 1) * BANK].rearrange("p (k n) -> p k n", k=4)
                             for w in (bt_hi, bt_lo))
            return tuple(w[:, ks, slice(0, ER) if k == 0 else slice(ER, AGW)] for w in (ag_hi, ag_lo))

        def piece_cols(kind, k):
            return AGW - ER if (kind, k) == ("ag", 1) else P

        def turned():
            n = 0
            for i, (kind, k) in enumerate(items):
                if kind != "wo":
                    for half in range(2):
                        yield n, i, kind, k, half, units_to[i] - 2 + half
                        n += 1

        def tile_of(hp, e):
            return hp * 2 + e

        def after(hp, e):
            return (hp, 1) if e == 0 else (hp + 1, 0)

        def tile_loops(eng, body):
            half = NT // 2
            for b in range(B):
                with eng.Fori(0, half - 1) as p:
                    for e in range(2):
                        body(p + b * half, e, b, b, True, True)
                hp = (b + 1) * half - 1
                for e in range(2):
                    i = 2 * hp + e
                    body(hp, e, b, min(B - 1, (i + 1) // NT), i + 1 < B * NT, i + 2 < B * NT)

        def phase_b_sync(sp):
            for i, (kind, k) in enumerate(items):
                if i >= len(stage):
                    sp.wait_ge(st_lo, units_to[i - len(stage)])
                to = stage[i % len(stage)]
                if kind == "wo":
                    sp.dma_start(to, wo[k * P:(k + 1) * P, :]).then_inc(st_ld[i % len(stage)], 16)
                elif kind == "wb":
                    sp.dma_start(to, W_base[k * P:(k + 1) * P, :]).then_inc(st_ld[i % len(stage)], 16)
                elif kind == "bt":
                    v = to.rearrange("p (t e r) -> p t e r", t=KT, e=E_)
                    for e in range(E_):
                        sp.dma_start(v[:, :, e, :], B_w[e].rearrange("(t p) r -> p t r", p=P)).then_inc(st_ld[i % len(stage)], 16)
                elif k == 0:
                    sp.dma_start(to, A_w.rearrange("e r d -> (e r) d")).then_inc(st_ld[i % len(stage)], 16)
                else:
                    sp.dma_start(to[0:E_, :], W_gate).then_inc(st_ld[i % len(stage)], 16)
                    for r in range(E_, AGW - ER):
                        sp.dma_start(to[r:r + 1, :], W_thr.rearrange("(a d) -> a d", a=1)).then_inc(st_ld[i % len(stage)], 16)
                if i == 2:
                    for b in range(B):
                        sp.dma_start(ga[:, b, :], mod_dram[b:b + 1, 2 * D:3 * D].broadcast_to([P, D])).then_inc(rows_ld, 16)
                        sp.dma_start(gb[:, b, :], mod_dram[b:b + 1, 5 * D:6 * D].broadcast_to([P, D])).then_inc(rows_ld, 16)
                        sp.dma_start(mcol_rows[b * 16:(b + 1) * 16, :], mod_dram[b, 3 * D:5 * D].rearrange(
                            "(r p) -> r p", p=P)).then_inc(mcol2_ld, 16)
                    sp.dma_start(bias[:, :], b_base.rearrange("(a d) -> a d", a=1).broadcast_to([P, D])).then_inc(rows_ld, 16)
                    sp.dma_start(bthr[:, 0:1], b_thr.rearrange("(a d) -> a d", a=1).broadcast_to([P, 1])).then_inc(rows_ld, 16)

            def load_a(i):
                sp.dma_start(a_raw[:, :, :], attn_dram.rearrange("(k p) t -> p k t", p=P)[
                    :, :, bass.ds(i * P, P)]).then_inc(a_ld, 16)

            def load_x(i, e):
                sp.dma_start(x1[:, e, :], x_rows[bass.ds(i * P, P), :]).then_inc(x_ld[e], 16)

            def body(hp, e, b, bj, has_next, has_next2):
                i = tile_of(hp, e)
                if has_next2:
                    sp.wait_ge(a_lo_ok, i + 2)
                    load_a(i + 2)
                sp.wait_ge(out_ok, i + 2)
                sp.dma_start(out_rows[bass.ds(i * P, P), :], x1[:, e, :]).then_inc(out_st, 16)
                if has_next2:
                    sp.wait_ge(out_st, 16 * i + 16)
                    load_x(i + 2, e)

            sp.wait_ge(rows_ok, 1)
            load_a(0)
            sp.wait_ge(st_lo, UNITS)
            load_x(0, 0)
            load_x(1, 1)
            sp.wait_ge(a_lo_ok, 1)
            load_a(1)
            tile_loops(sp, body)
            sp.wait_ge(out_st, 16 * B * NT)

        def phase_b_tensor(pe):
            pe.wait_ge(mcol2_ld, 32)
            pe.wait_ge(at_ok, 8 * B * G + 1)
            pe.transpose(ps_pv[:, 0:4 * KT], mcol_rows[:, :], ident[0:4 * KT, 0:4 * KT]).then_inc(mcol2_t, 1)
            for n, i, kind, k, half, u in turned():
                if n == 0:
                    pe.wait_ge(ev["dve"], EVAC["dve"] * B * G + 1)
                    pe.wait_ge(ev["act"], EVAC["act"] * B * G + 1)
                if half == 0:
                    pe.wait_ge(st_ld[i % len(stage)], loaded[i])
                if n >= 2:
                    pe.wait_ge(st_lo, u - 1)
                rows = piece_cols(kind, k)
                for j in range(4):
                    kt = 4 * half + j
                    mm = pe.transpose(ps_t[n % 2][:, j * rows:(j + 1) * rows],
                                      stage[i % len(stage)][0:rows, kt * P:(kt + 1) * P], ident[0:rows, 0:rows])
                mm.then_inc(st_t, 1)

            def three(out_ap, hi, lo, w_hi_ap, w_lo_ap, first, final):
                pe.matmul(out_ap, hi, w_hi_ap, start=first, stop=False)
                pe.matmul(out_ap, hi, w_lo_ap, start=False, stop=False)
                return pe.matmul(out_ap, lo, w_hi_ap, start=False, stop=final)

            def project(j):
                pe.wait_ge(a_hi_ok, j + 1)
                pe.wait_ge(a_lo_ok, j + 1)
                if not isinstance(j, int) or j:
                    pe.wait_ge(gated, j)
                for c in range(0, D, BANK):
                    for kt in range(KT):
                        mm = three(ps_s[0][:, c:c + BANK], a_hi[:, kt, :], a_lo[:, kt, :], wo_hi[:, kt, c:c + BANK],
                                   wo_lo[:, kt, c:c + BANK], kt == 0, kt == KT - 1)
                mm.then_inc(wo_ok, 1)

            def turn_xn(j):
                pe.wait_ge(xn_ok, j + 1)
                if not isinstance(j, int) or j:
                    pe.wait_ge(h2t_ok, 2 * j)
                for half in range(2):
                    for q in range(4):
                        kt = 4 * half + q
                        mm = pe.transpose(ps_t[half][:, q * P:(q + 1) * P], xn[:, kt * P:(kt + 1) * P], ident[:, :])
                    mm.then_inc(xt_ok, 1)

            def body(hp, e, b, bj, has_next, has_next2):
                i = tile_of(hp, e)
                if has_next:
                    project(i + 1)
                pe.wait_ge(h2_hi_ok, 2 * i + 2)
                pe.wait_ge(h2_lo_ok, 2 * i + 2)
                pe.wait_ge(ag_cp, i + 1)
                for kt in range(KT):
                    mm = three(ps_qkv[:, 0:AGW], h2_hi[:, kt, :], h2_lo[:, kt, :], ag_hi[:, kt, :], ag_lo[:, kt, :],
                               kt == 0, kt == KT - 1)
                mm.then_inc(ag_ok, 1)
                pe.wait_ge(y_ev, i + 1)
                for c in range(0, D, BANK):
                    for kt in range(KT):
                        three(ps_s[1][:, c:c + BANK], h2_hi[:, kt, :], h2_lo[:, kt, :], wb_hi[:, kt, c:c + BANK],
                              wb_lo[:, kt, c:c + BANK], kt == 0, False)
                pe.wait_ge(hw_ok, i + 2)
                pe.wait_ge(hwT_lo_ok, i + 1)
                pe.transpose(ps_pv[:, 0:P], hw[:, :, :].rearrange("p e r -> p (e r)"), ident[:, :]).then_inc(hwT_ok, 1)
                if has_next:
                    turn_xn(i + 1)
                pe.wait_ge(hwT_hi_ok, i + 1)
                pe.wait_ge(hwT_lo_ok, i + 2)
                for c in range(0, D, BANK):
                    mm = three(ps_s[1][:, c:c + BANK], hwT_hi[:, :], hwT_lo[:, :], bt_hi[:, c:c + BANK],
                               bt_lo[:, c:c + BANK], False, True)
                mm.then_inc(y_ok, 1)

            pe.wait_ge(st_hi, UNITS)
            pe.wait_ge(st_lo, UNITS)
            project(0)
            turn_xn(0)
            tile_loops(pe, body)

        def phase_b_scalar(act):
            halves = list(turned())
            for i, (kind, k) in enumerate(items):
                if kind == "wo":
                    act.wait_ge(st_ld[i % len(stage)], loaded[i])
                    act.copy(wo_hi[:, k, :], stage[i % len(stage)]).then_inc(st_hi, 1)
            for n, i, kind, k, half, u in halves:
                rows = piece_cols(kind, k)
                act.wait_ge(st_t, n + 1)
                act.copy(piece(kind, k, half)[0], ps_t[n % 2][:, 0:4 * rows].rearrange(
                    "p (k n) -> p k n", k=4)).then_inc(st_hi, 1)

            def split_a(i):
                act.wait_ge(a_ld, 16 * i + 16)
                if not isinstance(i, int) or i:
                    act.wait_ge(wo_ok, i)
                act.copy(a_hi[:, :, :], a_raw[:, :, :]).then_inc(a_hi_ok, 1)

            def split_h(j):
                for half in range(2):
                    act.wait_ge(h2t_ok, 2 * j + half + 1)
                    act.copy(h2_hi[:, 4 * half:4 * half + 4, :],
                             h2t[:, :].rearrange("p (k t) -> p k t", k=4)).then_inc(h2_hi_ok, 1)

            def body(hp, e, b, bj, has_next, has_next2):
                i = tile_of(hp, e)
                act.wait_ge(ag_cp, i + 2)
                act.activation(gsm[:, 9:10], ag_out[:, ER + E_:ER + E_ + 1], ACT.Exp, bias=bthr[:, 1:2],
                               scale=-1.0).then_inc(gate_exp, 1)
                act.wait_ge(gate_max, i + 1)
                act.activation(gsm[:, 0:E_], ag_out[:, ER:ER + E_], ACT.Exp, bias=gsm[:, 8:9], scale=1.0,
                               accum_out=gsm[:, 10:11]).then_inc(gate_exp, 1)
                if has_next2:
                    split_a(i + 2)
                act.wait_ge(hwT_ok, i + 1)
                act.copy(hwT_hi[:, :], ps_pv[:, 0:P]).then_inc(hwT_hi_ok, 1)
                if has_next:
                    split_h(i + 1)

            split_a(0)
            split_a(1)
            split_h(0)
            tile_loops(act, body)

        def phase_b_vector(dve):
            dve.sem_inc(ag_cp, 1)
            dve.sem_inc(hw_ok, 1)
            dve.sem_inc(hwT_lo_ok, 1)
            dve.sem_inc(y_ev, 1)
            dve.wait_ge(mcol2_t, 1)
            dve.tensor_copy(modcol[:, :], ps_pv[:, 0:4 * KT])
            dve.tensor_scalar(modcol1[:, :], ps_pv[:, 0:4 * KT], 1.0, None, ALU.add)
            halves = list(turned())
            for i, (kind, k) in enumerate(items):
                if kind == "wo":
                    dve.wait_ge(st_hi, i + 1)
                    dve.tensor_tensor(wo_lo[:, k, :], stage[i % len(stage)], wo_hi[:, k, :].bitcast(F32),
                                      ALU.subtract).then_inc(st_lo, 1)
            for n, i, kind, k, half, u in halves:
                rows = piece_cols(kind, k)
                hi, lo = piece(kind, k, half)
                dve.wait_ge(st_hi, u + 1)
                dve.tensor_tensor(lo, ps_t[n % 2][:, 0:4 * rows].rearrange("p (k n) -> p k n", k=4), hi.bitcast(F32),
                                  ALU.subtract).then_inc(st_lo, 1)
            dve.wait_ge(rows_ld, 16 * (2 * B + 2))
            sign, size = h2t[:, :], a_raw[:, 0:4, :].rearrange("p k t -> p (k t)")
            n = 0
            for g in (ga, gb):
                for b in range(B):
                    for c in range(0, D, BANK):
                        gc = g[:, b, c:c + BANK]
                        for o in (lambda: dve.tensor_scalar(sign, gc, 0.0, 2.0, ALU.is_ge, ALU.mult),
                                  lambda: dve.scalar_tensor_tensor(size, sign, -1.0, gc, ALU.add, ALU.mult),
                                  lambda: dve.tensor_scalar(sign, sign, -1.0, None, ALU.add),
                                  lambda: dve.scalar_tensor_tensor(gc, size, 0.25, sign, ALU.max, ALU.mult)):
                            n += 1
                            o().then_inc(gate_tmp, 1)
                            dve.wait_ge(gate_tmp, n)
            dve.tensor_scalar(bthr[:, 1:2], bthr[:, 0:1], -1.0, None, ALU.mult).then_inc(rows_ok, 1)
            dve.wait_ge(rows_ok, 1)

            def residual(j, hp, e, b):
                dve.wait_ge(wo_ok, j + 1)
                if not isinstance(j, int) or j:
                    dve.wait_ge(xt_ok, 2 * j)
                    dve.wait_ge(out_ok, j)
                dve.tensor_tensor(xn[:, :], ps_s[0][:, :], ga[:, b, :], ALU.mult).then_inc(gated, 1)
                dve.wait_ge(gated, j + 1)
                dve.wait_ge(x_ld[e], 16 * hp + 16)
                dve.tensor_tensor(x1[:, e, :], x1[:, e, :], xn[:, :], ALU.add).then_inc(x1_ok, 1)
                dve.wait_ge(x1_ok, j + 1)
                for c in range(2):
                    st = dve.bn_stats(stats[:, c, :], x1[:, e, c * BANK:(c + 1) * BANK])
                st.then_inc(bn_ok, 1)
                own(dve)
                dve.wait_ge(bn_ok, j + 1)
                dve.bn_aggr(mv[:, :], stats[:, :, :].rearrange("p a s -> p (a s)")).then_inc(b_st, 1)

            def norm(j, e):
                dve.wait_ge(b_rs, j + 1)
                dve.tensor_scalar(xn[:, :], x1[:, e, :], mv[:, 0:1], rstd[:, 0:1], ALU.subtract,
                                  ALU.mult).then_inc(xn_ok, 1)

            def modulate(j, b):
                for half in range(2):
                    dve.wait_ge(xt_ok, 2 * j + half + 1)
                    if half or not isinstance(j, int) or j:
                        dve.wait_ge(h2_hi_ok, 2 * j + half)
                        dve.wait_ge(h2_lo_ok, 2 * j + half)
                    for q in range(4):
                        kt = 4 * half + q
                        o = dve.tensor_scalar(h2t[:, q * P:(q + 1) * P], ps_t[half][:, q * P:(q + 1) * P],
                                              modcol1[:, b * 16 + 8 + kt:b * 16 + 9 + kt],
                                              modcol[:, b * 16 + kt:b * 16 + kt + 1], ALU.mult, ALU.add)
                    o.then_inc(h2t_ok, 1)

            def route(i):
                done = [0]

                def then(ins):
                    done[0] += 1
                    ins.then_inc(gate_seq, 1)
                    dve.wait_ge(gate_seq, i * GATE_STEPS + done[0])

                ex, nm, ue, sm = gsm[:, 0:E_], gsm[:, 8:9], gsm[:, 9:10], gsm[:, 10:11]
                rs, u1, th, t8, ws, wd, rw = (gsm[:, 11 + q:12 + q] for q in range(7))
                ad, w, wn = gsm[:, 18:26], gsm[:, 26:34], gsm[:, 34:42]
                dve.wait_ge(ag_ok, i + 1)
                dve.tensor_copy(ag_out[:, :], ps_qkv[:, 0:AGW]).then_inc(ag_cp, 1)
                dve.wait_ge(ag_cp, i + 2)
                dve.tensor_reduce(nm, ag_out[:, ER:ER + E_], AX_X, ALU.max, negate=True).then_inc(gate_max, 1)
                dve.wait_ge(gate_exp, 2 * i + 1)
                then(dve.tensor_scalar(u1, ue, 1.0, None, ALU.add))
                then(dve.reciprocal(th, u1))
                dve.tensor_scalar(t8, th, MAX_THRESHOLD, None, ALU.mult)
                dve.wait_ge(gate_exp, 2 * i + 2)
                then(dve.reciprocal(rs, sm))
                then(dve.tensor_scalar(ad, ex, rs, t8, ALU.mult, ALU.subtract))
                then(dve.tensor_scalar(w, ad, 0.0, 0.0, ALU.max, ALU.add, accum_out=ws))
                then(dve.scalar_tensor_tensor(wd, ws, 0.0, ws, ALU.is_equal, ALU.add))
                then(dve.reciprocal(rw, wd))
                then(dve.tensor_scalar(wn, w, rw, SCALING, ALU.mult, ALU.mult))
                assert done[0] == GATE_STEPS
                dve.tensor_tensor(hw[:, :, :], ag_out[:, 0:ER].rearrange("p (e r) -> p e r", e=E_),
                                  wn.unsqueeze(2).broadcast_to([P, E_, R_]), ALU.mult).then_inc(hw_ok, 1)

            def body(hp, e, b, bj, has_next, has_next2):
                i = tile_of(hp, e)
                if has_next:
                    residual(i + 1, *after(hp, e), bj)
                route(i)
                if has_next:
                    norm(i + 1, 1 - e)
                dve.wait_ge(hwT_hi_ok, i + 1)
                dve.tensor_tensor(hwT_lo[:, :], ps_pv[:, 0:P], hwT_hi[:, :].bitcast(F32), ALU.subtract)\
                   .then_inc(hwT_lo_ok, 1)
                if has_next:
                    modulate(i + 1, bj)
                dve.wait_ge(out_ok, i + 1)
                dve.wait_ge(y_ok, i + 1)
                dve.tensor_tensor(xn[:, :], ps_s[1][:, :], bias[:, :], ALU.add).then_inc(y_ev, 1)

            residual(0, 0, 0, 0)
            norm(0, 0)
            modulate(0, 0)
            tile_loops(dve, body)

        def phase_b_gpsimd(pool):
            pool.sem_inc(out_ok, 1)

            def rsqrt(j):
                pool.wait_ge(b_st, j + 1)
                pool.tensor_tensor(vareps[:, :], mv[:, 1:2], eps[:, :], ALU.add).then_inc(b_ve, 1)
                pool.wait_ge(b_ve, j + 1)
                pool.tensor_tensor(rstd[:, :], vareps[:, :], minus_half[:, :], ALU.pow).then_inc(b_rs, 1)

            def split_a(i):
                pool.wait_ge(a_hi_ok, i + 1)
                pool.tensor_tensor(a_lo[:, :, :], a_raw[:, :, :], a_hi[:, :, :].bitcast(F32),
                                   ALU.subtract).then_inc(a_lo_ok, 1)

            def split_h(j):
                for half in range(2):
                    pool.wait_ge(h2_hi_ok, 2 * j + half + 1)
                    hi = h2_hi[:, 4 * half:4 * half + 4, :]
                    pool.tensor_tensor(h2_lo[:, 4 * half:4 * half + 4, :], h2t[:, :].rearrange("p (k t) -> p k t", k=4),
                                       hi.bitcast(F32), ALU.subtract).then_inc(h2_lo_ok, 1)

            def body(hp, e, b, bj, has_next, has_next2):
                i = tile_of(hp, e)
                if has_next:
                    rsqrt(i + 1)
                if has_next2:
                    split_a(i + 2)
                if has_next:
                    split_h(i + 1)
                pool.wait_ge(y_ev, i + 2)
                pool.tensor_tensor(xn[:, :], xn[:, :], gb[:, b, :], ALU.mult).then_inc(y_gated, 1)
                pool.wait_ge(y_gated, i + 1)
                pool.tensor_tensor(x1[:, e, :], x1[:, e, :], xn[:, :], ALU.add).then_inc(out_ok, 1)

            split_a(0)
            rsqrt(0)
            split_a(1)
            split_h(0)
            tile_loops(pool, body)

        def own(eng):
            eng.wait_ge(c_t, 1)

        block = outer.enter_context(nc.Block())

        @block.sync
        def _(sp):
            sp.dma_start(ident[:, :], ident_c).then_inc(const_ld, 16)
            sp.dma_start(c_rows[:, :], c_in.rearrange("b (k p) -> (b k) p", p=P)).then_inc(const_ld, 16)
            sp.dma_start(rinvT[:, :], mask_c).then_inc(const_ld, 16)
            sp.dma_start(sel[:, :], sel_c).then_inc(const_ld, 16)

            def load_wmod(k):
                if k >= 2:
                    sp.wait_ge(mod_mm, k - 1)
                sp.dma_start(wm_buf[k % 2], wmod.rearrange("(k p) n -> p k n", p=P)[
                    :, :, k * BANK:(k + 1) * BANK]).then_inc(wm_ld[k % 2], 16)

            def load_x(b, tt):
                n = b * NT + tt
                if tt >= 2:
                    sp.wait_ge(ln_tr, 2 * (n - 1))
                elif b:
                    sp.wait_ge(stacked[0], stack_groups * G * b)
                    sp.wait_ge(stacked[1], stack_groups * G * b)
                sp.dma_start(xb[:, tt % 2, :], x_rows[n * P:(n + 1) * P, :]).then_inc(ln_x[tt % 2], 16)

            def load_w(it, g):
                if not isinstance(it, int) or it > 0:
                    sp.wait_ge(w_hi_ok, 2 * it)
                    sp.wait_ge(w_lo_ok, 2 * it)
                for j, w in enumerate((wq, wk, wv)):
                    sp.dma_start(w_raw[:, :, j, :], w.rearrange("(k p) n -> p k n", p=P)[
                        :, :, bass.ds(g * P, P)]).then_inc(w_ld, 16)

            def stack(it, half):
                if half == 0 and (not isinstance(it, int) or it > 0):
                    sp.wait_ge(s_ok, HU * it)
                sp.wait_ge(qk_hi, 8 * it + 4 * (half + 1))
                sp.wait_ge(qk_lo, 8 * it + 4 * (half + 1))
                cols = slice(half * (S // 2), (half + 1) * (S // 2))
                for h in range(GH):
                    rows = slice(h * HD, (h + 1) * HD)
                    for dst, j, parts in ((q_stack, 0, (0, 1, 0)), (k_stack, 1, (0, 0, 1))):
                        for r, part in enumerate(parts):
                            sp.dma_start(dst[r * HD:(r + 1) * HD, h, cols].bitcast(F32),
                                         qkT[rows, part, j, cols]).then_inc(stacked[half], 16)

            def store_attn(it, b, g):
                sp.wait_ge(at_ok, 8 * it + 8 + 1)
                sp.dma_start(attn_dram[bass.ds(g * P, P), b * S:(b + 1) * S], attnT[:, :]).then_inc(at_st, 16)

            def store_mod(k):
                sp.wait_ge(mod_rw, k + 1)
                sp.dma_start(mod_dram[:, k * BANK:(k + 1) * BANK], mod_row).then_inc(mod_st, 16)

            load_wmod(0)
            load_wmod(1)
            load_x(0, 0)
            load_x(0, 1)
            load_w(0, 0)
            load_wmod(2)
            sp.dma_start(rope_tab[:, :, :, :, :], rope_c).then_inc(rope_ld, 16)
            load_wmod(3)
            for k in range(4):
                store_mod(k)
            sp.wait_ge(mod_st, 16 * 4)
            for b in range(B):
                sp.dma_start(mcol_rows[b * 16:(b + 1) * 16, :], mod_dram[b, 0:2 * D].rearrange(
                    "(r p) -> r p", p=P)).then_inc(mcol_ld, 16)
            load_wmod(4)
            load_wmod(5)
            for tt in range(2, NT):
                load_x(0, tt)
            load_w(1, 1)
            for k in range(4, MODC):
                if k + 2 < MODC:
                    load_wmod(k + 2)
                store_mod(k)
            for b in range(B):
                it0 = b * G
                stack(it0, 0)
                stack(it0, 1)
                with sp.Fori(0, G - 2) as g:
                    load_w(g + (it0 + 2), g + 2)
                    stack(g + (it0 + 1), 0)
                    stack(g + (it0 + 1), 1)
                    store_attn(g + it0, b, g)
                if b == 0:
                    load_w(G, 0)
                stack(it0 + G - 1, 0)
                stack(it0 + G - 1, 1)
                store_attn(it0 + G - 2, b, G - 2)
                if b == 0:
                    for tt in range(NT):
                        load_x(1, tt)
                    load_w(G + 1, 1)
                store_attn(it0 + G - 1, b, G - 1)
            sp.wait_ge(at_st, 16 * (B * G + 1))
            sp.wait_ge(mod_st, 16 * MODC)
            phase_b_sync(sp)

        @block.tensor
        def _(pe):
            pe.wait_ge(const_ld, 64)
            pe.transpose(ps_pv[:, 0:B * KT], c_rows[:, :], ident[0:B * KT, 0:B * KT]).then_inc(c_t, 1)

            def mod_chunk(k):
                if k == 0:
                    pe.wait_ge(c_done, 2)
                pe.wait_ge(wm_ld[k % 2], 16 * (k // 2 + 1))
                if k:
                    pe.wait_ge(mod_ev, k)
                for kt in range(KT):
                    j = kt % 4
                    mm = pe.matmul(ps_s[0][j * HD:(j + 1) * HD, 0:BANK], c_pad[:, kt, :], wm_buf[k % 2][:, kt, :],
                                   start=(kt < 4), stop=(kt >= 4), tile_position=(0, j * HD))
                mm.then_inc(mod_mm, 1)

            def mod_rows(k):
                pe.wait_ge(mod_ev, k + 1)
                if k:
                    pe.wait_ge(mod_rw, k)
                pe.matmul(ps_pv[0:B, 0:BANK], sel[:, :], mod_part, start=True, stop=True).then_inc(mod_sum, 1)

            def ln_half(b, tt, half):
                n = b * NT + tt
                pe.wait_ge(ln_xn, n + 1)
                if n or half:
                    pe.wait_ge(ln_tt, 2 * n + half)
                if b and tt == 0 and half == 0:
                    pe.wait_ge(qkv_cp, 8 * G * b)
                for j in range(4):
                    kt = 4 * half + j
                    mm = pe.transpose(ps_qkv[:, j * P:(j + 1) * P], xb[:, tt % 2, kt * P:(kt + 1) * P], ident[:, :])
                mm.then_inc(ln_tr, 1)

            def qkv(it, tt, kts, b=None):
                if kts[0] == 0:
                    if b is not None:
                        pe.wait_ge(ln_hi, 2 * (b * NT + tt + 1))
                        pe.wait_ge(ln_lo, 2 * (b * NT + tt + 1))
                    if not isinstance(it, int) or it or tt:
                        pe.wait_ge(qkv_cp, 8 * it + tt)
                    if b is not None and tt == 0:
                        pe.wait_ge(ln_tt, 2 * NT * (b + 1))
                for kt in kts:
                    if tt == 0 and kt % 4 == 0:
                        pe.wait_ge(w_hi_ok, 2 * it + kt // 4 + 1)
                        pe.wait_ge(w_lo_ok, 2 * it + kt // 4 + 1)
                    hh, hl = (h[:, kt, tt * P:(tt + 1) * P] for h in (hT_hi, hT_lo))
                    pe.matmul(ps_qkv[:, 0:3 * P], hh, w_hi[:, kt, :], start=(kt == 0), stop=False)
                    pe.matmul(ps_qkv[:, 0:3 * P], hh, w_lo[:, kt, :], start=False, stop=False)
                    mm = pe.matmul(ps_qkv[:, 0:3 * P], hl, w_hi[:, kt, :], start=False, stop=(kt == KT - 1))
                if kts[-1] == KT - 1:
                    mm.then_inc(qkv_mm, 1)

            def ring_free(order, r, it, it_q):
                if r < 2:
                    if not isinstance(it, int) or it:
                        pe.wait_ge(ev["dve"], EVAC["dve"] * it + 1)
                        pe.wait_ge(ev["act"], EVAC["act"] * it + 1)
                    pe.wait_ge(qk_lo, 8 * it + 8)
                    return
                was = order[r - 2]
                if was[0] == "qk":
                    pe.wait_ge(qk_lo, 8 * it_q + was[1] + 1)
                else:
                    eng, num = PLAN[was[1:]][:2]
                    pe.wait_ge(ev[eng], EVAC[eng] * it + num + 2)

            def qk_transpose(it_q, tt, bank):
                pe.wait_ge(roped, 16 * it_q + 2 * tt + 2)
                pe.transpose(bank[:, 0:P], qk_rot[:, tt % 2, 0:P], ident[:, :])
                pe.transpose(bank[:, P:2 * P], qk_rot[:, tt % 2, P:2 * P], ident[:, :]).then_inc(qk_t, 1)

            def scores(it, n):
                qt, h = n // GH, n % GH
                if n == 0:
                    pe.wait_ge(stacked[0], stack_groups * (it + 1))
                if n == HU // 2:
                    pe.wait_ge(stacked[1], stack_groups * (it + 1))
                pe.wait_ge(exp_ok, HU * it + n + 1)
                w = (qt + 1) * P
                for c0 in range(0, w, BANK):
                    c1 = min(w, c0 + BANK)
                    pe.matmul(ps_s[n % 2][:, c0:c1], q_stack[:, h, qt * P:(qt + 1) * P], k_stack[:, h, c0:c1],
                              start=True, stop=(c1 < w))
                pe.matmul(ps_s[n % 2][:, w - P:w], ident16[:, :], mask[:, :], start=False, stop=True).then_inc(s_ok, 1)

            def turn(it, it_q, n, order, r):
                h = n % GH
                pe.wait_ge(exp_ok, HU * it + n + 1 + 2)
                for c, (k0, m) in enumerate(chunks_of(n)):
                    ring_free(order, r, it, it_q)
                    for j in range(m):
                        mm = pe.transpose(ps_t[r % 2][:, j * P:(j + 1) * P], probs[:, h, (k0 + j) * P:(k0 + j + 1) * P],
                                          ident[:, :])
                    mm.then_inc(t_ok, 1)
                    r += 1
                return r

            def values(it, u):
                for eng in ("dve", "act"):
                    done = max(num for (n, c), (e, num, *_) in PLAN.items() if e == eng and n // GH <= u)
                    pe.wait_ge(ev[eng], EVAC[eng] * it + done + 2)
                if u == 0:
                    pe.wait_ge(v_ok, it + 1)
                pe.wait_ge(at_ok, 8 * it + u + 1)
                pe.wait_ge(rinv_ok, 8 * it + u + 1)
                for kt in range(u + 1):
                    for h in range(GH):
                        pe.matmul(ps_pv[h * HD:(h + 1) * HD, 0:P], v_now[:, kt, h * HD:(h + 1) * HD],
                                  probsT[:, kt, h, :], start=(kt == 0), stop=(kt == u), tile_position=(0, h * HD))
                pe.transpose(ps_pv[:, P:2 * P], rinv_wide[:, :, :].rearrange("p h d -> p (h d)"),
                             ident[:, :]).then_inc(pv_ok, 1)

            def steps(it, it_q, ln_b=None):
                order = ring_order(True, it_q is not None)
                r = 0
                for n in range(LAST_STEP):
                    if n < HU:
                        scores(it, n)
                        if it_q is not None:
                            qkv(it_q, n // 4, [2 * (n % 4), 2 * (n % 4) + 1])
                        if ln_b is not None and n % 2:
                            ln_half(ln_b, n // 4, n // 2 % 2)
                    if n >= 6 and (n - 6) % 4 == 0:
                        if it_q is not None:
                            ring_free(order, r, it, it_q)
                            qk_transpose(it_q, (n - 6) // 4, ps_t[r % 2])
                            r += 1
                        values(it, (n - 6) // 4)
                    if 0 <= n - 2 < HU:
                        r = turn(it, it_q, n - 2, order, r)

            for k in range(4):
                mod_chunk(k)
                mod_rows(k)
            pe.wait_ge(mcol_ld, 32)
            pe.wait_ge(mod_rw, 4)
            pe.transpose(ps_pv[:, 0:4 * KT], mcol_rows[:, :], ident[0:4 * KT, 0:4 * KT]).then_inc(mcol_t, 1)
            for tt in range(NT):
                for half in range(2):
                    ln_half(0, tt, half)
            for b in range(B):
                it0 = b * G
                order = [("qk", tt) for tt in range(NT)]

                def first_qk(tt):
                    if tt >= 2:
                        pe.wait_ge(qk_lo, 8 * it0 + tt - 1)
                    elif b:
                        pe.wait_ge(ev["dve"], EVAC["dve"] * it0 + 1)
                        pe.wait_ge(ev["act"], EVAC["act"] * it0 + 1)
                    qk_transpose(it0, tt, ps_t[tt % 2])

                for tt in range(NT):
                    qkv(it0, tt, list(range(KT)), b)
                    if tt:
                        first_qk(tt - 1)
                    if b == 0:
                        if tt == 0:
                            pe.wait_ge(mcol, 1)
                        mod_chunk(4 + tt)
                        mod_rows(4 + tt)
                first_qk(NT - 1)
                if b == 0:
                    pe.wait_ge(mod_rw, MODC)
                with pe.Fori(0, G - 1) as g:
                    steps(g + it0, g + (it0 + 1))
                steps(it0 + G - 1, None, 1 if b == 0 else None)
            phase_b_tensor(pe)

        @block.scalar
        def _(act):
            act.sem_inc(exp_ok, 2)
            act.sem_inc(ev["act"], 1)
            act.wait_ge(c_t, 1)
            act.activation(c_e[:, :], ps_pv[:, 0:B * KT], ACT.Exp, scale=-1.0).then_inc(c_ex, 1)

            def mod_out(k):
                act.wait_ge(mod_mm, k + 1)
                if k:
                    act.wait_ge(mod_sum, k)
                act.copy(mod_part, ps_s[0][:, 0:BANK]).then_inc(mod_ev, 1)

            def ln_split(b, tt, half):
                n = 2 * (b * NT + tt) + half
                act.wait_ge(ln_tt, n + 1)
                act.copy(hT_hi[:, 4 * half:4 * half + 4, tt * P:(tt + 1) * P],
                         ht[:, half, :].rearrange("p (k t) -> p k t", k=4)).then_inc(ln_hi, 1)

            def split_w(it):
                act.wait_ge(w_ld, 48 * (it + 1))
                if not isinstance(it, int) or it:
                    act.wait_ge(qkv_mm, 8 * it)
                for half in range(2):
                    act.copy(w_hi[:, 4 * half:4 * half + 4, :], w_raw[:, 4 * half:4 * half + 4, :, :].rearrange(
                        "p k j n -> p k (j n)")).then_inc(w_hi_ok, 1)

            def copy_qkv(it, tt):
                act.wait_ge(qkv_mm, 8 * it + tt + 1)
                if not isinstance(it, int) or 8 * it + tt >= 2:
                    act.wait_ge(roped, 16 * it + 2 * tt - 2)
                act.copy(qkv_sb[:, tt % 2, :], ps_qkv[:, 0:3 * P]).then_inc(qkv_cp, 1)

            def qk_split(it, tt, bank):
                act.wait_ge(qk_t, 8 * it + tt + 1)
                if tt % 4 == 0 and (not isinstance(it, int) or it):
                    act.wait_ge(stacked[tt // 4], stack_groups * it)
                act.copy(qkT[:, 0, :, tt * P:(tt + 1) * P].bitcast(F32R),
                         bank[:, 0:2 * P].rearrange("p (j t) -> p j t", j=2)).then_inc(qk_hi, 1)

            def softmax_exp(it, n):
                qt, h = n // GH, n % GH
                w = (qt + 1) * P
                act.wait_ge(max_ok, HU * it + n + 1)
                before = max((PLAN[k][2] + 1 for k in PLAN if k[0] <= n - GH), default=0)
                act.wait_ge(t_ok, TCHUNKS * it + before + 1)
                act.activation(probs[:, h, 0:w], ps_s[n % 2][:, 0:w], ACT.Exp, bias=nmax[:, n:n + 1], scale=1.0,
                               accum_out=sums[:, n:n + 1]).then_inc(exp_ok, 1)

            def evac(it, n, c, bank):
                eng, num, at, k0, m = PLAN[n, c]
                act.wait_ge(t_ok, TCHUNKS * it + at + 2)
                act.wait_ge(pv_ok, 8 * it + n // GH + 1)
                act.copy(probsT[:, k0:k0 + m, n % GH, :],
                         bank[:, 0:m * P].rearrange("p (k q) -> p k q", k=m)).then_inc(ev["act"], 1)

            def steps(it, it_q, ln_b=None):
                r = 0
                for n in range(LAST_STEP):
                    if n == 0 and it_q is not None:
                        split_w(it_q)
                    if n < HU:
                        softmax_exp(it, n)
                        if ln_b is not None and n % 2:
                            ln_split(ln_b, n // 4, n // 2 % 2)
                        if it_q is not None and n % 4 == 3:
                            copy_qkv(it_q, n // 4)
                    if n >= 6 and (n - 6) % 4 == 0:
                        u = (n - 6) // 4
                        if it_q is not None:
                            qk_split(it_q, u, ps_t[r % 2])
                            r += 1
                        act.wait_ge(pv_ok, 8 * it + u + 2)
                        act.copy(rinvT[:, :], ps_pv[:, P:2 * P]).then_inc(rinvT_ok, 1)
                    if 0 <= n - 2 < HU:
                        for c in range(len(chunks_of(n - 2))):
                            if PLAN[n - 2, c][0] == "act":
                                evac(it, n - 2, c, ps_t[r % 2])
                            r += 1

            for k in range(4):
                mod_out(k)
            for tt in range(NT):
                for half in range(2):
                    ln_split(0, tt, half)
            for b in range(B):
                it0 = b * G
                split_w(it0)
                for tt in range(NT):
                    copy_qkv(it0, tt)
                    if tt:
                        qk_split(it0, tt - 1, ps_t[(tt - 1) % 2])
                    if b == 0:
                        mod_out(4 + tt)
                qk_split(it0, NT - 1, ps_t[(NT - 1) % 2])
                with act.Fori(0, G - 1) as g:
                    steps(g + it0, g + (it0 + 1))
                steps(it0 + G - 1, None, 1 if b == 0 else None)
            phase_b_scalar(act)

        @block.vector
        def _(dve):
            dve.sem_inc(ev["dve"], 1)
            dve.sem_inc(at_ok, 1)
            dve.sem_inc(t_ok, 1)
            dve.sem_inc(pv_ok, 1)
            dve.sem_inc(at_st, 16)

            def then(ins):
                seq["dve"] += 1
                ins.then_inc(dve_seq, 1)
                dve.wait_ge(dve_seq, seq["dve"])

            dve.memset(c_pad[:, :, :], 0.0).then_inc(dve_seq, 1)
            seq["dve"] += 1
            dve.wait_ge(const_ld, 64)
            dve.tensor_copy(mask[:, :], rinvT[:, :])
            dve.tensor_copy(ident16[:, :], ident[:, :]).then_inc(c_done, 1)
            dve.wait_ge(c_ex, 1)
            then(dve.tensor_scalar(c_e1[:, :], c_e[:, :], 1.0, None, ALU.add))
            then(dve.reciprocal(c_sig[:, :], c_e1[:, :]))
            dve.tensor_tensor(c_pad[:, :, 0:B].rearrange("p k b -> p b k"),
                              ps_pv[:, 0:B * KT].rearrange("p (b k) -> p b k", b=B),
                              c_sig[:, :].rearrange("p (b k) -> p b k", b=B), ALU.mult).then_inc(c_done, 1)

            def mod_store(k):
                dve.wait_ge(mod_sum, k + 1)
                if k:
                    dve.wait_ge(mod_st, 16 * k)
                dve.tensor_copy(mod_row, ps_pv[0:B, 0:BANK]).then_inc(mod_rw, 1)

            def ln_norm(b, tt):
                n = b * NT + tt
                xt = xb[:, tt % 2, :]
                dve.wait_ge(ln_x[tt % 2], 16 * (b * NT // 2 + tt // 2 + 1))
                for i in range(2):
                    st = dve.bn_stats(stats[:, i, :], xt[:, i * BANK:(i + 1) * BANK])
                then(st)
                dve.bn_aggr(mv[:, :], stats[:, :, :].rearrange("p a s -> p (a s)")).then_inc(ln_st, 1)
                dve.wait_ge(ln_st, n + 1)
                dve.wait_ge(ln_rs, n + 1)
                dve.tensor_scalar(xt, xt, mv[:, 0:1], rstd[:, 0:1], ALU.subtract, ALU.mult).then_inc(ln_xn, 1)

            def ln_mod(b, tt, half):
                n = 2 * (b * NT + tt) + half
                dve.wait_ge(ln_tr, n + 1)
                if n >= 2:
                    dve.wait_ge(ln_hi, n - 1)
                    dve.wait_ge(ln_lo, n - 1)
                for j in range(4):
                    kt = 4 * half + j
                    o = dve.tensor_scalar(ht[:, half, j * P:(j + 1) * P], ps_qkv[:, j * P:(j + 1) * P],
                                          modcol1[:, b * 16 + 8 + kt:b * 16 + 9 + kt],
                                          modcol[:, b * 16 + kt:b * 16 + kt + 1], ALU.mult, ALU.add)
                o.then_inc(ln_tt, 1)

            def qk_rest(it, tt, bank):
                dve.wait_ge(qk_hi, 8 * it + tt + 1)
                dve.tensor_tensor(qkT[:, 1, :, tt * P:(tt + 1) * P].bitcast(F32R),
                                  bank[:, 0:2 * P].rearrange("p (j t) -> p j t", j=2),
                                  qkT[:, 0, :, tt * P:(tt + 1) * P], ALU.subtract).then_inc(qk_lo, 1)

            def row_max(it, n):
                w = (n // GH + 1) * P
                dve.wait_ge(s_ok, HU * it + n + 1)
                dve.tensor_reduce(nmax[:, n:n + 1], ps_s[n % 2][:, 0:w], AX_X, ALU.max, negate=True).then_inc(max_ok, 1)

            def evac(it, n, c, bank):
                eng, num, at, k0, m = PLAN[n, c]
                dve.wait_ge(t_ok, TCHUNKS * it + at + 2)
                dve.wait_ge(pv_ok, 8 * it + n // GH + 1)
                dve.tensor_copy(probsT[:, k0:k0 + m, n % GH, :],
                                bank[:, 0:m * P].rearrange("p (k q) -> p k q", k=m)).then_inc(ev["dve"], 1)

            def invert(it, u):
                dve.wait_ge(exp_ok, HU * it + GH * (u + 1) + 2)
                dve.reciprocal(rinv[:, :], sums[:, GH * u:GH * (u + 1)]).then_inc(inv_ok, 1)
                dve.wait_ge(inv_ok, 8 * it + u + 1)
                dve.wait_ge(pv_ok, 8 * it + u + 1)
                dve.tensor_copy(rinv_wide[:, :, :], rinv[:, :].unsqueeze(2).broadcast_to([P, GH, HD]))\
                   .then_inc(rinv_ok, 1)

            def normalise(it, u):
                dve.wait_ge(rinvT_ok, 8 * it + u + 1)
                if u == 0:
                    dve.wait_ge(at_st, 16 * it + 16)
                dve.tensor_tensor(attnT[:, u * P:(u + 1) * P], ps_pv[:, 0:P], rinvT[:, :], ALU.mult).then_inc(at_ok, 1)

            def steps(it, it_q, ln_b=None):
                r = 0
                for n in range(LAST_STEP):
                    if n < HU:
                        row_max(it, n)
                        if ln_b is not None:
                            if n % 4 == 0:
                                ln_norm(ln_b, n // 4)
                            if n % 2:
                                ln_mod(ln_b, n // 4, n // 2 % 2)
                    if n >= 7 and (n - 7) % 4 == 0:
                        normalise(it, (n - 7) // 4)
                    if n >= 5 and (n - 5) % 4 == 0 and n < HU + 2:
                        invert(it, (n - 5) // 4)
                    if n >= 6 and (n - 6) % 4 == 0:
                        if it_q is not None:
                            qk_rest(it_q, (n - 6) // 4, ps_t[r % 2])
                            r += 1
                    if 0 <= n - 2 < HU:
                        for c in range(len(chunks_of(n - 2))):
                            if PLAN[n - 2, c][0] == "dve":
                                evac(it, n - 2, c, ps_t[r % 2])
                            r += 1

            for k in range(4):
                mod_store(k)
            dve.wait_ge(mcol_t, 1)
            dve.tensor_copy(modcol[:, :], ps_pv[:, 0:4 * KT])
            then(dve.tensor_scalar(modcol1[:, :], ps_pv[:, 0:4 * KT], 1.0, None, ALU.add))
            dve.sem_inc(mcol, 1)
            for tt in range(NT):
                ln_norm(0, tt)
                ln_mod(0, tt, 0)
                ln_mod(0, tt, 1)
            for b in range(B):
                it0 = b * G
                for tt in range(NT):
                    if tt:
                        qk_rest(it0, tt - 1, ps_t[(tt - 1) % 2])
                    if b == 0:
                        mod_store(4 + tt)
                qk_rest(it0, NT - 1, ps_t[(NT - 1) % 2])
                if b == 0:
                    dve.wait_ge(mod_st, 16 * MODC)
                with dve.Fori(0, G - 1) as g:
                    steps(g + it0, g + (it0 + 1))
                steps(it0 + G - 1, None, 1 if b == 0 else None)
            phase_b_vector(dve)

        @block.gpsimd
        def _(pool):
            pool.memset(eps[:, :], EPS)
            pool.memset(minus_half[:, :], -0.5).then_inc(pool_half, 1)
            pool.wait_ge(pool_half, 1)

            def ln_rstd(b, tt):
                n = b * NT + tt
                pool.wait_ge(ln_st, n + 1)
                pool.tensor_tensor(vareps[:, :], mv[:, 1:2], eps[:, :], ALU.add).then_inc(pool_ve, 1)
                pool.wait_ge(pool_ve, n + 1)
                pool.tensor_tensor(rstd[:, :], vareps[:, :], minus_half[:, :], ALU.pow).then_inc(ln_rs, 1)

            def ln_rest(b, tt, half):
                n = 2 * (b * NT + tt) + half
                pool.wait_ge(ln_hi, n + 1)
                hi = hT_hi[:, 4 * half:4 * half + 4, tt * P:(tt + 1) * P]
                pool.tensor_tensor(hT_lo[:, 4 * half:4 * half + 4, tt * P:(tt + 1) * P],
                                   ht[:, half, :].rearrange("p (k t) -> p k t", k=4), hi.bitcast(F32),
                                   ALU.subtract).then_inc(ln_lo, 1)

            def rest_w(it, half):
                pool.wait_ge(w_hi_ok, 2 * it + half + 1)
                ks = slice(4 * half, 4 * half + 4)
                pool.tensor_tensor(w_lo[:, ks, :], w_raw[:, ks, :, :].rearrange("p k j n -> p k (j n)"),
                                   w_hi[:, ks, :].bitcast(F32), ALU.subtract).then_inc(w_lo_ok, 1)

            def rotate(it, tt):
                pool.wait_ge(qkv_cp, 8 * it + tt + 1)
                src = qkv_sb[:, tt % 2, :]
                pairs = src[:, 0:2 * P].rearrange("p (j h d) -> p j h d", j=2, h=GH)
                if not isinstance(it, int) or 8 * it + tt:
                    pool.wait_ge(roped, 16 * it + 2 * tt)
                for i, dst in enumerate((rope_a, rope_b)):
                    for j in range(2):
                        tab = rope_tab[:, i, tt, j, :].unsqueeze(1).broadcast_to([P, GH, HD])
                        pool.tensor_tensor(dst[:, j * P:(j + 1) * P].rearrange("p (h d) -> p h d", h=GH),
                                           pairs[:, j], tab, ALU.mult).then_inc(pool_seq, 1)
                pool.tensor_copy(v_next[:, tt, :], src[:, 2 * P:3 * P]).then_inc(pool_seq, 1)
                pool.wait_ge(pool_seq, 5 * (8 * it + tt + 1))
                if not isinstance(it, int) or 8 * it + tt >= 2:
                    pool.wait_ge(qk_t, 8 * it + tt - 1)
                for i, (t, op) in enumerate(((rope_a, ALU.subtract), (rope_b, ALU.add))):
                    v = t[:, :].rearrange("p (g i e) -> p g i e", g=2 * GH, e=2)
                    dst = qk_rot[:, tt % 2, :].rearrange("p (g e i) -> p g e i", g=2 * GH, e=2)[:, :, i, :]
                    pool.tensor_tensor(dst, v[:, :, :, 0], v[:, :, :, 1], op).then_inc(roped, 1)

            def place_v(it):
                pool.tensor_copy(v_now[:, :, :], v_next[:, :, :]).then_inc(v_ok, 1)
                pool.wait_ge(v_ok, it + 1)

            def steps(it, it_q, ln_b=None):
                pool.wait_ge(pv_ok, 8 * it + 1)
                pool.wait_ge(roped, 16 * it + 16)
                if it_q is not None:
                    rest_w(it_q, 0)
                place_v(it)
                if it_q is not None:
                    rest_w(it_q, 1)
                for tt in range(NT):
                    if it_q is not None:
                        rotate(it_q, tt)
                    if ln_b is not None:
                        ln_rstd(ln_b, tt)
                        ln_rest(ln_b, tt, 0)
                        ln_rest(ln_b, tt, 1)

            for tt in range(NT):
                ln_rstd(0, tt)
                ln_rest(0, tt, 0)
                ln_rest(0, tt, 1)
            pool.wait_ge(rope_ld, 16)
            for b in range(B):
                it0 = b * G
                rest_w(it0, 0)
                rest_w(it0, 1)
                for tt in range(NT):
                    rotate(it0, tt)
                if b == 0:
                    pool.wait_ge(mod_mm, MODC)
                with pool.Fori(0, G - 1) as g:
                    steps(g + it0, g + (it0 + 1))
                steps(it0 + G - 1, None, 1 if b == 0 else None)
            phase_b_gpsimd(pool)


_INS = ['L0_attn_x', 'L0_attn_wq', 'L0_attn_wk', 'L0_attn_wv', 'L0_attn_wo', 'L0_ffn_W_base', 'L0_ffn_b_base',
        'L0_ffn_W_gate', 'L0_ffn_W_thr', 'L0_ffn_b_thr', 'L0_ffn_A_w', 'L0_ffn_B_w', 'L0_c', 'L0_wmod']


def shape_constants():
    import numpy as np

    inv = 1.0 / 10000.0 ** (np.arange(0, HD, 2).astype(np.float32) / HD)
    f = np.outer(np.arange(S), inv).astype(np.float32)
    cos, sin = np.cos(f), np.sin(f)
    tabs = np.stack([np.stack([cos, sin], -1), np.stack([sin, cos], -1)]).reshape(2, NT, P, HD)
    scale = np.float32(1.0) / np.sqrt(np.float32(HD))
    rope = np.stack([tabs * scale, tabs], 3).transpose(2, 0, 1, 3, 4)
    q, k = np.arange(P)[:, None], np.arange(P)[None, :]
    return {
        "rope": np.ascontiguousarray(rope, np.float32),
        "ident": np.eye(P, dtype=np.float32),
        "mask": np.where(k > q, np.float32(MASKED), np.float32(0)),
        "sel": (np.arange(P)[:, None] % HD == np.arange(B)[None, :]).astype(np.float32),
    }


def kernel(**inputs):
    import numpy as np
    import concourse.bacc as bacc
    from concourse.bass_utils import run_bass_kernel_spmd

    nc = bacc.Bacc("TRN2", target_bir_lowering=False, num_devices=1)
    arrays, args = {}, []
    for name, a in [(n, inputs[n]) for n in _INS] + list(shape_constants().items()):
        a = np.ascontiguousarray(a)
        arrays[f"in_{name}_dram"] = a
        args.append(nc.dram_tensor(f"in_{name}_dram", a.shape, mybir.dt.from_np(a.dtype), kind="ExternalInput").ap())
    args.append(nc.dram_tensor("out_0_dram", (B, S, D), F32, kind="ExternalOutput").ap())
    adaln_block(nc, *args)
    r = run_bass_kernel_spmd(nc, [arrays], core_ids=[0])
    return r.results[0]["out_0_dram"]
```

```python
from contextlib import ExitStack

import concourse.bass as bass
from concourse import mybir

F32 = mybir.dt.float32
F32R = mybir.dt.float32r
BF16 = mybir.dt.bfloat16
ALU = mybir.AluOpType
ACT = mybir.ActivationFunctionType
AX_X = mybir.AxisListType.X

P = 128
B, S, D = 2, 1024, 1024
H, HD = 32, 32
GH = P // HD
G = H // GH
NT = S // P
KT = D // P
BANK = 512
E_, R_ = 8, 16
ER = E_ * R_
EPS = 1e-5
SCALING = 2.0
MAX_THRESHOLD = 0.125
MASKED = -1e30
AGW = ER + 10
MODC = 6 * D // BANK
HU = GH * NT
EARLY = 7


def chunks_of(n):
    kts = n // GH + 1
    return [(k0, min(4, kts - k0)) for k0 in range(0, kts, 4)]


def attention_plan():
    plan, count = {}, {"dve": 0, "act": 0}
    at = 0
    for n in range(HU):
        for c, (k0, m) in enumerate(chunks_of(n)):
            eng = ("dve", "act")[(n + c) % 2] if n < HU // 2 else ("dve", "act")[c]
            plan[n, c] = (eng, count[eng], at, k0, m)
            count[eng] += 1
            at += 1
    return plan, count, at


PLAN, EVAC, TCHUNKS = attention_plan()
MOD_BETWEEN = [2, 1, 1, 1, 1, 1, 1]
assert sum(MOD_BETWEEN) == MODC - 4 and len(MOD_BETWEEN) == EARLY


SKIP, LAST_QK = (9, 13, 23), 1


class Steps:

    def __init__(self, following, norm=False):
        self.quarters = {n: [(0, EARLY + n // 4, n % 4)] for n in range(4 * (NT - EARLY))}
        if following:
            if norm:
                free = list(range(16, HU)) + [n for n in range(HU, 99) for _ in range(2)]
            else:
                free = sorted([n for n in range(5, HU + 3) if n not in SKIP] + [HU + 1])
            for m, n in zip(range(4 * EARLY), free):
                self.quarters.setdefault(n, []).append((1, m // 4, m % 4))
        self.ends = {n: e[:2] for n, es in self.quarters.items() for e in es if e[2] == 3}
        self.qk = {n + 3: e for n, e in self.ends.items() if e != (1, EARLY - 1)}
        self.qk[LAST_QK] = (0, EARLY - 1)
        self.last = max(HU + 4, max(self.quarters) + 1, max(self.qk) + 1)
        self.split = {1 + q: q for q in range(4)} if following else {}
        self.norm = {11 + 3 * tt + j: (tt, j) for tt in range(NT) for j in range(3)} if norm else {}
        self.ring = []
        for n in range(self.last):
            if n in self.norm and self.norm[n][1]:
                self.ring.append(("norm", *self.norm[n]))
            if 0 <= n - 2 < HU:
                self.ring += [("probs", n - 2, c) for c in range(len(chunks_of(n - 2)))]
            if n in self.qk:
                self.ring.append(("qk", *self.qk[n]))
        self.place = {u: i for i, u in enumerate(self.ring)}


INNER, HANDOVER, FINAL = Steps(True), Steps(True, norm=True), Steps(False)


def adaln_block(nc, x_in, wq, wk, wv, wo, W_base, b_base, W_gate, W_thr, b_thr, A_w, B_w, c_in, wmod,
                rope_c, ident_c, mask_c, sel_c, out):
    attn_dram = nc.dram_tensor("attn_scratch", [D, B * S], F32, kind="Internal").ap()
    mod_dram = nc.dram_tensor("mod_scratch", [B, 6 * D], F32, kind="Internal").ap()
    x_rows = x_in.rearrange("b s d -> (b s) d")
    out_rows = out.rearrange("b s d -> (b s) d")

    outer = ExitStack()
    with outer:
        def sem(name):
            return outer.enter_context(nc.semaphore(name))

        def keep(name, shape, dt):
            return outer.enter_context(nc.sbuf_tensor(name, shape, dt))

        def psum(name, cols):
            return outer.enter_context(nc.psum_tensor(name, [P, cols], F32))

        ps_s = [psum("ps_s0", 2 * BANK), psum("ps_s1", 2 * BANK)]
        ps_t = [psum("ps_t0", BANK), psum("ps_t1", BANK)]
        ps_qkv = psum("ps_qkv", BANK)
        ps_pv = psum("ps_pv", BANK)

        ident = keep("ident", [P, P], F32)
        modcol = keep("modcol", [P, 4 * KT], F32)
        modcol1 = keep("modcol1", [P, 4 * KT], F32)
        mcol_rows = keep("mcol_rows", [4 * KT, P], F32)
        stats = keep("stats", [P, 2, 6], F32)
        mv = keep("mv", [P, 2], F32)
        vareps = keep("vareps", [P, 1], F32)
        minus_half = keep("minus_half", [P, 1], F32)
        eps = keep("eps", [P, 1], F32)
        rstd = keep("rstd", [P, 1], F32)

        phase_a = ExitStack()

        def sb(name, shape, dt):
            return phase_a.enter_context(nc.sbuf_tensor(name, shape, dt))

        hT_hi = sb("hT_hi", [P, KT, S], F32R)
        hT_lo = sb("hT_lo", [P, KT, S], F32R)
        w_raw = sb("w_raw", [P, KT, 3, P], F32)
        w_hi = sb("w_hi", [P, KT, 3 * P], F32R)
        w_lo = sb("w_lo", [P, KT, 3 * P], F32R)
        qkv_sb = sb("qkv_sb", [P, 2, 3 * P], F32)
        qk_rot = sb("qk_rot", [P, 2, 2 * P], F32)
        rope_a = sb("rope_a", [P, 2 * P], F32)
        rope_b = sb("rope_b", [P, 2 * P], F32)
        rope_tab = sb("rope_tab", [P, 2, NT, 2, HD], F32)
        qkT = sb("qkT", [P, 2, 2, S], F32)
        qk_stack = sb("qk_stack", [3 * HD, 2, GH, S], F32R)
        v_next = sb("v_next", [P, EARLY, P], F32)
        v_now = sb("v_now", [P, NT, P], F32)
        probs = sb("probs", [P, GH, S], F32)
        probsT = sb("probsT", [P, NT, GH, P], F32)
        nmax = sb("nmax", [P, HU], F32)
        sums = sb("sums", [P, HU], F32)
        rinv = sb("rinv", [P, GH], F32)
        rinv_wide = sb("rinv_wide", [P, GH, HD], F32)
        rinvT = sb("rinvT", [P, P], F32)
        attnT = sb("attnT", [P, S], F32)
        mask = sb("mask", [P, P], BF16)
        ident16 = sb("ident16", [P, P], BF16)
        sel = sb("sel", [P, B], F32)
        c_rows = sb("c_rows", [B * KT, P], F32)
        c_e = sb("c_e", [P, B * KT], F32)
        c_e1 = sb("c_e1", [P, B * KT], F32)
        c_sig = sb("c_sig", [P, B * KT], F32)
        c_pad = v_now[:, 0:2, :].rearrange("p a (k b) -> p (a k) b", b=HD)
        w_flat = w_raw[:, :, :, :].rearrange("p k j n -> p (k j n)")
        xb = [qkT[:, 0, :, :], w_flat[:, 0:2 * D].rearrange("p (a n) -> p a n", a=2)]
        ht = [qkT[:, 1, 0, :].rearrange("p (a n) -> p a n", a=2),
              w_flat[:, 2 * D:3 * D].rearrange("p (a n) -> p a n", a=2)]
        wm_buf = [probs[:, :, :].rearrange("p h s -> p (h s)").rearrange("p (k n) -> p k n", k=KT),
                  probsT[:, :, :, :].rearrange("p k h q -> p k (h q)")]
        mod_part = attnT[:, 0:BANK]
        mod_row = attnT[0:B, BANK:2 * BANK]
        phase_a.close()

        phase_b = ExitStack()

        def sb2(name, shape, dt):
            return phase_b.enter_context(nc.sbuf_tensor(name, shape, dt))

        wo_hi = sb2("wo_hi", [P, KT, D], F32R)
        wo_lo = sb2("wo_lo", [P, KT, D], F32R)
        wb_hi = sb2("wb_hi", [P, KT, D], F32R)
        wb_lo = sb2("wb_lo", [P, KT, D], F32R)
        ag_hi = sb2("ag_hi", [P, KT, AGW], F32R)
        ag_lo = sb2("ag_lo", [P, KT, AGW], F32R)
        bt_hi = sb2("bt_hi", [P, D], F32R)
        bt_lo = sb2("bt_lo", [P, D], F32R)
        ga = sb2("ga", [P, B, D], F32)
        gb = sb2("gb", [P, B, D], F32)
        bias = sb2("bias", [P, D], F32)
        a_raw = sb2("a_raw", [P, KT, P], F32)
        a_hi = sb2("a_hi", [P, KT, P], F32R)
        a_lo = sb2("a_lo", [P, KT, P], F32R)
        x1 = sb2("x1", [P, 2, D], F32)
        xn = sb2("xn", [P, D], F32)
        h2t = sb2("h2t", [P, BANK], F32)
        h2_hi = sb2("h2_hi", [P, KT, P], F32R)
        h2_lo = sb2("h2_lo", [P, KT, P], F32R)
        gsm = sb2("gsm", [P, 48], F32)
        bthr = sb2("bthr", [P, 2], F32)
        ag_out = sb2("ag_out", [P, AGW], F32)
        hw = sb2("hw", [P, E_, R_], F32)
        hwT_hi = sb2("hwT_hi", [P, P], F32R)
        hwT_lo = sb2("hwT_lo", [P, P], F32R)
        stage = [x1[:, 0, :], x1[:, 1, :], xn[:, :]]
        phase_b.close()

        const_ld = sem("const_ld")
        rope_ld = sem("rope_ld")
        c_t = sem("c_t")
        c_ex = sem("c_ex")
        c_done = sem("c_done")
        wm_ld = [sem("wm_ld0"), sem("wm_ld1")]
        mod_mm = sem("mod_mm")
        mod_ev = sem("mod_ev")
        mod_sum = sem("mod_sum")
        mod_rw = sem("mod_rw")
        mod_st = sem("mod_st")
        mcol_ld = sem("mcol_ld")
        mcol_t = sem("mcol_t")
        mcol = sem("mcol")
        ln_x = [sem("ln_x0"), sem("ln_x1")]
        ln_st = sem("ln_st")
        ln_rs = sem("ln_rs")
        ln_xn = sem("ln_xn")
        ln_tr = sem("ln_tr")
        ln_tt = sem("ln_tt")
        ln_hi = sem("ln_hi")
        ln_lo = sem("ln_lo")
        w_ld = sem("w_ld")
        w_hi_ok = sem("w_hi_ok")
        w_lo_ok = sem("w_lo_ok")
        w_used = sem("w_used")
        qkv_mm = sem("qkv_mm")
        qkv_cp = sem("qkv_cp")
        roped = sem("roped")
        qk_t = sem("qk_t")
        qk_hi = sem("qk_hi")
        qk_lo = sem("qk_lo")
        stacked = [[sem(f"stacked_{half}_h{h}") for h in range(GH)] for half in ("first", "second")]
        v_cp = sem("v_cp")
        v_ok = sem("v_ok")
        s_ok = sem("s_ok")
        max_ok = sem("max_ok")
        exp_ok = sem("exp_ok")
        t_ok = sem("t_ok")
        ev = {"dve": sem("ev_dve"), "act": sem("ev_act")}
        rinv_ok = sem("rinv_ok")
        pv_ok = sem("pv_ok")
        rinvT_ok = sem("rinvT_ok")
        at_ok = sem("at_ok")
        at_st = sem("at_st")
        pool_seq = sem("pool_seq")
        dve_seq = sem("dve_seq")
        inv_ok = sem("inv_ok")
        pool_half = sem("pool_half")
        pool_ve = sem("pool_ve")
        st_ld = [sem(f"st_ld{i}") for i in range(3)]
        st_t = sem("st_t")
        st_hi = sem("st_hi")
        st_lo = sem("st_lo")
        rows_ld = sem("rows_ld")
        gate_tmp = sem("gate_tmp")
        rows_ok = sem("rows_ok")
        mcol2_ld = sem("mcol2_ld")
        mcol2_t = sem("mcol2_t")
        a_ld = sem("a_ld")
        a_hi_ok = sem("a_hi_ok")
        a_lo_ok = sem("a_lo_ok")
        x_ld = [sem("x_ld0"), sem("x_ld1")]
        wo_ok = sem("wo_ok")
        gated = sem("gated")
        x1_ok = sem("x1_ok")
        bn_ok = sem("bn_ok")
        b_st = sem("b_st")
        b_ve = sem("b_ve")
        b_rs = sem("b_rs")
        xn_ok = sem("xn_ok")
        xt_ok = sem("xt_ok")
        h2t_ok = sem("h2t_ok")
        h2_hi_ok = sem("h2_hi_ok")
        h2_lo_ok = sem("h2_lo_ok")
        ag_ok = sem("ag_ok")
        ag_cp = sem("ag_cp")
        gate_max = sem("gate_max")
        gate_exp = sem("gate_exp")
        gate_seq = sem("gate_seq")
        hw_ok = sem("hw_ok")
        hwT_ok = sem("hwT_ok")
        hwT_hi_ok = sem("hwT_hi_ok")
        hwT_lo_ok = sem("hwT_lo_ok")
        y_ok = sem("y_ok")
        y_ev = sem("y_ev")
        y_gated = sem("y_gated")
        out_ok = sem("out_ok")
        out_st = sem("out_st")
        STACKING = 3 * 16

        seq = {"dve": 0, "pool": 0}

        items = [("wo", k) for k in range(KT)] + [("ag", 0), ("ag", 1), ("bt", 0)] + [("wb", o) for o in range(KT)]
        n_dma = {"bt": E_}
        loaded, units_to, unit = [], [], 0
        for kind, k in items:
            n = 1 + AGW - ER - E_ if (kind, k) == ("ag", 1) else n_dma.get(kind, 1)
            loaded.append((loaded[-len(stage)] if len(loaded) >= len(stage) else 0) + 16 * n)
            unit += 1 if kind == "wo" else 2
            units_to.append(unit)
        UNITS = unit
        GATE_STEPS = 8

        def piece(kind, k, half):
            ks = slice(4 * half, 4 * half + 4)
            if kind == "wb":
                return tuple(w[:, ks, k * P:(k + 1) * P] for w in (wb_hi, wb_lo))
            if kind == "bt":
                return tuple(w[:, half * BANK:(half + 1) * BANK].rearrange("p (k n) -> p k n", k=4)
                             for w in (bt_hi, bt_lo))
            return tuple(w[:, ks, slice(0, ER) if k == 0 else slice(ER, AGW)] for w in (ag_hi, ag_lo))

        def piece_cols(kind, k):
            return AGW - ER if (kind, k) == ("ag", 1) else P

        def turned():
            n = 0
            for i, (kind, k) in enumerate(items):
                if kind != "wo":
                    for half in range(2):
                        yield n, i, kind, k, half, units_to[i] - 2 + half
                        n += 1

        def tile_of(hp, e):
            return hp * 2 + e

        def after(hp, e):
            return (hp, 1) if e == 0 else (hp + 1, 0)

        def tile_loops(eng, body):
            half = NT // 2
            for b in range(B):
                with eng.Fori(0, half - 1) as p:
                    for e in range(2):
                        body(p + b * half, e, b, b, True, True)
                hp = (b + 1) * half - 1
                for e in range(2):
                    i = 2 * hp + e
                    body(hp, e, b, min(B - 1, (i + 1) // NT), i + 1 < B * NT, i + 2 < B * NT)

        def phase_b_sync(sp):
            for i, (kind, k) in enumerate(items):
                if i >= len(stage):
                    sp.wait_ge(st_lo, units_to[i - len(stage)])
                to = stage[i % len(stage)]
                if kind == "wo":
                    sp.dma_start(to, wo[k * P:(k + 1) * P, :]).then_inc(st_ld[i % len(stage)], 16)
                elif kind == "wb":
                    sp.dma_start(to, W_base[k * P:(k + 1) * P, :]).then_inc(st_ld[i % len(stage)], 16)
                elif kind == "bt":
                    v = to.rearrange("p (t e r) -> p t e r", t=KT, e=E_)
                    for e in range(E_):
                        sp.dma_start(v[:, :, e, :], B_w[e].rearrange("(t p) r -> p t r", p=P)).then_inc(st_ld[i % len(stage)], 16)
                elif k == 0:
                    sp.dma_start(to, A_w.rearrange("e r d -> (e r) d")).then_inc(st_ld[i % len(stage)], 16)
                else:
                    sp.dma_start(to[0:E_, :], W_gate).then_inc(st_ld[i % len(stage)], 16)
                    for r in range(E_, AGW - ER):
                        sp.dma_start(to[r:r + 1, :], W_thr.rearrange("(a d) -> a d", a=1)).then_inc(st_ld[i % len(stage)], 16)
                if i == 2:
                    for b in range(B):
                        sp.dma_start(ga[:, b, :], mod_dram[b:b + 1, 2 * D:3 * D].broadcast_to([P, D])).then_inc(rows_ld, 16)
                        sp.dma_start(gb[:, b, :], mod_dram[b:b + 1, 5 * D:6 * D].broadcast_to([P, D])).then_inc(rows_ld, 16)
                        sp.dma_start(mcol_rows[b * 16:(b + 1) * 16, :], mod_dram[b, 3 * D:5 * D].rearrange(
                            "(r p) -> r p", p=P)).then_inc(mcol2_ld, 16)
                    sp.dma_start(bias[:, :], b_base.rearrange("(a d) -> a d", a=1).broadcast_to([P, D])).then_inc(rows_ld, 16)
                    sp.dma_start(bthr[:, 0:1], b_thr.rearrange("(a d) -> a d", a=1).broadcast_to([P, 1])).then_inc(rows_ld, 16)

            def load_a(i):
                sp.dma_start(a_raw[:, :, :], attn_dram.rearrange("(k p) t -> p k t", p=P)[
                    :, :, bass.ds(i * P, P)]).then_inc(a_ld, 16)

            def load_x(i, e):
                sp.dma_start(x1[:, e, :], x_rows[bass.ds(i * P, P), :]).then_inc(x_ld[e], 16)

            def body(hp, e, b, bj, has_next, has_next2):
                i = tile_of(hp, e)
                if has_next2:
                    sp.wait_ge(a_lo_ok, i + 2)
                    load_a(i + 2)
                sp.wait_ge(out_ok, i + 2)
                sp.dma_start(out_rows[bass.ds(i * P, P), :], x1[:, e, :]).then_inc(out_st, 16)
                if has_next2:
                    sp.wait_ge(out_st, 16 * i + 16)
                    load_x(i + 2, e)

            sp.wait_ge(rows_ok, 1)
            load_a(0)
            sp.wait_ge(st_lo, UNITS)
            load_x(0, 0)
            load_x(1, 1)
            sp.wait_ge(a_lo_ok, 1)
            load_a(1)
            tile_loops(sp, body)
            sp.wait_ge(out_st, 16 * B * NT)

        def phase_b_tensor(pe):
            pe.wait_ge(mcol2_ld, 32)
            pe.wait_ge(at_ok, 8 * B * G + 1)
            pe.transpose(ps_pv[:, 0:4 * KT], mcol_rows[:, :], ident[0:4 * KT, 0:4 * KT]).then_inc(mcol2_t, 1)
            for n, i, kind, k, half, u in turned():
                if n == 0:
                    pe.wait_ge(ev["dve"], EVAC["dve"] * B * G + 1)
                    pe.wait_ge(ev["act"], EVAC["act"] * B * G + 1)
                if half == 0:
                    pe.wait_ge(st_ld[i % len(stage)], loaded[i])
                if n >= 2:
                    pe.wait_ge(st_lo, u - 1)
                rows = piece_cols(kind, k)
                for j in range(4):
                    kt = 4 * half + j
                    mm = pe.transpose(ps_t[n % 2][:, j * rows:(j + 1) * rows],
                                      stage[i % len(stage)][0:rows, kt * P:(kt + 1) * P], ident[0:rows, 0:rows])
                mm.then_inc(st_t, 1)

            def three(out_ap, hi, lo, w_hi_ap, w_lo_ap, first, final):
                pe.matmul(out_ap, hi, w_hi_ap, start=first, stop=False)
                pe.matmul(out_ap, hi, w_lo_ap, start=False, stop=False)
                return pe.matmul(out_ap, lo, w_hi_ap, start=False, stop=final)

            def project(j):
                pe.wait_ge(a_hi_ok, j + 1)
                pe.wait_ge(a_lo_ok, j + 1)
                if not isinstance(j, int) or j:
                    pe.wait_ge(gated, j)
                for c in range(0, D, BANK):
                    for kt in range(KT):
                        mm = three(ps_s[0][:, c:c + BANK], a_hi[:, kt, :], a_lo[:, kt, :], wo_hi[:, kt, c:c + BANK],
                                   wo_lo[:, kt, c:c + BANK], kt == 0, kt == KT - 1)
                mm.then_inc(wo_ok, 1)

            def turn_xn(j):
                pe.wait_ge(xn_ok, j + 1)
                if not isinstance(j, int) or j:
                    pe.wait_ge(h2t_ok, 2 * j)
                for half in range(2):
                    for q in range(4):
                        kt = 4 * half + q
                        mm = pe.transpose(ps_t[half][:, q * P:(q + 1) * P], xn[:, kt * P:(kt + 1) * P], ident[:, :])
                    mm.then_inc(xt_ok, 1)

            def body(hp, e, b, bj, has_next, has_next2):
                i = tile_of(hp, e)
                if has_next:
                    project(i + 1)
                pe.wait_ge(h2_hi_ok, 2 * i + 2)
                pe.wait_ge(h2_lo_ok, 2 * i + 2)
                pe.wait_ge(ag_cp, i + 1)
                for kt in range(KT):
                    mm = three(ps_qkv[:, 0:AGW], h2_hi[:, kt, :], h2_lo[:, kt, :], ag_hi[:, kt, :], ag_lo[:, kt, :],
                               kt == 0, kt == KT - 1)
                mm.then_inc(ag_ok, 1)
                pe.wait_ge(y_ev, i + 1)
                for c in range(0, D, BANK):
                    for kt in range(KT):
                        three(ps_s[1][:, c:c + BANK], h2_hi[:, kt, :], h2_lo[:, kt, :], wb_hi[:, kt, c:c + BANK],
                              wb_lo[:, kt, c:c + BANK], kt == 0, False)
                pe.wait_ge(hw_ok, i + 2)
                pe.wait_ge(hwT_lo_ok, i + 1)
                pe.transpose(ps_pv[:, 0:P], hw[:, :, :].rearrange("p e r -> p (e r)"), ident[:, :]).then_inc(hwT_ok, 1)
                if has_next:
                    turn_xn(i + 1)
                pe.wait_ge(hwT_hi_ok, i + 1)
                pe.wait_ge(hwT_lo_ok, i + 2)
                for c in range(0, D, BANK):
                    mm = three(ps_s[1][:, c:c + BANK], hwT_hi[:, :], hwT_lo[:, :], bt_hi[:, c:c + BANK],
                               bt_lo[:, c:c + BANK], False, True)
                mm.then_inc(y_ok, 1)

            pe.wait_ge(st_hi, UNITS)
            pe.wait_ge(st_lo, UNITS)
            project(0)
            turn_xn(0)
            tile_loops(pe, body)

        def phase_b_scalar(act):
            halves = list(turned())
            for i, (kind, k) in enumerate(items):
                if kind == "wo":
                    act.wait_ge(st_ld[i % len(stage)], loaded[i])
                    act.copy(wo_hi[:, k, :], stage[i % len(stage)]).then_inc(st_hi, 1)
            for n, i, kind, k, half, u in halves:
                rows = piece_cols(kind, k)
                act.wait_ge(st_t, n + 1)
                act.copy(piece(kind, k, half)[0], ps_t[n % 2][:, 0:4 * rows].rearrange(
                    "p (k n) -> p k n", k=4)).then_inc(st_hi, 1)

            def split_a(i):
                act.wait_ge(a_ld, 16 * i + 16)
                if not isinstance(i, int) or i:
                    act.wait_ge(wo_ok, i)
                act.copy(a_hi[:, :, :], a_raw[:, :, :]).then_inc(a_hi_ok, 1)

            def split_h(j):
                for half in range(2):
                    act.wait_ge(h2t_ok, 2 * j + half + 1)
                    act.copy(h2_hi[:, 4 * half:4 * half + 4, :],
                             h2t[:, :].rearrange("p (k t) -> p k t", k=4)).then_inc(h2_hi_ok, 1)

            def body(hp, e, b, bj, has_next, has_next2):
                i = tile_of(hp, e)
                act.wait_ge(ag_cp, i + 2)
                act.activation(gsm[:, 9:10], ag_out[:, ER + E_:ER + E_ + 1], ACT.Exp, bias=bthr[:, 1:2],
                               scale=-1.0).then_inc(gate_exp, 1)
                act.wait_ge(gate_max, i + 1)
                act.activation(gsm[:, 0:E_], ag_out[:, ER:ER + E_], ACT.Exp, bias=gsm[:, 8:9], scale=1.0,
                               accum_out=gsm[:, 10:11]).then_inc(gate_exp, 1)
                if has_next2:
                    split_a(i + 2)
                act.wait_ge(hwT_ok, i + 1)
                act.copy(hwT_hi[:, :], ps_pv[:, 0:P]).then_inc(hwT_hi_ok, 1)
                if has_next:
                    split_h(i + 1)

            split_a(0)
            split_a(1)
            split_h(0)
            tile_loops(act, body)

        def phase_b_vector(dve):
            dve.sem_inc(ag_cp, 1)
            dve.sem_inc(hw_ok, 1)
            dve.sem_inc(hwT_lo_ok, 1)
            dve.sem_inc(y_ev, 1)
            dve.wait_ge(mcol2_t, 1)
            dve.tensor_copy(modcol[:, :], ps_pv[:, 0:4 * KT])
            dve.tensor_scalar(modcol1[:, :], ps_pv[:, 0:4 * KT], 1.0, None, ALU.add)
            halves = list(turned())
            for i, (kind, k) in enumerate(items):
                if kind == "wo":
                    dve.wait_ge(st_hi, i + 1)
                    dve.tensor_tensor(wo_lo[:, k, :], stage[i % len(stage)], wo_hi[:, k, :].bitcast(F32),
                                      ALU.subtract).then_inc(st_lo, 1)
            for n, i, kind, k, half, u in halves:
                rows = piece_cols(kind, k)
                hi, lo = piece(kind, k, half)
                dve.wait_ge(st_hi, u + 1)
                dve.tensor_tensor(lo, ps_t[n % 2][:, 0:4 * rows].rearrange("p (k n) -> p k n", k=4), hi.bitcast(F32),
                                  ALU.subtract).then_inc(st_lo, 1)
            dve.wait_ge(rows_ld, 16 * (2 * B + 2))
            sign, size = h2t[:, :], a_raw[:, 0:4, :].rearrange("p k t -> p (k t)")
            n = 0
            for g in (ga, gb):
                for b in range(B):
                    for c in range(0, D, BANK):
                        gc = g[:, b, c:c + BANK]
                        for o in (lambda: dve.tensor_scalar(sign, gc, 0.0, 2.0, ALU.is_ge, ALU.mult),
                                  lambda: dve.scalar_tensor_tensor(size, sign, -1.0, gc, ALU.add, ALU.mult),
                                  lambda: dve.tensor_scalar(sign, sign, -1.0, None, ALU.add),
                                  lambda: dve.scalar_tensor_tensor(gc, size, 0.25, sign, ALU.max, ALU.mult)):
                            n += 1
                            o().then_inc(gate_tmp, 1)
                            dve.wait_ge(gate_tmp, n)
            dve.tensor_scalar(bthr[:, 1:2], bthr[:, 0:1], -1.0, None, ALU.mult).then_inc(rows_ok, 1)
            dve.wait_ge(rows_ok, 1)

            def residual(j, hp, e, b):
                dve.wait_ge(wo_ok, j + 1)
                if not isinstance(j, int) or j:
                    dve.wait_ge(xt_ok, 2 * j)
                    dve.wait_ge(out_ok, j)
                dve.tensor_tensor(xn[:, :], ps_s[0][:, :], ga[:, b, :], ALU.mult).then_inc(gated, 1)
                dve.wait_ge(gated, j + 1)
                dve.wait_ge(x_ld[e], 16 * hp + 16)
                dve.tensor_tensor(x1[:, e, :], x1[:, e, :], xn[:, :], ALU.add).then_inc(x1_ok, 1)
                dve.wait_ge(x1_ok, j + 1)
                for c in range(2):
                    st = dve.bn_stats(stats[:, c, :], x1[:, e, c * BANK:(c + 1) * BANK])
                st.then_inc(bn_ok, 1)
                own(dve)
                dve.wait_ge(bn_ok, j + 1)
                dve.bn_aggr(mv[:, :], stats[:, :, :].rearrange("p a s -> p (a s)")).then_inc(b_st, 1)

            def norm(j, e):
                dve.wait_ge(b_rs, j + 1)
                dve.tensor_scalar(xn[:, :], x1[:, e, :], mv[:, 0:1], rstd[:, 0:1], ALU.subtract,
                                  ALU.mult).then_inc(xn_ok, 1)

            def modulate(j, b):
                for half in range(2):
                    dve.wait_ge(xt_ok, 2 * j + half + 1)
                    if half or not isinstance(j, int) or j:
                        dve.wait_ge(h2_hi_ok, 2 * j + half)
                        dve.wait_ge(h2_lo_ok, 2 * j + half)
                    for q in range(4):
                        kt = 4 * half + q
                        o = dve.tensor_scalar(h2t[:, q * P:(q + 1) * P], ps_t[half][:, q * P:(q + 1) * P],
                                              modcol1[:, b * 16 + 8 + kt:b * 16 + 9 + kt],
                                              modcol[:, b * 16 + kt:b * 16 + kt + 1], ALU.mult, ALU.add)
                    o.then_inc(h2t_ok, 1)

            def route(i):
                done = [0]

                def then(ins):
                    done[0] += 1
                    ins.then_inc(gate_seq, 1)
                    dve.wait_ge(gate_seq, i * GATE_STEPS + done[0])

                ex, nm, ue, sm = gsm[:, 0:E_], gsm[:, 8:9], gsm[:, 9:10], gsm[:, 10:11]
                rs, u1, th, t8, ws, wd, rw = (gsm[:, 11 + q:12 + q] for q in range(7))
                ad, w, wn = gsm[:, 18:26], gsm[:, 26:34], gsm[:, 34:42]
                dve.wait_ge(ag_ok, i + 1)
                dve.tensor_copy(ag_out[:, :], ps_qkv[:, 0:AGW]).then_inc(ag_cp, 1)
                dve.wait_ge(ag_cp, i + 2)
                dve.tensor_reduce(nm, ag_out[:, ER:ER + E_], AX_X, ALU.max, negate=True).then_inc(gate_max, 1)
                dve.wait_ge(gate_exp, 2 * i + 1)
                then(dve.tensor_scalar(u1, ue, 1.0, None, ALU.add))
                then(dve.reciprocal(th, u1))
                dve.tensor_scalar(t8, th, MAX_THRESHOLD, None, ALU.mult)
                dve.wait_ge(gate_exp, 2 * i + 2)
                then(dve.reciprocal(rs, sm))
                then(dve.tensor_scalar(ad, ex, rs, t8, ALU.mult, ALU.subtract))
                then(dve.tensor_scalar(w, ad, 0.0, 0.0, ALU.max, ALU.add, accum_out=ws))
                then(dve.scalar_tensor_tensor(wd, ws, 0.0, ws, ALU.is_equal, ALU.add))
                then(dve.reciprocal(rw, wd))
                then(dve.tensor_scalar(wn, w, rw, SCALING, ALU.mult, ALU.mult))
                assert done[0] == GATE_STEPS
                dve.tensor_tensor(hw[:, :, :], ag_out[:, 0:ER].rearrange("p (e r) -> p e r", e=E_),
                                  wn.unsqueeze(2).broadcast_to([P, E_, R_]), ALU.mult).then_inc(hw_ok, 1)

            def body(hp, e, b, bj, has_next, has_next2):
                i = tile_of(hp, e)
                if has_next:
                    residual(i + 1, *after(hp, e), bj)
                route(i)
                if has_next:
                    norm(i + 1, 1 - e)
                dve.wait_ge(hwT_hi_ok, i + 1)
                dve.tensor_tensor(hwT_lo[:, :], ps_pv[:, 0:P], hwT_hi[:, :].bitcast(F32), ALU.subtract)\
                   .then_inc(hwT_lo_ok, 1)
                if has_next:
                    modulate(i + 1, bj)
                dve.wait_ge(out_ok, i + 1)
                dve.wait_ge(y_ok, i + 1)
                dve.tensor_tensor(xn[:, :], ps_s[1][:, :], bias[:, :], ALU.add).then_inc(y_ev, 1)

            residual(0, 0, 0, 0)
            norm(0, 0)
            modulate(0, 0)
            tile_loops(dve, body)

        def phase_b_gpsimd(pool):
            pool.sem_inc(out_ok, 1)

            def rsqrt(j):
                pool.wait_ge(b_st, j + 1)
                pool.tensor_tensor(vareps[:, :], mv[:, 1:2], eps[:, :], ALU.add).then_inc(b_ve, 1)
                pool.wait_ge(b_ve, j + 1)
                pool.tensor_tensor(rstd[:, :], vareps[:, :], minus_half[:, :], ALU.pow).then_inc(b_rs, 1)

            def split_a(i):
                pool.wait_ge(a_hi_ok, i + 1)
                pool.tensor_tensor(a_lo[:, :, :], a_raw[:, :, :], a_hi[:, :, :].bitcast(F32),
                                   ALU.subtract).then_inc(a_lo_ok, 1)

            def split_h(j):
                for half in range(2):
                    pool.wait_ge(h2_hi_ok, 2 * j + half + 1)
                    hi = h2_hi[:, 4 * half:4 * half + 4, :]
                    pool.tensor_tensor(h2_lo[:, 4 * half:4 * half + 4, :], h2t[:, :].rearrange("p (k t) -> p k t", k=4),
                                       hi.bitcast(F32), ALU.subtract).then_inc(h2_lo_ok, 1)

            def body(hp, e, b, bj, has_next, has_next2):
                i = tile_of(hp, e)
                if has_next:
                    rsqrt(i + 1)
                if has_next2:
                    split_a(i + 2)
                if has_next:
                    split_h(i + 1)
                pool.wait_ge(y_ev, i + 2)
                pool.tensor_tensor(xn[:, :], xn[:, :], gb[:, b, :], ALU.mult).then_inc(y_gated, 1)
                pool.wait_ge(y_gated, i + 1)
                pool.tensor_tensor(x1[:, e, :], x1[:, e, :], xn[:, :], ALU.add).then_inc(out_ok, 1)

            split_a(0)
            rsqrt(0)
            split_a(1)
            split_h(0)
            tile_loops(pool, body)

        def own(eng):
            eng.wait_ge(c_t, 1)

        block = outer.enter_context(nc.Block())

        @block.sync
        def _(sp):
            sp.dma_start(ident[:, :], ident_c).then_inc(const_ld, 16)
            sp.dma_start(c_rows[:, :], c_in.rearrange("b (k p) -> (b k) p", p=P)).then_inc(const_ld, 16)
            sp.dma_start(rinvT[:, :], mask_c).then_inc(const_ld, 16)
            sp.dma_start(sel[:, :], sel_c).then_inc(const_ld, 16)

            def load_wmod(k):
                if k >= 2:
                    sp.wait_ge(mod_mm, k - 1)
                sp.dma_start(wm_buf[k % 2], wmod.rearrange("(k p) n -> p k n", p=P)[
                    :, :, k * BANK:(k + 1) * BANK]).then_inc(wm_ld[k % 2], 16)

            def load_x(b, tt):
                n = b * NT + tt
                if tt >= 2:
                    sp.wait_ge(ln_tr, 2 * (n - 1))
                elif b:
                    sp.wait_ge(w_hi_ok, 4 * (G * b + 1))
                    sp.wait_ge(w_lo_ok, 4 * (G * b + 1))
                sp.dma_start(xb[b][:, tt % 2, :], x_rows[n * P:(n + 1) * P, :]).then_inc(ln_x[tt % 2], 16)

            def load_w(it, g):
                if not isinstance(it, int) or it > 0:
                    sp.wait_ge(w_hi_ok, 4 * it)
                    sp.wait_ge(w_lo_ok, 4 * it)
                for j, w in enumerate((wq, wk, wv)):
                    sp.dma_start(w_raw[:, :, j, :], w.rearrange("(k p) n -> p k n", p=P)[
                        :, :, bass.ds(g * P, P)]).then_inc(w_ld, 16)

            def stack(half):
                cols = slice(half * (S // 2), (half + 1) * (S // 2))
                for h in range(GH):
                    parts = qkT[h * HD:(h + 1) * HD, :, :, cols].rearrange("p j a s -> p (j a) s")
                    for r, pair in enumerate((slice(0, 3, 2), slice(1, 3), slice(0, 4, 3))):
                        sp.dma_start(qk_stack[r * HD:(r + 1) * HD, :, h, cols].bitcast(F32), parts[:, pair, :])\
                          .then_inc(stacked[half][h], 16)

            def stack_half(it, half):
                own(sp)
                if not isinstance(it, int) or it:
                    sp.wait_ge(s_ok, HU * it)
                sp.wait_ge(qk_hi, 8 * it + 4 * half + 4)
                sp.wait_ge(qk_lo, 8 * it + 4 * half + 4)
                stack(half)

            def store_attn(it, b, g):
                sp.wait_ge(at_ok, 8 * it + 8 + 1)
                sp.dma_start(attn_dram[bass.ds(g * P, P), b * S:(b + 1) * S], attnT[:, :]).then_inc(at_st, 16)

            def store_mod(k):
                sp.wait_ge(mod_rw, k + 1)
                sp.dma_start(mod_dram[:, k * BANK:(k + 1) * BANK], mod_row).then_inc(mod_st, 16)

            load_wmod(0)
            load_wmod(1)
            load_x(0, 0)
            load_x(0, 1)
            load_w(0, 0)
            load_wmod(2)
            sp.dma_start(rope_tab[:, :, :, :, :], rope_c).then_inc(rope_ld, 16)
            load_wmod(3)
            for k in range(4):
                store_mod(k)
            sp.wait_ge(mod_st, 16 * 4)
            for b in range(B):
                sp.dma_start(mcol_rows[b * 16:(b + 1) * 16, :], mod_dram[b, 0:2 * D].rearrange(
                    "(r p) -> r p", p=P)).then_inc(mcol_ld, 16)
            load_wmod(4)
            load_wmod(5)
            for tt in range(2, NT):
                load_x(0, tt)
            for k in range(4, MODC):
                if k + 2 < MODC:
                    load_wmod(k + 2)
                store_mod(k)
            load_w(1, 1)
            stack_half(0, 0)
            for b in range(B):
                it0 = b * G

                def stores(it, g, following):
                    stack_half(it, 1)
                    if following is not None:
                        load_w(it + 2, following)
                    stack_half(it + 1, 0)
                    store_attn(it, b, g)

                with sp.Fori(0, G - 2) as g:
                    stores(g + it0, g, g + 2)
                stores(it0 + G - 2, G - 2, None if b else 0)
                stack_half(it0 + G - 1, 1)
                if b == 0:
                    for tt in range(NT):
                        load_x(1, tt)
                    sp.wait_ge(ln_hi, 2 * NT * B)
                    sp.wait_ge(ln_lo, 2 * NT * B)
                    load_w(G + 1, 1)
                    stack_half(G, 0)
                store_attn(it0 + G - 1, b, G - 1)
            sp.wait_ge(at_st, 16 * (B * G + 1))
            sp.wait_ge(mod_st, 16 * MODC)
            phase_b_sync(sp)

        @block.tensor
        def _(pe):
            pe.wait_ge(const_ld, 64)
            pe.transpose(ps_pv[:, 0:B * KT], c_rows[:, :], ident[0:B * KT, 0:B * KT]).then_inc(c_t, 1)

            def mod_chunk(k):
                if k == 0:
                    pe.wait_ge(c_done, 2)
                pe.wait_ge(wm_ld[k % 2], 16 * (k // 2 + 1))
                if k:
                    pe.wait_ge(mod_ev, k)
                for kt in range(KT):
                    j = kt % 4
                    mm = pe.matmul(ps_s[0][j * HD:(j + 1) * HD, 0:BANK], c_pad[:, kt, :], wm_buf[k % 2][:, kt, :],
                                   start=(kt < 4), stop=(kt >= 4), tile_position=(0, j * HD))
                mm.then_inc(mod_mm, 1)

            def mod_rows(k):
                pe.wait_ge(mod_ev, k + 1)
                if k:
                    pe.wait_ge(mod_rw, k)
                pe.matmul(ps_pv[0:B, 0:BANK], sel[:, :], mod_part, start=True, stop=True).then_inc(mod_sum, 1)

            def ln_half(b, tt, half, bank):
                n = b * NT + tt
                pe.wait_ge(ln_xn, n + 1)
                for j in range(4):
                    kt = 4 * half + j
                    mm = pe.transpose(bank[:, j * P:(j + 1) * P], xb[b][:, tt % 2, kt * P:(kt + 1) * P], ident[:, :])
                mm.then_inc(ln_tr, 1)

            def qkv(it, tt, kts, b=None):
                if kts[0] == 0:
                    if b is not None:
                        done = tt + 1 if tt < EARLY - 1 else NT
                        pe.wait_ge(ln_hi, 2 * (b * NT + done))
                        pe.wait_ge(ln_lo, 2 * (b * NT + done))
                    if b == 0 and tt == 0:
                        pe.wait_ge(ln_tt, 2 * NT)
                    if not isinstance(it, int) or it or tt:
                        pe.wait_ge(qkv_cp, 8 * it + tt)
                for kt in kts:
                    if tt == 0 and kt % 2 == 0:
                        pe.wait_ge(w_hi_ok, 4 * it + kt // 2 + 1)
                        pe.wait_ge(w_lo_ok, 4 * it + kt // 2 + 1)
                    hh, hl = (h[:, kt, tt * P:(tt + 1) * P] for h in (hT_hi, hT_lo))
                    pe.matmul(ps_qkv[:, 0:3 * P], hh, w_hi[:, kt, :], start=(kt == 0), stop=False)
                    pe.matmul(ps_qkv[:, 0:3 * P], hh, w_lo[:, kt, :], start=False, stop=False)
                    mm = pe.matmul(ps_qkv[:, 0:3 * P], hl, w_hi[:, kt, :], start=False, stop=(kt == KT - 1))
                    if tt == NT - 1 and kt % 2 and kt < KT - 1:
                        mm.then_inc(w_used, 1)
                if kts[-1] == KT - 1:
                    mm.then_inc(qkv_mm, 1)

            def ring_free(st, r, its):
                it = its[0]
                if r < 2:
                    if not isinstance(it, int) or it:
                        pe.wait_ge(ev["dve"], EVAC["dve"] * it + 1)
                        pe.wait_ge(ev["act"], EVAC["act"] * it + 1)
                    pe.wait_ge(qk_lo, 8 * it + EARLY - 1)
                    return
                was = st.ring[r - 2]
                if was[0] == "qk":
                    pe.wait_ge(qk_lo, 8 * its[was[1]] + was[2] + 1)
                elif was[0] == "norm":
                    pe.wait_ge(ln_tt, 2 * (NT + was[1]) + was[2])
                else:
                    eng, num = PLAN[was[1:]][:2]
                    pe.wait_ge(ev[eng], EVAC[eng] * it + num + 2)

            def qk_transpose(it_q, tt, bank):
                pe.wait_ge(roped, 16 * it_q + 2 * tt + 2)
                pe.transpose(bank[:, 0:P], qk_rot[:, tt % 2, 0:P], ident[:, :])
                pe.transpose(bank[:, P:2 * P], qk_rot[:, tt % 2, P:2 * P], ident[:, :]).then_inc(qk_t, 1)

            def scores(it, n):
                qt, h = n // GH, n % GH
                if n % (HU // 2) < GH:
                    pe.wait_ge(stacked[n // (HU // 2)][h], STACKING * (it + 1))
                pe.wait_ge(exp_ok, HU * it + n + 1)
                w = (qt + 1) * P
                for c0 in range(0, w, BANK):
                    c1 = min(w, c0 + BANK)
                    pe.matmul(ps_s[n % 2][:, c0:c1], qk_stack[:, 0, h, qt * P:(qt + 1) * P], qk_stack[:, 1, h, c0:c1],
                              start=True, stop=(c1 < w))
                pe.matmul(ps_s[n % 2][:, w - P:w], ident16[:, :], mask[:, :], start=False, stop=True).then_inc(s_ok, 1)

            def turn(st, its, n):
                h = n % GH
                pe.wait_ge(exp_ok, HU * its[0] + n + 1 + 2)
                for c, (k0, m) in enumerate(chunks_of(n)):
                    r = st.place["probs", n, c]
                    ring_free(st, r, its)
                    for j in range(m):
                        mm = pe.transpose(ps_t[r % 2][:, j * P:(j + 1) * P], probs[:, h, (k0 + j) * P:(k0 + j + 1) * P],
                                          ident[:, :])
                    mm.then_inc(t_ok, 1)

            def values(it, u):
                for eng in ("dve", "act"):
                    done = max(num for (n, c), (e, num, *_) in PLAN.items() if e == eng and n // GH <= u)
                    pe.wait_ge(ev[eng], EVAC[eng] * it + done + 2)
                if u == 0:
                    pe.wait_ge(v_ok, 2 * it + 1)
                if u == EARLY - 1:
                    pe.wait_ge(v_ok, 2 * it + 2)
                if u >= EARLY:
                    pe.wait_ge(v_cp, 8 * it + u + 1)
                pe.wait_ge(at_ok, 8 * it + u + 1)
                pe.wait_ge(rinv_ok, 8 * it + u + 1)
                for kt in range(u + 1):
                    for h in range(GH):
                        pe.matmul(ps_pv[h * HD:(h + 1) * HD, 0:P], v_now[:, kt, h * HD:(h + 1) * HD],
                                  probsT[:, kt, h, :], start=(kt == 0), stop=(kt == u), tile_position=(0, h * HD))
                pe.transpose(ps_pv[:, P:2 * P], rinv_wide[:, :, :].rearrange("p h d -> p (h d)"),
                             ident[:, :]).then_inc(pv_ok, 1)

            def attention(st, its):
                it = its[0]
                for n in range(st.last):
                    if n < HU:
                        scores(it, n)
                    if n in st.quarters:
                        for w, tt, q in st.quarters[n]:
                            qkv(its[w], tt, [2 * q, 2 * q + 1], 1 if st.norm and w else None)
                    if n in st.norm and st.norm[n][1]:
                        tt, j = st.norm[n]
                        r = st.place["norm", tt, j]
                        ring_free(st, r, its)
                        ln_half(1, tt, j - 1, ps_t[r % 2])
                    if n >= 6 and (n - 6) % 4 == 0 and (n - 6) // 4 < NT:
                        values(it, (n - 6) // 4)
                    if 0 <= n - 2 < HU:
                        turn(st, its, n - 2)
                    if n in st.qk:
                        w, tt = st.qk[n]
                        r = st.place["qk", w, tt]
                        ring_free(st, r, its)
                        qk_transpose(its[w], tt, ps_t[r % 2])

            for k in range(4):
                mod_chunk(k)
                mod_rows(k)
            pe.wait_ge(mcol_ld, 32)
            pe.wait_ge(mod_rw, 4)
            pe.transpose(ps_pv[:, 0:4 * KT], mcol_rows[:, :], ident[0:4 * KT, 0:4 * KT]).then_inc(mcol_t, 1)
            for tt in range(NT):
                for half in range(2):
                    if tt or half:
                        pe.wait_ge(ln_tt, 2 * tt + half)
                    ln_half(0, tt, half, ps_qkv)

            def first_qk(tt):
                if tt >= 2:
                    pe.wait_ge(qk_lo, tt - 1)
                qk_transpose(0, tt, ps_t[tt % 2])

            chunk = 4
            for tt in range(EARLY):
                qkv(0, tt, list(range(KT)), 0)
                if tt:
                    first_qk(tt - 1)
                if tt == 0:
                    pe.wait_ge(mcol, 1)
                for _ in range(MOD_BETWEEN[tt]):
                    mod_chunk(chunk)
                    mod_rows(chunk)
                    chunk += 1
            pe.wait_ge(mod_rw, MODC)
            for b in range(B):
                it0 = b * G
                with pe.Fori(0, G - 1) as g:
                    attention(INNER, (g + it0, g + (it0 + 1)))
                attention(FINAL if b else HANDOVER, (it0 + G - 1, it0 + G))
            phase_b_tensor(pe)

        @block.scalar
        def _(act):
            act.sem_inc(exp_ok, 2)
            act.sem_inc(ev["act"], 1)
            act.wait_ge(c_t, 1)
            act.activation(c_e[:, :], ps_pv[:, 0:B * KT], ACT.Exp, scale=-1.0).then_inc(c_ex, 1)

            def mod_out(k):
                act.wait_ge(mod_mm, k + 1)
                if k:
                    act.wait_ge(mod_sum, k)
                act.copy(mod_part, ps_s[0][:, 0:BANK]).then_inc(mod_ev, 1)

            def ln_split(b, tt, half):
                n = 2 * (b * NT + tt) + half
                act.wait_ge(ln_tt, n + 1)
                act.copy(hT_hi[:, 4 * half:4 * half + 4, tt * P:(tt + 1) * P],
                         ht[b][:, half, :].rearrange("p (k t) -> p k t", k=4)).then_inc(ln_hi, 1)

            def split_w(it, q):
                if q == 0:
                    act.wait_ge(w_ld, 48 * (it + 1))
                if not isinstance(it, int) or it:
                    if q < 3:
                        act.wait_ge(w_used, 3 * it - 2 + q)
                    else:
                        act.wait_ge(qkv_mm, 8 * it)
                act.copy(w_hi[:, 2 * q:2 * q + 2, :], w_raw[:, 2 * q:2 * q + 2, :, :].rearrange(
                    "p k j n -> p k (j n)")).then_inc(w_hi_ok, 1)

            def copy_qkv(it, tt):
                act.wait_ge(qkv_mm, 8 * it + tt + 1)
                if not isinstance(it, int) or 8 * it + tt >= 2:
                    act.wait_ge(v_cp, 8 * it + tt - 1)
                act.copy(qkv_sb[:, tt % 2, :], ps_qkv[:, 0:3 * P]).then_inc(qkv_cp, 1)

            def qk_split(it, tt, bank):
                act.wait_ge(qk_t, 8 * it + tt + 1)
                if not isinstance(it, int) or it:
                    if tt % 4 == 0:
                        for h in range(GH):
                            act.wait_ge(stacked[tt // 4][h], STACKING * it)
                act.copy(qkT[:, :, 0, tt * P:(tt + 1) * P].bitcast(F32R),
                         bank[:, 0:2 * P].rearrange("p (j t) -> p j t", j=2)).then_inc(qk_hi, 1)

            def softmax_exp(it, n):
                qt, h = n // GH, n % GH
                w = (qt + 1) * P
                act.wait_ge(max_ok, HU * it + n + 1)
                before = max((PLAN[k][2] + 1 for k in PLAN if k[0] <= n - GH), default=0)
                act.wait_ge(t_ok, TCHUNKS * it + before + 1)
                act.activation(probs[:, h, 0:w], ps_s[n % 2][:, 0:w], ACT.Exp, bias=nmax[:, n:n + 1], scale=1.0,
                               accum_out=sums[:, n:n + 1]).then_inc(exp_ok, 1)

            def evac(it, n, c, bank):
                eng, num, at, k0, m = PLAN[n, c]
                act.wait_ge(t_ok, TCHUNKS * it + at + 2)
                act.wait_ge(pv_ok, 8 * it + n // GH + 1)
                act.copy(probsT[:, k0:k0 + m, n % GH, :],
                         bank[:, 0:m * P].rearrange("p (k q) -> p k q", k=m)).then_inc(ev["act"], 1)

            def attention(st, its):
                it = its[0]
                for n in range(st.last):
                    if n in st.split:
                        split_w(its[1], st.split[n])
                    if n in st.ends:
                        w, tt = st.ends[n]
                        copy_qkv(its[w], tt)
                    if n < HU:
                        softmax_exp(it, n)
                    if n in st.norm and st.norm[n][1]:
                        tt, j = st.norm[n]
                        ln_split(1, tt, j - 1)
                    if n >= 6 and (n - 6) % 4 == 0 and (n - 6) // 4 < NT:
                        act.wait_ge(pv_ok, 8 * it + (n - 6) // 4 + 2)
                        act.copy(rinvT[:, :], ps_pv[:, P:2 * P]).then_inc(rinvT_ok, 1)
                    if 0 <= n - 2 < HU:
                        for c in range(len(chunks_of(n - 2))):
                            if PLAN[n - 2, c][0] == "act":
                                evac(it, n - 2, c, ps_t[st.place["probs", n - 2, c] % 2])
                    if n in st.qk:
                        w, tt = st.qk[n]
                        qk_split(its[w], tt, ps_t[st.place["qk", w, tt] % 2])

            for k in range(4):
                mod_out(k)
            for tt in range(NT):
                for half in range(2):
                    ln_split(0, tt, half)
            for q in range(4):
                split_w(0, q)
            chunk = 4
            for tt in range(EARLY):
                copy_qkv(0, tt)
                if tt:
                    qk_split(0, tt - 1, ps_t[(tt - 1) % 2])
                for _ in range(MOD_BETWEEN[tt]):
                    mod_out(chunk)
                    chunk += 1
            for b in range(B):
                it0 = b * G
                with act.Fori(0, G - 1) as g:
                    attention(INNER, (g + it0, g + (it0 + 1)))
                attention(FINAL if b else HANDOVER, (it0 + G - 1, it0 + G))
            phase_b_scalar(act)

        @block.vector
        def _(dve):
            dve.sem_inc(ev["dve"], 1)
            dve.sem_inc(at_ok, 1)
            dve.sem_inc(t_ok, 1)
            dve.sem_inc(pv_ok, 1)
            dve.sem_inc(at_st, 16)

            def then(ins):
                seq["dve"] += 1
                ins.then_inc(dve_seq, 1)
                dve.wait_ge(dve_seq, seq["dve"])

            dve.memset(c_pad[:, :, :], 0.0).then_inc(dve_seq, 1)
            seq["dve"] += 1
            dve.wait_ge(const_ld, 64)
            dve.tensor_copy(mask[:, :], rinvT[:, :])
            dve.tensor_copy(ident16[:, :], ident[:, :]).then_inc(c_done, 1)
            dve.wait_ge(c_ex, 1)
            then(dve.tensor_scalar(c_e1[:, :], c_e[:, :], 1.0, None, ALU.add))
            then(dve.reciprocal(c_sig[:, :], c_e1[:, :]))
            dve.tensor_tensor(c_pad[:, :, 0:B].rearrange("p k b -> p b k"),
                              ps_pv[:, 0:B * KT].rearrange("p (b k) -> p b k", b=B),
                              c_sig[:, :].rearrange("p (b k) -> p b k", b=B), ALU.mult).then_inc(c_done, 1)

            def mod_store(k):
                dve.wait_ge(mod_sum, k + 1)
                if k:
                    dve.wait_ge(mod_st, 16 * k)
                dve.tensor_copy(mod_row, ps_pv[0:B, 0:BANK]).then_inc(mod_rw, 1)

            def ln_norm(b, tt):
                n = b * NT + tt
                xt = xb[b][:, tt % 2, :]
                dve.wait_ge(ln_x[tt % 2], 16 * (b * NT // 2 + tt // 2 + 1))
                for i in range(2):
                    st = dve.bn_stats(stats[:, i, :], xt[:, i * BANK:(i + 1) * BANK])
                then(st)
                dve.bn_aggr(mv[:, :], stats[:, :, :].rearrange("p a s -> p (a s)")).then_inc(ln_st, 1)
                dve.wait_ge(ln_st, n + 1)
                dve.wait_ge(ln_rs, n + 1)
                dve.tensor_scalar(xt, xt, mv[:, 0:1], rstd[:, 0:1], ALU.subtract, ALU.mult).then_inc(ln_xn, 1)

            def ln_mod(b, tt, half, bank):
                n = 2 * (b * NT + tt) + half
                dve.wait_ge(ln_tr, n + 1)
                if n >= 2:
                    dve.wait_ge(ln_hi, n - 1)
                    dve.wait_ge(ln_lo, n - 1)
                for j in range(4):
                    kt = 4 * half + j
                    o = dve.tensor_scalar(ht[b][:, half, j * P:(j + 1) * P], bank[:, j * P:(j + 1) * P],
                                          modcol1[:, b * 16 + 8 + kt:b * 16 + 9 + kt],
                                          modcol[:, b * 16 + kt:b * 16 + kt + 1], ALU.mult, ALU.add)
                o.then_inc(ln_tt, 1)

            def rest_w(it, q):
                dve.wait_ge(w_hi_ok, 4 * it + q + 1)
                ks = slice(2 * q, 2 * q + 2)
                dve.tensor_tensor(w_lo[:, ks, :], w_raw[:, ks, :, :].rearrange("p k j n -> p k (j n)"),
                                  w_hi[:, ks, :].bitcast(F32), ALU.subtract).then_inc(w_lo_ok, 1)

            def qk_rest(it, tt, bank):
                dve.wait_ge(qk_hi, 8 * it + tt + 1)
                dve.tensor_tensor(qkT[:, :, 1, tt * P:(tt + 1) * P].bitcast(F32R),
                                  bank[:, 0:2 * P].rearrange("p (j t) -> p j t", j=2),
                                  qkT[:, :, 0, tt * P:(tt + 1) * P], ALU.subtract).then_inc(qk_lo, 1)

            def row_max(it, n):
                w = (n // GH + 1) * P
                dve.wait_ge(s_ok, HU * it + n + 1)
                dve.tensor_reduce(nmax[:, n:n + 1], ps_s[n % 2][:, 0:w], AX_X, ALU.max, negate=True).then_inc(max_ok, 1)

            def evac(it, n, c, bank):
                eng, num, at, k0, m = PLAN[n, c]
                dve.wait_ge(t_ok, TCHUNKS * it + at + 2)
                dve.wait_ge(pv_ok, 8 * it + n // GH + 1)
                dve.tensor_copy(probsT[:, k0:k0 + m, n % GH, :],
                                bank[:, 0:m * P].rearrange("p (k q) -> p k q", k=m)).then_inc(ev["dve"], 1)

            def invert(it, u):
                dve.wait_ge(exp_ok, HU * it + GH * (u + 1) + 2)
                dve.reciprocal(rinv[:, :], sums[:, GH * u:GH * (u + 1)]).then_inc(inv_ok, 1)
                dve.wait_ge(inv_ok, 8 * it + u + 1)
                dve.wait_ge(pv_ok, 8 * it + u + 1)
                dve.tensor_copy(rinv_wide[:, :, :], rinv[:, :].unsqueeze(2).broadcast_to([P, GH, HD]))\
                   .then_inc(rinv_ok, 1)

            def normalise(it, u):
                dve.wait_ge(rinvT_ok, 8 * it + u + 1)
                if u == 0:
                    dve.wait_ge(at_st, 16 * it + 16)
                dve.tensor_tensor(attnT[:, u * P:(u + 1) * P], ps_pv[:, 0:P], rinvT[:, :], ALU.mult).then_inc(at_ok, 1)

            def place_v(it):
                dve.wait_ge(v_cp, 8 * it + EARLY - 1)
                dve.wait_ge(pv_ok, 8 * it + 1)
                dve.tensor_copy(v_now[:, 0:EARLY - 1, :], v_next[:, 0:EARLY - 1, :]).then_inc(v_ok, 1)

            def place_last_v(it):
                dve.wait_ge(v_cp, 8 * it + EARLY)
                dve.tensor_copy(v_now[:, EARLY - 1, :], v_next[:, EARLY - 1, :]).then_inc(v_ok, 1)

            def attention(st, its):
                it = its[0]
                for n in range(st.last):
                    if n == 0:
                        place_v(it)
                    if n == 9:
                        place_last_v(it)
                    if n < HU:
                        row_max(it, n)
                    if n in st.split:
                        rest_w(its[1], st.split[n])
                    if n in st.norm:
                        tt, j = st.norm[n]
                        if j == 0:
                            ln_norm(1, tt)
                        else:
                            ln_mod(1, tt, j - 1, ps_t[st.place["norm", tt, j] % 2])
                    if n >= 7 and (n - 7) % 4 == 0 and (n - 7) // 4 < NT:
                        normalise(it, (n - 7) // 4)
                    if n >= 5 and (n - 5) % 4 == 0 and (n - 5) // 4 < NT:
                        invert(it, (n - 5) // 4)
                    if 0 <= n - 2 < HU:
                        for c in range(len(chunks_of(n - 2))):
                            if PLAN[n - 2, c][0] == "dve":
                                evac(it, n - 2, c, ps_t[st.place["probs", n - 2, c] % 2])
                    if n in st.qk:
                        w, tt = st.qk[n]
                        qk_rest(its[w], tt, ps_t[st.place["qk", w, tt] % 2])

            for k in range(4):
                mod_store(k)
            dve.wait_ge(mcol_t, 1)
            dve.tensor_copy(modcol[:, :], ps_pv[:, 0:4 * KT])
            then(dve.tensor_scalar(modcol1[:, :], ps_pv[:, 0:4 * KT], 1.0, None, ALU.add))
            dve.sem_inc(mcol, 1)
            for tt in range(NT):
                ln_norm(0, tt)
                ln_mod(0, tt, 0, ps_qkv)
                ln_mod(0, tt, 1, ps_qkv)
            for q in range(4):
                rest_w(0, q)
            chunk = 4
            for tt in range(EARLY):
                if tt:
                    qk_rest(0, tt - 1, ps_t[(tt - 1) % 2])
                for _ in range(MOD_BETWEEN[tt]):
                    mod_store(chunk)
                    chunk += 1
            dve.wait_ge(mod_mm, MODC)
            dve.wait_ge(mod_st, 16 * MODC)
            for b in range(B):
                it0 = b * G
                with dve.Fori(0, G - 1) as g:
                    attention(INNER, (g + it0, g + (it0 + 1)))
                attention(FINAL if b else HANDOVER, (it0 + G - 1, it0 + G))
            phase_b_vector(dve)

        @block.gpsimd
        def _(pool):
            pool.memset(eps[:, :], EPS)
            pool.memset(minus_half[:, :], -0.5).then_inc(pool_half, 1)
            pool.wait_ge(pool_half, 1)

            def ln_rstd(b, tt):
                n = b * NT + tt
                pool.wait_ge(ln_st, n + 1)
                pool.tensor_tensor(vareps[:, :], mv[:, 1:2], eps[:, :], ALU.add).then_inc(pool_ve, 1)
                pool.wait_ge(pool_ve, n + 1)
                pool.tensor_tensor(rstd[:, :], vareps[:, :], minus_half[:, :], ALU.pow).then_inc(ln_rs, 1)

            def ln_rest(b, tt, half):
                n = 2 * (b * NT + tt) + half
                pool.wait_ge(ln_hi, n + 1)
                hi = hT_hi[:, 4 * half:4 * half + 4, tt * P:(tt + 1) * P]
                pool.tensor_tensor(hT_lo[:, 4 * half:4 * half + 4, tt * P:(tt + 1) * P],
                                   ht[b][:, half, :].rearrange("p (k t) -> p k t", k=4), hi.bitcast(F32),
                                   ALU.subtract).then_inc(ln_lo, 1)

            def rotate(it, tt):
                if tt == 0 and (not isinstance(it, int) or it):
                    pool.wait_ge(v_ok, 2 * it)
                if tt == EARLY:
                    pool.wait_ge(pv_ok, 8 * it + 1)
                pool.wait_ge(qkv_cp, 8 * it + tt + 1)
                src = qkv_sb[:, tt % 2, :]
                pairs = src[:, 0:2 * P].rearrange("p (j h d) -> p j h d", j=2, h=GH)
                if not isinstance(it, int) or 8 * it + tt:
                    pool.wait_ge(roped, 16 * it + 2 * tt)
                for i, dst in enumerate((rope_a, rope_b)):
                    for j in range(2):
                        tab = rope_tab[:, i, tt, j, :].unsqueeze(1).broadcast_to([P, GH, HD])
                        pool.tensor_tensor(dst[:, j * P:(j + 1) * P].rearrange("p (h d) -> p h d", h=GH),
                                           pairs[:, j], tab, ALU.mult).then_inc(pool_seq, 1)
                pool.wait_ge(pool_seq, 4 * (8 * it + tt + 1))
                if not isinstance(it, int) or 8 * it + tt >= 2:
                    pool.wait_ge(qk_t, 8 * it + tt - 1)
                for i, (t, op) in enumerate(((rope_a, ALU.subtract), (rope_b, ALU.add))):
                    v = t[:, :].rearrange("p (g i e) -> p g i e", g=2 * GH, e=2)
                    dst = qk_rot[:, tt % 2, :].rearrange("p (g e i) -> p g e i", g=2 * GH, e=2)[:, :, i, :]
                    pool.tensor_tensor(dst, v[:, :, :, 0], v[:, :, :, 1], op).then_inc(roped, 1)
                v_to = v_next if tt < EARLY else v_now
                pool.tensor_copy(v_to[:, tt, :], src[:, 2 * P:3 * P]).then_inc(v_cp, 1)

            def attention(st, its):
                it = its[0]
                for n in range(st.last):
                    if n in st.norm:
                        tt, j = st.norm[n]
                        if j == 0:
                            ln_rstd(1, tt)
                        else:
                            ln_rest(1, tt, j - 1)
                    if n in st.ends:
                        w, tt = st.ends[n]
                        rotate(its[w], tt)

            for tt in range(NT):
                ln_rstd(0, tt)
                ln_rest(0, tt, 0)
                ln_rest(0, tt, 1)
            pool.wait_ge(rope_ld, 16)
            for tt in range(EARLY):
                rotate(0, tt)
            for b in range(B):
                it0 = b * G
                with pool.Fori(0, G - 1) as g:
                    attention(INNER, (g + it0, g + (it0 + 1)))
                attention(FINAL if b else HANDOVER, (it0 + G - 1, it0 + G))
            phase_b_gpsimd(pool)


_INS = ['L0_attn_x', 'L0_attn_wq', 'L0_attn_wk', 'L0_attn_wv', 'L0_attn_wo', 'L0_ffn_W_base', 'L0_ffn_b_base',
        'L0_ffn_W_gate', 'L0_ffn_W_thr', 'L0_ffn_b_thr', 'L0_ffn_A_w', 'L0_ffn_B_w', 'L0_c', 'L0_wmod']


def shape_constants():
    import numpy as np

    inv = 1.0 / 10000.0 ** (np.arange(0, HD, 2).astype(np.float32) / HD)
    f = np.outer(np.arange(S), inv).astype(np.float32)
    cos, sin = np.cos(f), np.sin(f)
    tabs = np.stack([np.stack([cos, sin], -1), np.stack([sin, cos], -1)]).reshape(2, NT, P, HD)
    scale = np.float32(1.0) / np.sqrt(np.float32(HD))
    rope = np.stack([tabs * scale, tabs], 3).transpose(2, 0, 1, 3, 4)
    q, k = np.arange(P)[:, None], np.arange(P)[None, :]
    return {
        "rope": np.ascontiguousarray(rope, np.float32),
        "ident": np.eye(P, dtype=np.float32),
        "mask": np.where(k > q, np.float32(MASKED), np.float32(0)),
        "sel": (np.arange(P)[:, None] % HD == np.arange(B)[None, :]).astype(np.float32),
    }


def kernel(**inputs):
    import numpy as np
    import concourse.bacc as bacc
    from concourse.bass_utils import run_bass_kernel_spmd

    nc = bacc.Bacc("TRN2", target_bir_lowering=False, num_devices=1)
    arrays, args = {}, []
    for name, a in [(n, inputs[n]) for n in _INS] + list(shape_constants().items()):
        a = np.ascontiguousarray(a)
        arrays[f"in_{name}_dram"] = a
        args.append(nc.dram_tensor(f"in_{name}_dram", a.shape, mybir.dt.from_np(a.dtype), kind="ExternalInput").ap())
    args.append(nc.dram_tensor("out_0_dram", (B, S, D), F32, kind="ExternalOutput").ap())
    adaln_block(nc, *args)
    r = run_bass_kernel_spmd(nc, [arrays], core_ids=[0])
    return r.results[0]["out_0_dram"]
```

```python
from contextlib import ExitStack

import concourse.bass as bass
from concourse import mybir

F32 = mybir.dt.float32
F32R = mybir.dt.float32r
BF16 = mybir.dt.bfloat16
ALU = mybir.AluOpType
ACT = mybir.ActivationFunctionType
AX_X = mybir.AxisListType.X

P = 128
B, S, D = 2, 1024, 1024
H, HD = 32, 32
GH = P // HD
G = H // GH
NT = S // P
KT = D // P
BANK = 512
E_, R_ = 8, 16
ER = E_ * R_
EPS = 1e-5
SCALING = 2.0
MAX_THRESHOLD = 0.125
MASKED = -1e30
AGW = ER + 10
MODC = 6 * D // BANK
HU = GH * NT
EARLY = 7


def chunks_of(n):
    kts = n // GH + 1
    return [(k0, min(4, kts - k0)) for k0 in range(0, kts, 4)]


def attention_plan():
    plan, count = {}, {"dve": 0, "act": 0}
    at = 0
    for n in range(HU):
        for c, (k0, m) in enumerate(chunks_of(n)):
            eng = ("dve", "act")[(n + c) % 2] if n < HU // 2 else ("dve", "act")[c]
            plan[n, c] = (eng, count[eng], at, k0, m)
            count[eng] += 1
            at += 1
    return plan, count, at


PLAN, EVAC, TCHUNKS = attention_plan()
FIRST_MOD = 2 * D // BANK
GATE_CHUNKS = [k for k in range(MODC) if k * BANK // D in (2, 5)]
assert NT == MODC - FIRST_MOD and EARLY == NT - 1


SKIP, LAST_QK = (19, 23, 27), 2


NORM_STEPS = [("stats", 0), ("norm", 1), (("turn", 0), 3), (("scale", 0), 3), (("turn", 1), 4), (("split", 0), 4),
              (("scale", 1), 5), (("split", 1), 6)]


class Steps:

    def __init__(self, following, norm=False, wo=False):
        self.quarters = {n: [(0, EARLY + n // 4, n % 4)] for n in range(4 * (NT - EARLY))}
        if following:
            if norm:
                free = list(range(18, HU)) + [n for n in range(HU, 99) for _ in range(2)]
            else:
                free = [n for n in range(4, HU + 3) if n not in SKIP]
            for m, n in zip(range(4 * EARLY), free):
                self.quarters.setdefault(n, []).append((1, m // 4, m % 4))
        self.ends = {n: e[:2] for n, es in self.quarters.items() for e in es if e[2] == 3}
        self.qk = {}
        for n, e in self.ends.items():
            if e != (1, EARLY - 1):
                self.qk[min([v for v in range(6, HU + 4, 4) if v >= n + 3], default=n + 3)] = e
        self.qk[LAST_QK] = (0, EARLY - 1)
        self.last = max(HU + 4, max(self.quarters) + 1, max(self.qk) + 1)
        self.split = {1 + q: q for q in range(4)} if following else {}
        self.norm = {}
        if norm:
            for tt in range(NT):
                for what, at in NORM_STEPS:
                    self.norm.setdefault(10 + 3 * tt + at, []).append((tt, what))
        self.wo = {6 + 3 * k: k for k in range(KT)} if wo else {}
        self.ring = []
        for n in range(self.last):
            self.ring += [("norm", tt, what[1]) for tt, what in self.norm.get(n, ()) if what[0] == "turn"]
            if n in self.qk:
                self.ring.append(("qk", *self.qk[n]))
            if 0 <= n - 2 < HU:
                self.ring += [("probs", n - 2, c) for c in range(len(chunks_of(n - 2)))]
        self.place = {u: i for i, u in enumerate(self.ring)}


INNER, HANDOVER, FINAL = Steps(True), Steps(True, norm=True), Steps(False, wo=True)


def adaln_block(nc, x_in, wq, wk, wv, wo, W_base, b_base, W_gate, W_thr, b_thr, A_w, B_w, c_in, wmod,
                rope_c, ident_c, mask_c, sel_c, out):
    attn_dram = nc.dram_tensor("attn_scratch", [D, B * S], F32, kind="Internal").ap()
    mod_dram = nc.dram_tensor("mod_scratch", [B, 6 * D], F32, kind="Internal").ap()
    x_rows = x_in.rearrange("b s d -> (b s) d")
    out_rows = out.rearrange("b s d -> (b s) d")

    outer = ExitStack()
    with outer:
        def sem(name):
            return outer.enter_context(nc.semaphore(name))

        def keep(name, shape, dt):
            return outer.enter_context(nc.sbuf_tensor(name, shape, dt))

        def psum(name, cols):
            return outer.enter_context(nc.psum_tensor(name, [P, cols], F32))

        ps_s = [psum("ps_s0", 2 * BANK), psum("ps_s1", 2 * BANK)]
        ps_t = [psum("ps_t0", BANK), psum("ps_t1", BANK)]
        ps_qkv = psum("ps_qkv", BANK)
        ps_pv = psum("ps_pv", BANK)

        ident = keep("ident", [P, P], F32)
        modcol = keep("modcol", [P, 4 * KT], F32)
        modcol1 = keep("modcol1", [P, 4 * KT], F32)
        mcol_rows = keep("mcol_rows", [4 * KT, P], F32)
        stats = keep("stats", [P, 2, 6], F32)
        mv = keep("mv", [P, 2], F32)
        vareps = keep("vareps", [P, 1], F32)
        minus_half = keep("minus_half", [P, 1], F32)
        eps = keep("eps", [P, 1], F32)
        rstd = keep("rstd", [P, 1], F32)

        start = ExitStack()
        wm_more = start.enter_context(nc.sbuf_tensor("wm_more", [P, 2, KT, BANK], F32))
        x_start = start.enter_context(nc.sbuf_tensor("x_start", [P, 2, D], F32))
        h_start = start.enter_context(nc.sbuf_tensor("h_start", [P, 2, BANK], F32))
        start.close()

        phase_a = ExitStack()

        def sb(name, shape, dt):
            return phase_a.enter_context(nc.sbuf_tensor(name, shape, dt))

        hT_hi = sb("hT_hi", [P, KT, S], F32R)
        qk_stack = sb("qk_stack", [3 * HD, 2, GH, S], F32R)
        hT_lo = sb("hT_lo", [P, KT, S], F32R)
        w_raw = sb("w_raw", [P, KT, 3, P], F32)
        w_hi = sb("w_hi", [P, KT, 3 * P], F32R)
        w_lo = sb("w_lo", [P, KT, 3 * P], F32R)
        qkv_sb = sb("qkv_sb", [P, 2, 3 * P], F32)
        qk_rot = sb("qk_rot", [P, 2, 2 * P], F32)
        rope_a = sb("rope_a", [P, 2 * P], F32)
        rope_b = sb("rope_b", [P, 2 * P], F32)
        rope_tab = sb("rope_tab", [P, 2, NT, 2, HD], F32)
        qkT = sb("qkT", [P, 2, 2, S], F32)
        v_next = sb("v_next", [P, EARLY, P], F32)
        v_now = sb("v_now", [P, NT, P], F32)
        probs = sb("probs", [P, GH, S], F32)
        probsT = sb("probsT", [P, NT, GH, P], F32)
        nmax = sb("nmax", [P, HU], F32)
        sums = sb("sums", [P, HU], F32)
        rinv = sb("rinv", [P, GH], F32)
        rinv_wide = sb("rinv_wide", [P, GH, HD], F32)
        rinvT = sb("rinvT", [P, P], F32)
        attnT = sb("attnT", [P, S], F32)
        mask = sb("mask", [P, P], BF16)
        ident16 = sb("ident16", [P, P], BF16)
        sel = sb("sel", [P, B], F32)
        c_rows = sb("c_rows", [B * KT, P], F32)
        c_e = sb("c_e", [P, B * KT], F32)
        c_e1 = sb("c_e1", [P, B * KT], F32)
        c_sig = sb("c_sig", [P, B * KT], F32)
        c_pad = v_now[:, 0:2, :].rearrange("p a (k b) -> p (a k) b", b=HD)
        w_flat = w_raw[:, :, :, :].rearrange("p k j n -> p (k j n)")
        xb = [x_start[:, :, :], w_flat[:, 0:2 * D].rearrange("p (a n) -> p a n", a=2)]
        ht = [h_start[:, :, :],
              w_flat[:, 2 * D:3 * D].rearrange("p (a n) -> p a n", a=2)]
        wm_buf = [probs[:, :, :].rearrange("p h s -> p (h s)").rearrange("p (k n) -> p k n", k=KT),
                  probsT[:, :, :, :].rearrange("p k h q -> p k (h q)")]
        wm_buf += [wm_more[:, a] for a in range(2)]
        wo_raw = [w_flat[:, i * D:(i + 1) * D] for i in range(3)]
        mod_part = attnT[:, 0:BANK]
        mod_rows_sb = [qkT[0:B, 0, :, :].rearrange("p a s -> p (a s)")[:, k * BANK:(k + 1) * BANK]
                       for k in range(FIRST_MOD)] + [attnT[0:B, BANK:2 * BANK]] * (MODC - FIRST_MOD)
        gate_sign = v_now[0:B, 4:8, :].rearrange("p a n -> p (a n)")
        phase_a.close()

        phase_b = ExitStack()

        def sb2(name, shape, dt):
            return phase_b.enter_context(nc.sbuf_tensor(name, shape, dt))

        wo_hi = sb2("wo_hi", [P, KT, D], F32R)
        wb_hi = sb2("wb_hi", [P, KT, D], F32R)
        wo_lo = sb2("wo_lo", [P, KT, D], F32R)
        wb_lo = sb2("wb_lo", [P, KT, D], F32R)
        gb = sb2("gb", [P, B, D], F32)
        bias = sb2("bias", [P, D], F32)
        spare = sb2("spare", [P, D], F32)
        a_raw = sb2("a_raw", [P, KT, P], F32)
        a_hi = sb2("a_hi", [P, KT, P], F32R)
        a_lo = sb2("a_lo", [P, KT, P], F32R)
        ag_hi = sb2("ag_hi", [P, KT, AGW], F32R)
        ag_lo = sb2("ag_lo", [P, KT, AGW], F32R)
        bt_hi = sb2("bt_hi", [P, D], F32R)
        bt_lo = sb2("bt_lo", [P, D], F32R)
        ga = sb2("ga", [P, B, D], F32)
        x1 = sb2("x1", [P, 2, D], F32)
        xn = sb2("xn", [P, D], F32)
        h2t = sb2("h2t", [P, BANK], F32)
        h2_hi = sb2("h2_hi", [P, KT, P], F32R)
        h2_lo = sb2("h2_lo", [P, KT, P], F32R)
        gsm = sb2("gsm", [P, 48], F32)
        bthr = sb2("bthr", [P, 2], F32)
        ag_out = sb2("ag_out", [P, AGW], F32)
        hw = sb2("hw", [P, E_, R_], F32)
        hwT_hi = sb2("hwT_hi", [P, P], F32R)
        hwT_lo = sb2("hwT_lo", [P, P], F32R)
        stage = [gb[:, 0, :], gb[:, 1, :], bias[:, :], spare[:, :]]
        phase_b.close()

        const_ld = sem("const_ld")
        rope_ld = sem("rope_ld")
        c_t = sem("c_t")
        c_ex = sem("c_ex")
        c_done = sem("c_done")
        wm_ld = [sem(f"wm_ld{i}") for i in range(FIRST_MOD)]
        mod_mm = sem("mod_mm")
        mod_ev = sem("mod_ev")
        mod_sum = sem("mod_sum")
        mod_rw = sem("mod_rw")
        mod_st = sem("mod_st")
        mcol_ld = sem("mcol_ld")
        mcol_t = sem("mcol_t")
        mcol = sem("mcol")
        ln_x = [sem("ln_x0"), sem("ln_x1")]
        ln_st = sem("ln_st")
        ln_rs = sem("ln_rs")
        ln_xn = sem("ln_xn")
        ln_tr = sem("ln_tr")
        ln_tt = [sem("ln_tt0"), sem("ln_tt1")]
        ln_raw = [sem("ln_raw0"), sem("ln_raw1")]
        ln_hi = sem("ln_hi")
        ln_lo = sem("ln_lo")
        w_ld = sem("w_ld")
        w_hi_ok = sem("w_hi_ok")
        w_lo_ok = sem("w_lo_ok")
        w_used = sem("w_used")
        qkv_mm = sem("qkv_mm")
        qkv_cp = sem("qkv_cp")
        rope_b_ok = sem("rope_b_ok")
        roped = sem("roped")
        qk_t = sem("qk_t")
        qk_hi = sem("qk_hi")
        qk_lo = sem("qk_lo")
        stacked = [[sem(f"stacked_{half}_h{h}") for h in range(GH)] for half in ("first", "second")]
        v_cp = sem("v_cp")
        v_ok = sem("v_ok")
        s_ok = sem("s_ok")
        max_ok = sem("max_ok")
        exp_ok = sem("exp_ok")
        t_ok = sem("t_ok")
        ev = {"dve": sem("ev_dve"), "act": sem("ev_act")}
        rinv_ok = sem("rinv_ok")
        pv_ok = sem("pv_ok")
        rinvT_ok = sem("rinvT_ok")
        at_ok = sem("at_ok")
        at_st = sem("at_st")
        pool_seq = sem("pool_seq")
        dve_seq = sem("dve_seq")
        inv_ok = sem("inv_ok")
        pool_half = sem("pool_half")
        pool_ve = sem("pool_ve")
        st_ld = [sem(f"st_ld{i}") for i in range(4)]
        wo_ld = [sem(f"wo_ld{i}") for i in range(3)]
        wo_hi_ok = sem("wo_hi_ok")
        wo_lo_ok = sem("wo_lo_ok")
        st_t = sem("st_t")
        st_hi = sem("st_hi")
        st_lo = sem("st_lo")
        rows_ld = sem("rows_ld")
        late_ld = sem("late_ld")
        rows_ok = sem("rows_ok")
        mcol2_ld = sem("mcol2_ld")
        mcol2_t = sem("mcol2_t")
        a_ld = sem("a_ld")
        a_hi_ok = sem("a_hi_ok")
        a_lo_ok = sem("a_lo_ok")
        x_ld = [sem("x_ld0"), sem("x_ld1")]
        wo_ok = sem("wo_ok")
        gated = sem("gated")
        x1_ok = sem("x1_ok")
        bn_ok = sem("bn_ok")
        b_st = sem("b_st")
        b_ve = sem("b_ve")
        b_rs = sem("b_rs")
        xn_ok = sem("xn_ok")
        xt_ok = sem("xt_ok")
        h2t_ok = sem("h2t_ok")
        h2_hi_ok = sem("h2_hi_ok")
        h2_lo_ok = sem("h2_lo_ok")
        ag_ok = sem("ag_ok")
        ag_cp = sem("ag_cp")
        gate_max = sem("gate_max")
        gate_exp = sem("gate_exp")
        gate_seq = sem("gate_seq")
        hw_ok = sem("hw_ok")
        hwT_ok = sem("hwT_ok")
        hwT_hi_ok = sem("hwT_hi_ok")
        hwT_lo_ok = sem("hwT_lo_ok")
        y_ok = sem("y_ok")
        y_ev = sem("y_ev")
        y_gated = sem("y_gated")
        out_ok = sem("out_ok")
        last_y = sem("last_y")
        last_ok = sem("last_ok")
        out_st = sem("out_st")
        STACKING = 3 * 16

        seq = {"dve": 0, "pool": 0}

        items = [("ag", 0), ("ag", 1), ("bt", 0)] + [("wb", o) for o in range(KT)]
        n_dma = {"bt": E_}
        loaded, units_to, unit = [], [], 0
        for kind, k in items:
            n = 1 + AGW - ER - E_ if (kind, k) == ("ag", 1) else n_dma.get(kind, 1)
            loaded.append((loaded[-len(stage)] if len(loaded) >= len(stage) else 0) + 16 * n)
            unit += 2
            units_to.append(unit)
        UNITS = unit
        GATE_STEPS = 8

        def piece(kind, k, half):
            ks = slice(4 * half, 4 * half + 4)
            if kind == "wb":
                return tuple(w[:, ks, k * P:(k + 1) * P] for w in (wb_hi, wb_lo))
            if kind == "bt":
                return tuple(w[:, half * BANK:(half + 1) * BANK].rearrange("p (k n) -> p k n", k=4)
                             for w in (bt_hi, bt_lo))
            return tuple(w[:, ks, slice(0, ER) if k == 0 else slice(ER, AGW)] for w in (ag_hi, ag_lo))

        def piece_cols(kind, k):
            return AGW - ER if (kind, k) == ("ag", 1) else P

        parts = [slice(0, 4), slice(4, 6), slice(6, len(items))]
        turn_bank = [ps_t[0], ps_t[1], ps_qkv, ps_pv]

        def turned(part):
            for i, (kind, k) in list(enumerate(items))[parts[part]]:
                for half in range(2):
                    n = 2 * i + half
                    yield n, i, kind, k, half, turn_bank[n % len(turn_bank)]

        def tile_of(hp, e):
            return hp * 2 + e

        def after(hp, e):
            return (hp, 1) if e == 0 else (hp + 1, 0)

        def tile_loops(eng, body):
            half = NT // 2
            for b in range(B):
                with eng.Fori(0, half - 1) as p:
                    for e in range(2):
                        body(p + b * half, e, b, b, True, True)
                hp = (b + 1) * half - 1
                for e in range(2):
                    i = 2 * hp + e
                    body(hp, e, b, min(B - 1, (i + 1) // NT), i + 1 < B * NT, i + 2 < B * NT)

        def load_piece(sp, i):
            kind, k = items[i]
            to, ld = stage[i % len(stage)], st_ld[i % len(stage)]
            if kind == "wb":
                sp.dma_start(to, W_base[k * P:(k + 1) * P, :]).then_inc(ld, 16)
            elif kind == "bt":
                v = to.rearrange("p (t e r) -> p t e r", t=KT, e=E_)
                for e in range(E_):
                    sp.dma_start(v[:, :, e, :], B_w[e].rearrange("(t p) r -> p t r", p=P)).then_inc(ld, 16)
            elif k == 0:
                sp.dma_start(to, A_w.rearrange("e r d -> (e r) d")).then_inc(ld, 16)
            else:
                sp.dma_start(to[0:E_, :], W_gate).then_inc(ld, 16)
                for r in range(E_, AGW - ER):
                    sp.dma_start(to[r:r + 1, :], W_thr.rearrange("(a d) -> a d", a=1)).then_inc(ld, 16)

        def load_early(sp):
            for h in range(GH):
                sp.wait_ge(stacked[1][h], STACKING * B * G)
            sp.wait_ge(v_cp, NT * B * G)
            for i in range(len(stage)):
                load_piece(sp, i)

        def load_a(sp, i):
            sp.dma_start(a_raw[:, :, :], attn_dram.rearrange("(k p) t -> p k t", p=P)[
                :, :, bass.ds(i * P, P)]).then_inc(a_ld, 16)

        def phase_b_sync(sp):
            def load_pieces(some):
                for i in some:
                    sp.wait_ge(st_lo, units_to[i - len(stage)])
                    load_piece(sp, i)

            def load_x(i, e):
                sp.dma_start(x1[:, e, :], x_rows[bass.ds(i * P, P), :]).then_inc(x_ld[e], 16)

            sp.wait_ge(a_lo_ok, 1)
            load_a(sp, 1)
            for b in range(B):
                sp.dma_start(ga[:, b, :], mod_dram[b:b + 1, 2 * D:3 * D].broadcast_to([P, D])).then_inc(rows_ld, 16)
            sp.dma_start(bthr[:, 0:1], b_thr.rearrange("(a d) -> a d", a=1).broadcast_to([P, 1])).then_inc(rows_ld, 16)
            load_x(0, 0)
            load_pieces(range(len(stage), len(items)))
            load_x(1, 1)
            sp.wait_ge(at_st, 16 * (B * G + 2))
            sp.wait_ge(st_lo, UNITS)
            for b in range(B):
                sp.dma_start(gb[:, b, :], mod_dram[b:b + 1, 5 * D:6 * D].broadcast_to([P, D])).then_inc(late_ld, 16)
            sp.dma_start(bias[:, :], b_base.rearrange("(a d) -> a d", a=1).broadcast_to([P, D])).then_inc(late_ld, 16)

            def body(hp, e, b, bj, has_next, has_next2):
                i = tile_of(hp, e)
                if has_next2:
                    sp.wait_ge(a_lo_ok, i + 2)
                    load_a(sp, i + 2)
                sp.wait_ge(out_ok, i + 2)
                if not has_next:
                    sp.wait_ge(last_ok, 1)
                sp.dma_start(out_rows[bass.ds(i * P, P), :], x1[:, e, :]).then_inc(out_st, 16)
                if has_next2:
                    sp.wait_ge(out_st, 16 * i + 16)
                    load_x(i + 2, e)

            tile_loops(sp, body)
            sp.wait_ge(out_st, 16 * B * NT)

        def phase_b_tensor(pe):
            pe.wait_ge(mcol2_ld, 32)
            pe.wait_ge(at_ok, 8 * B * G + 1)
            pe.transpose(ps_pv[:, 0:4 * KT], mcol_rows[:, :], ident[0:4 * KT, 0:4 * KT]).then_inc(mcol2_t, 1)
            def turn_weights(part):
                for n, i, kind, k, half, bank in turned(part):
                    if n == 0:
                        pe.wait_ge(ev["dve"], EVAC["dve"] * B * G + 1)
                        pe.wait_ge(ev["act"], EVAC["act"] * B * G + 1)
                        pe.wait_ge(qkv_cp, NT * B * G)
                        pe.wait_ge(mcol, 2)
                    if half == 0:
                        pe.wait_ge(st_ld[i % len(stage)], loaded[i])
                    if n >= len(turn_bank):
                        pe.wait_ge(st_lo, n - len(turn_bank) + 1)
                    rows = piece_cols(kind, k)
                    for j in range(4):
                        kt = 4 * half + j
                        mm = pe.transpose(bank[:, j * rows:(j + 1) * rows], stage[i % len(stage)][0:rows, kt * P:(kt + 1) * P], ident[0:rows, 0:rows])
                    mm.then_inc(st_t, 1)

            def three(out_ap, hi, lo, w_hi_ap, w_lo_ap, first, final):
                pe.matmul(out_ap, hi, w_hi_ap, start=first, stop=False)
                pe.matmul(out_ap, hi, w_lo_ap, start=False, stop=False)
                return pe.matmul(out_ap, lo, w_hi_ap, start=False, stop=final)

            def project(j, between=None):
                pe.wait_ge(a_hi_ok, j + 1)
                pe.wait_ge(a_lo_ok, j + 1)
                if not isinstance(j, int) or j:
                    pe.wait_ge(gated, j)
                for c in range(0, D, BANK):
                    if c and between is not None:
                        between()
                    for kt in range(KT):
                        mm = three(ps_s[0][:, c:c + BANK], a_hi[:, kt, :], a_lo[:, kt, :], wo_hi[:, kt, c:c + BANK],
                                   wo_lo[:, kt, c:c + BANK], kt == 0, kt == KT - 1)
                mm.then_inc(wo_ok, 1)

            def turn_xn(j):
                pe.wait_ge(xn_ok, j + 1)
                if not isinstance(j, int) or j:
                    pe.wait_ge(h2t_ok, 2 * j)
                for half in range(2):
                    for q in range(4):
                        kt = 4 * half + q
                        mm = pe.transpose(ps_t[half][:, q * P:(q + 1) * P], xn[:, kt * P:(kt + 1) * P], ident[:, :])
                    mm.then_inc(xt_ok, 1)

            def body(hp, e, b, bj, has_next, has_next2):
                i = tile_of(hp, e)
                pe.wait_ge(h2_hi_ok, 2 * i + 2)
                pe.wait_ge(h2_lo_ok, 2 * i + 2)
                pe.wait_ge(ag_cp, i + 1)
                pe.wait_ge(y_ev, i + 1)
                for c in range(0, D, BANK):
                    for kt in range(KT):
                        hi, lo, cols = h2_hi[:, kt, :], h2_lo[:, kt, :], slice(c, c + BANK)
                        passes = [(hi, wb_hi, ag_hi), (hi, wb_lo, ag_lo), (lo, wb_hi, ag_hi)]
                        for n, (h, w, a) in enumerate(passes):
                            pe.matmul(ps_s[1][:, cols], h, w[:, kt, cols], start=(kt == 0 and n == 0), stop=False)
                            if c == 0:
                                mm = pe.matmul(ps_qkv[:, 0:AGW], h, a[:, kt, :], start=(kt == 0 and n == 0),
                                               stop=(kt == KT - 1 and n == 2))
                    if c == 0:
                        mm.then_inc(ag_ok, 1)
                pe.wait_ge(hw_ok, i + 2)
                pe.wait_ge(hwT_lo_ok, i + 1)
                pe.transpose(ps_pv[:, 0:P], hw[:, :, :].rearrange("p e r -> p (e r)"), ident[:, :]).then_inc(hwT_ok, 1)
                if has_next:
                    turn_xn(i + 1)
                pe.wait_ge(hwT_hi_ok, i + 1)
                pe.wait_ge(hwT_lo_ok, i + 2)
                for c in range(0, D, BANK):
                    mm = three(ps_s[1][:, c:c + BANK], hwT_hi[:, :], hwT_lo[:, :], bt_hi[:, c:c + BANK],
                               bt_lo[:, c:c + BANK], False, True)
                mm.then_inc(y_ok, 1)
                if has_next2:
                    project(i + 2)

            pe.wait_ge(wo_hi_ok, KT)
            pe.wait_ge(wo_lo_ok, KT)
            pe.wait_ge(max_ok, HU * B * G)
            pe.wait_ge(exp_ok, HU * B * G + 2)
            project(0, lambda: turn_weights(0))
            turn_weights(1)

            def rest_and_xn():
                turn_weights(2)
                pe.wait_ge(st_hi, UNITS)
                pe.wait_ge(st_lo, UNITS)
                turn_xn(0)

            project(1, rest_and_xn)
            tile_loops(pe, body)

        def split_a(act, i):
            act.wait_ge(a_ld, 16 * i + 16)
            if not isinstance(i, int) or i:
                act.wait_ge(wo_ok, i)
            act.copy(a_hi[:, :, :], a_raw[:, :, :]).then_inc(a_hi_ok, 1)

        def phase_b_scalar(act):
            def split_h(j):
                for half in range(2):
                    act.wait_ge(h2t_ok, 2 * j + half + 1)
                    act.copy(h2_hi[:, 4 * half:4 * half + 4, :],
                             h2t[:, :].rearrange("p (k t) -> p k t", k=4)).then_inc(h2_hi_ok, 1)

            def body(hp, e, b, bj, has_next, has_next2):
                i = tile_of(hp, e)
                act.wait_ge(ag_cp, i + 2)
                act.activation(gsm[:, 9:10], ag_out[:, ER + E_:ER + E_ + 1], ACT.Exp, bias=bthr[:, 1:2],
                               scale=-1.0).then_inc(gate_exp, 1)
                act.wait_ge(gate_max, i + 1)
                act.activation(gsm[:, 0:E_], ag_out[:, ER:ER + E_], ACT.Exp, bias=gsm[:, 8:9], scale=1.0,
                               accum_out=gsm[:, 10:11]).then_inc(gate_exp, 1)
                if has_next2:
                    split_a(act, i + 2)
                act.wait_ge(hwT_ok, i + 1)
                act.copy(hwT_hi[:, :], ps_pv[:, 0:P]).then_inc(hwT_hi_ok, 1)
                if has_next:
                    split_h(i + 1)

            def split_weights(part):
                for n, i, kind, k, half, bank in turned(part):
                    rows = piece_cols(kind, k)
                    act.wait_ge(st_t, n + 1)
                    act.copy(piece(kind, k, half)[0], bank[:, 0:4 * rows].rearrange(
                        "p (k n) -> p k n", k=4)).then_inc(st_hi, 1)

            split_weights(0)
            split_a(act, 1)
            split_weights(1)
            split_weights(2)
            split_h(0)
            tile_loops(act, body)

        def phase_b_vector(dve):
            dve.sem_inc(ag_cp, 1)
            dve.sem_inc(hw_ok, 1)
            dve.sem_inc(hwT_lo_ok, 1)
            dve.sem_inc(y_ev, 1)
            dve.wait_ge(mcol2_t, 1)
            dve.tensor_copy(modcol[:, :], ps_pv[:, 0:4 * KT])
            dve.tensor_scalar(modcol1[:, :], ps_pv[:, 0:4 * KT], 1.0, None, ALU.add).then_inc(mcol, 1)

            def residual(j, hp, e, b):
                dve.wait_ge(wo_ok, j + 1)
                if not isinstance(j, int) or j:
                    dve.wait_ge(xt_ok, 2 * j)
                    dve.wait_ge(out_ok, j)
                dve.tensor_tensor(xn[:, :], ps_s[0][:, :], ga[:, b, :], ALU.mult).then_inc(gated, 1)
                dve.wait_ge(gated, j + 1)
                dve.wait_ge(x_ld[e], 16 * hp + 16)
                dve.tensor_tensor(x1[:, e, :], x1[:, e, :], xn[:, :], ALU.add).then_inc(x1_ok, 1)
                dve.wait_ge(x1_ok, j + 1)
                for c in range(2):
                    st = dve.bn_stats(stats[:, c, :], x1[:, e, c * BANK:(c + 1) * BANK])
                st.then_inc(bn_ok, 1)
                own(dve)
                dve.wait_ge(bn_ok, j + 1)
                dve.bn_aggr(mv[:, :], stats[:, :, :].rearrange("p a s -> p (a s)")).then_inc(b_st, 1)

            def norm(j, e):
                dve.wait_ge(b_rs, j + 1)
                dve.tensor_scalar(xn[:, :], x1[:, e, :], mv[:, 0:1], rstd[:, 0:1], ALU.subtract,
                                  ALU.mult).then_inc(xn_ok, 1)

            def modulate(j, b):
                for half in range(2):
                    dve.wait_ge(xt_ok, 2 * j + half + 1)
                    if half or not isinstance(j, int) or j:
                        dve.wait_ge(h2_hi_ok, 2 * j + half)
                        dve.wait_ge(h2_lo_ok, 2 * j + half)
                    for q in range(4):
                        kt = 4 * half + q
                        o = dve.tensor_scalar(h2t[:, q * P:(q + 1) * P], ps_t[half][:, q * P:(q + 1) * P],
                                              modcol1[:, b * 16 + 8 + kt:b * 16 + 9 + kt],
                                              modcol[:, b * 16 + kt:b * 16 + kt + 1], ALU.mult, ALU.add)
                    o.then_inc(h2t_ok, 1)

            def route(i):
                done = [0]

                def then(ins):
                    done[0] += 1
                    ins.then_inc(gate_seq, 1)
                    dve.wait_ge(gate_seq, i * GATE_STEPS + done[0])

                ex, nm, ue, sm = gsm[:, 0:E_], gsm[:, 8:9], gsm[:, 9:10], gsm[:, 10:11]
                rs, u1, th, t8, ws, wd, rw = (gsm[:, 11 + q:12 + q] for q in range(7))
                ad, w, wn = gsm[:, 18:26], gsm[:, 26:34], gsm[:, 34:42]
                dve.wait_ge(ag_ok, i + 1)
                dve.tensor_copy(ag_out[:, :], ps_qkv[:, 0:AGW]).then_inc(ag_cp, 1)
                dve.wait_ge(ag_cp, i + 2)
                dve.tensor_reduce(nm, ag_out[:, ER:ER + E_], AX_X, ALU.max, negate=True).then_inc(gate_max, 1)
                dve.wait_ge(gate_exp, 2 * i + 1)
                then(dve.tensor_scalar(u1, ue, 1.0, None, ALU.add))
                then(dve.reciprocal(th, u1))
                dve.tensor_scalar(t8, th, MAX_THRESHOLD, None, ALU.mult)
                dve.wait_ge(gate_exp, 2 * i + 2)
                then(dve.reciprocal(rs, sm))
                then(dve.tensor_scalar(ad, ex, rs, t8, ALU.mult, ALU.subtract))
                then(dve.tensor_scalar(w, ad, 0.0, 0.0, ALU.max, ALU.add, accum_out=ws))
                then(dve.scalar_tensor_tensor(wd, ws, 0.0, ws, ALU.is_equal, ALU.add))
                then(dve.reciprocal(rw, wd))
                then(dve.tensor_scalar(wn, w, rw, SCALING, ALU.mult, ALU.mult))
                assert done[0] == GATE_STEPS
                dve.tensor_tensor(hw[:, :, :], ag_out[:, 0:ER].rearrange("p (e r) -> p e r", e=E_),
                                  wn.unsqueeze(2).broadcast_to([P, E_, R_]), ALU.mult).then_inc(hw_ok, 1)

            def body(hp, e, b, bj, has_next, has_next2):
                i = tile_of(hp, e)
                if has_next:
                    residual(i + 1, *after(hp, e), bj)
                route(i)
                if has_next:
                    norm(i + 1, 1 - e)
                dve.wait_ge(hwT_hi_ok, i + 1)
                dve.tensor_tensor(hwT_lo[:, :], ps_pv[:, 0:P], hwT_hi[:, :].bitcast(F32), ALU.subtract)\
                   .then_inc(hwT_lo_ok, 1)
                if has_next:
                    modulate(i + 1, bj)
                dve.wait_ge(out_ok, i + 1)
                dve.wait_ge(y_ok, i + 1)
                if has_next:
                    dve.tensor_tensor(xn[:, :], ps_s[1][:, :], bias[:, :], ALU.add).then_inc(y_ev, 1)
                else:
                    for cols, done in ((slice(0, BANK), y_ev), (slice(BANK, D), last_y)):
                        dve.tensor_tensor(xn[:, cols], ps_s[1][:, cols], bias[:, cols], ALU.add).then_inc(done, 1)
                    dve.wait_ge(last_y, 1)
                    dve.wait_ge(late_ld, 16 * (B + 1))
                    dve.tensor_tensor(xn[:, cols], xn[:, cols], gb[:, b, cols], ALU.mult).then_inc(last_y, 1)
                    dve.wait_ge(last_y, 2)
                    dve.tensor_tensor(x1[:, e, cols], x1[:, e, cols], xn[:, cols], ALU.add).then_inc(last_ok, 1)

            def rest_weights(part):
                for n, i, kind, k, half, bank in turned(part):
                    rows = piece_cols(kind, k)
                    hi, lo = piece(kind, k, half)
                    dve.wait_ge(st_hi, n + 1)
                    dve.tensor_tensor(lo, bank[:, 0:4 * rows].rearrange("p (k n) -> p k n", k=4),
                                      hi.bitcast(F32), ALU.subtract).then_inc(st_lo, 1)

            dve.wait_ge(wo_lo_ok, KT)
            rest_weights(0)
            dve.wait_ge(rows_ld, 16 * (B + 1))
            dve.tensor_scalar(bthr[:, 1:2], bthr[:, 0:1], -1.0, None, ALU.mult).then_inc(rows_ok, 1)
            dve.wait_ge(rows_ok, 1)
            residual(0, 0, 0, 0)
            norm(0, 0)
            rest_weights(1)
            rest_weights(2)
            modulate(0, 0)
            dve.wait_ge(late_ld, 16 * (B + 1))
            tile_loops(dve, body)

        def phase_b_gpsimd(pool):
            pool.sem_inc(out_ok, 1)

            def rsqrt(j):
                pool.wait_ge(b_st, j + 1)
                pool.tensor_tensor(vareps[:, :], mv[:, 1:2], eps[:, :], ALU.add).then_inc(b_ve, 1)
                pool.wait_ge(b_ve, j + 1)
                pool.tensor_tensor(rstd[:, :], vareps[:, :], minus_half[:, :], ALU.pow).then_inc(b_rs, 1)

            def split_a(i):
                pool.wait_ge(a_hi_ok, i + 1)
                pool.tensor_tensor(a_lo[:, :, :], a_raw[:, :, :], a_hi[:, :, :].bitcast(F32),
                                   ALU.subtract).then_inc(a_lo_ok, 1)

            def split_h(j):
                for half in range(2):
                    pool.wait_ge(h2_hi_ok, 2 * j + half + 1)
                    hi = h2_hi[:, 4 * half:4 * half + 4, :]
                    pool.tensor_tensor(h2_lo[:, 4 * half:4 * half + 4, :], h2t[:, :].rearrange("p (k t) -> p k t", k=4),
                                       hi.bitcast(F32), ALU.subtract).then_inc(h2_lo_ok, 1)

            def body(hp, e, b, bj, has_next, has_next2):
                i = tile_of(hp, e)
                if has_next:
                    rsqrt(i + 1)
                if has_next2:
                    split_a(i + 2)
                if has_next:
                    split_h(i + 1)
                pool.wait_ge(y_ev, i + 2)
                cols = slice(0, D if has_next else BANK)
                pool.tensor_tensor(xn[:, cols], xn[:, cols], gb[:, b, cols], ALU.mult).then_inc(y_gated, 1)
                pool.wait_ge(y_gated, i + 1)
                pool.tensor_tensor(x1[:, e, cols], x1[:, e, cols], xn[:, cols], ALU.add).then_inc(out_ok, 1)

            split_a(0)
            split_a(1)
            rsqrt(0)
            split_h(0)
            pool.wait_ge(late_ld, 16 * (B + 1))
            tile_loops(pool, body)

        def own(eng):
            eng.wait_ge(c_t, 1)

        block = outer.enter_context(nc.Block())

        def wm_at(k):
            return k if k < FIRST_MOD else k % 2

        @block.sync
        def _(sp):
            sp.dma_start(ident[:, :], ident_c).then_inc(const_ld, 16)
            sp.dma_start(c_rows[:, :], c_in.rearrange("b (k p) -> (b k) p", p=P)).then_inc(const_ld, 16)
            sp.dma_start(rinvT[:, :], mask_c).then_inc(const_ld, 16)
            sp.dma_start(sel[:, :], sel_c).then_inc(const_ld, 16)

            def load_wmod(k):
                if k >= FIRST_MOD:
                    sp.wait_ge(mod_mm, k - FIRST_MOD + 1 if k < FIRST_MOD + 2 else k - 1)
                i = wm_at(k)
                sp.dma_start(wm_buf[i], wmod.rearrange("(k p) n -> p k n", p=P)[
                    :, :, k * BANK:(k + 1) * BANK]).then_inc(wm_ld[i], 16)

            def load_x(b, tt):
                n = b * NT + tt
                if tt >= 2:
                    sp.wait_ge(ln_tr, 2 * (n - 1))
                elif b:
                    sp.wait_ge(w_hi_ok, 4 * (G * b + 1))
                    sp.wait_ge(w_lo_ok, 4 * (G * b + 1))
                sp.dma_start(xb[b][:, tt % 2, :], x_rows[n * P:(n + 1) * P, :]).then_inc(ln_x[tt % 2], 16)

            def load_w(it, g):
                if not isinstance(it, int) or it > 0:
                    sp.wait_ge(w_hi_ok, 4 * it)
                    sp.wait_ge(w_lo_ok, 4 * it)
                for j, w in enumerate((wq, wk, wv)):
                    sp.dma_start(w_raw[:, :, j, :], w.rearrange("(k p) n -> p k n", p=P)[
                        :, :, bass.ds(g * P, P)]).then_inc(w_ld, 16)

            def stack(half):
                cols = slice(half * (S // 2), (half + 1) * (S // 2))
                for h in range(GH):
                    parts = qkT[h * HD:(h + 1) * HD, :, :, cols].rearrange("p j a s -> p (j a) s")
                    for r, pair in enumerate((slice(0, 3, 2), slice(1, 3), slice(0, 4, 3))):
                        sp.dma_start(qk_stack[r * HD:(r + 1) * HD, :, h, cols].bitcast(F32), parts[:, pair, :])\
                          .then_inc(stacked[half][h], 16)

            def stack_half(it, half):
                own(sp)
                if not isinstance(it, int) or it:
                    sp.wait_ge(s_ok, HU * it)
                sp.wait_ge(qk_hi, 8 * it + 4 * half + 4)
                sp.wait_ge(qk_lo, 8 * it + 4 * half + 4)
                stack(half)

            def store_attn(it, b, g, t0=0, t1=NT):
                sp.wait_ge(at_ok, 8 * it + t1 + 1)
                sp.dma_start(attn_dram[bass.ds(g * P, P), b * S + t0 * P:b * S + t1 * P],
                             attnT[:, t0 * P:t1 * P]).then_inc(at_st, 16)

            def store_mod(k):
                sp.wait_ge(mod_rw, k + 1)
                sp.dma_start(mod_dram[:, k * BANK:(k + 1) * BANK], mod_rows_sb[k]).then_inc(mod_st, 16)

            load_wmod(0)
            load_x(0, 0)
            load_wmod(1)
            load_x(0, 1)
            load_wmod(2)
            load_wmod(3)
            load_w(0, 0)
            sp.dma_start(rope_tab[:, :, :, :, :], rope_c).then_inc(rope_ld, 16)
            load_wmod(4)
            load_wmod(5)
            for k in range(FIRST_MOD):
                store_mod(k)
            sp.wait_ge(mod_st, 16 * FIRST_MOD)
            for b in range(B):
                sp.dma_start(mcol_rows[b * 16:(b + 1) * 16, :], mod_dram[b, 0:2 * D].rearrange(
                    "(r p) -> r p", p=P)).then_inc(mcol_ld, 16)
            for i in range(NT):
                if i + 2 < NT:
                    load_x(0, i + 2)
                if i + 6 < MODC:
                    load_wmod(i + 6)
                store_mod(i + FIRST_MOD)
                if i == 2:
                    load_w(1, 1)
            sp.wait_ge(ln_hi, 2 * NT)
            sp.wait_ge(ln_lo, 2 * NT)
            sp.wait_ge(ln_tr, 2 * NT)
            stack_half(0, 0)
            sp.wait_ge(mod_st, 16 * MODC)
            for b in range(B):
                sp.dma_start(mcol_rows[b * 16:(b + 1) * 16, :], mod_dram[b, 3 * D:5 * D].rearrange(
                    "(r p) -> r p", p=P)).then_inc(mcol2_ld, 16)
            for b in range(B):
                it0 = b * G

                def stores(it, g, following):
                    stack_half(it, 1)
                    if following is not None:
                        load_w(it + 2, following)
                    stack_half(it + 1, 0)
                    store_attn(it, b, g)

                with sp.Fori(0, G - 2) as g:
                    stores(g + it0, g, g + 2)
                stores(it0 + G - 2, G - 2, None if b else 0)

                def load_wo(k):
                    if k >= 3:
                        sp.wait_ge(wo_lo_ok, k - 2)
                    sp.dma_start(wo_raw[k % 3], wo[k * P:(k + 1) * P, :]).then_inc(wo_ld[k % 3], 16)

                if b:
                    sp.wait_ge(w_hi_ok, 4 * B * G)
                    sp.wait_ge(w_lo_ok, 4 * B * G)
                    for k in range(3):
                        load_wo(k)
                if b == 0:
                    load_x(1, 0)
                    load_x(1, 1)
                stack_half(it0 + G - 1, 1)
                if b:
                    load_early(sp)
                if b == 0:
                    for tt in range(2, NT):
                        load_x(1, tt)
                    sp.wait_ge(ln_hi, 2 * NT * B)
                    sp.wait_ge(ln_lo, 2 * NT * B)
                    load_w(G + 1, 1)
                    stack_half(G, 0)
                if b:
                    for k in range(3, KT):
                        load_wo(k)
                    store_attn(it0 + G - 1, b, G - 1, 0, NT // 2)
                    sp.wait_ge(at_st, 16 * (B * G + 1))
                    load_a(sp, 0)
                store_attn(it0 + G - 1, b, G - 1, NT // 2 if b else 0)
            phase_b_sync(sp)

        @block.tensor
        def _(pe):
            pe.wait_ge(const_ld, 64)
            pe.transpose(ps_pv[:, 0:B * KT], c_rows[:, :], ident[0:B * KT, 0:B * KT]).then_inc(c_t, 1)

            def mod_chunk(k):
                if k == 0:
                    pe.wait_ge(c_done, 2)
                pe.wait_ge(wm_ld[wm_at(k)], 16 if k < FIRST_MOD else 16 * ((k - FIRST_MOD) // 2 + 2))
                if k:
                    pe.wait_ge(mod_ev, k)
                for kt in range(KT):
                    j = kt % 4
                    mm = pe.matmul(ps_s[0][j * HD:(j + 1) * HD, 0:BANK], c_pad[:, kt, :], wm_buf[wm_at(k)][:, kt, :],
                                   start=(kt < 4), stop=(kt >= 4), tile_position=(0, j * HD))
                mm.then_inc(mod_mm, 1)

            def mod_rows(k):
                pe.wait_ge(mod_ev, k + 1)
                if k:
                    pe.wait_ge(mod_rw, k)
                pe.matmul(ps_pv[0:B, 0:BANK], sel[:, :], mod_part, start=True, stop=True).then_inc(mod_sum, 1)

            def ln_half(b, tt, half, bank):
                n = b * NT + tt
                pe.wait_ge(ln_xn, n + 1)
                for j in range(4):
                    kt = 4 * half + j
                    mm = pe.transpose(bank[:, j * P:(j + 1) * P], xb[b][:, tt % 2, kt * P:(kt + 1) * P], ident[:, :])
                mm.then_inc(ln_tr, 1)

            def qkv(it, tt, kts, b=None):
                if kts[0] == 0:
                    if b is not None:
                        pe.wait_ge(ln_hi, 2 * (b * NT + tt + 1))
                        pe.wait_ge(ln_lo, 2 * (b * NT + tt + 1))
                    if not isinstance(it, int) or it or tt:
                        pe.wait_ge(qkv_cp, 8 * it + tt)
                for kt in kts:
                    if tt == 0 and kt % 2 == 0:
                        pe.wait_ge(w_hi_ok, 4 * it + kt // 2 + 1)
                        pe.wait_ge(w_lo_ok, 4 * it + kt // 2 + 1)
                    hh, hl = (h[:, kt, tt * P:(tt + 1) * P] for h in (hT_hi, hT_lo))
                    pe.matmul(ps_qkv[:, 0:3 * P], hh, w_hi[:, kt, :], start=(kt == 0), stop=False)
                    pe.matmul(ps_qkv[:, 0:3 * P], hh, w_lo[:, kt, :], start=False, stop=False)
                    mm = pe.matmul(ps_qkv[:, 0:3 * P], hl, w_hi[:, kt, :], start=False, stop=(kt == KT - 1))
                    if tt == NT - 1 and kt % 2 and kt < KT - 1:
                        mm.then_inc(w_used, 1)
                if kts[-1] == KT - 1:
                    mm.then_inc(qkv_mm, 1)

            def ring_free(st, r, its):
                it = its[0]
                if r < 2:
                    if not isinstance(it, int) or it:
                        pe.wait_ge(ev["dve"], EVAC["dve"] * it + 1)
                        pe.wait_ge(ev["act"], EVAC["act"] * it + 1)
                    pe.wait_ge(qk_lo, 8 * it + EARLY - 1)
                    return
                was = st.ring[r - 2]
                if was[0] == "qk":
                    pe.wait_ge(qk_lo, 8 * its[was[1]] + was[2] + 1)
                elif was[0] == "norm":
                    pe.wait_ge(ln_raw[was[2]], was[1] + 1)
                else:
                    eng, num = PLAN[was[1:]][:2]
                    pe.wait_ge(ev[eng], EVAC[eng] * it + num + 2)

            def qk_transpose(it_q, tt, bank):
                pe.wait_ge(roped, 16 * it_q + 2 * tt + 2)
                pe.transpose(bank[:, 0:P], qk_rot[:, tt % 2, 0:P], ident[:, :])
                pe.transpose(bank[:, P:2 * P], qk_rot[:, tt % 2, P:2 * P], ident[:, :]).then_inc(qk_t, 1)

            def scores(it, n):
                qt, h = n // GH, n % GH
                if n % (HU // 2) < GH:
                    pe.wait_ge(stacked[n // (HU // 2)][h], STACKING * (it + 1))
                pe.wait_ge(exp_ok, HU * it + n + 1)
                w = (qt + 1) * P
                for c0 in range(0, w, BANK):
                    c1 = min(w, c0 + BANK)
                    pe.matmul(ps_s[n % 2][:, c0:c1], qk_stack[:, 0, h, qt * P:(qt + 1) * P], qk_stack[:, 1, h, c0:c1],
                              start=True, stop=(c1 < w))
                pe.matmul(ps_s[n % 2][:, w - P:w], ident16[:, :], mask[:, :], start=False, stop=True).then_inc(s_ok, 1)

            def turn(st, its, n):
                h = n % GH
                pe.wait_ge(exp_ok, HU * its[0] + n + 1 + 2)
                for c, (k0, m) in enumerate(chunks_of(n)):
                    r = st.place["probs", n, c]
                    ring_free(st, r, its)
                    for j in range(m):
                        mm = pe.transpose(ps_t[r % 2][:, j * P:(j + 1) * P], probs[:, h, (k0 + j) * P:(k0 + j + 1) * P],
                                          ident[:, :])
                    mm.then_inc(t_ok, 1)

            def values(it, u):
                for eng in ("dve", "act"):
                    done = max(num for (n, c), (e, num, *_) in PLAN.items() if e == eng and n // GH <= u)
                    pe.wait_ge(ev[eng], EVAC[eng] * it + done + 2)
                if u == 0:
                    pe.wait_ge(v_ok, 2 * it + 1)
                if u == EARLY - 1:
                    pe.wait_ge(v_ok, 2 * it + 2)
                if u >= EARLY:
                    pe.wait_ge(v_cp, 8 * it + u + 1)
                pe.wait_ge(at_ok, 8 * it + u + 1)
                pe.wait_ge(rinv_ok, 8 * it + u + 1)
                for kt in range(u + 1):
                    for h in range(GH):
                        pe.matmul(ps_pv[h * HD:(h + 1) * HD, 0:P], v_now[:, kt, h * HD:(h + 1) * HD],
                                  probsT[:, kt, h, :], start=(kt == 0), stop=(kt == u), tile_position=(0, h * HD))
                pe.transpose(ps_pv[:, P:2 * P], rinv_wide[:, :, :].rearrange("p h d -> p (h d)"),
                             ident[:, :]).then_inc(pv_ok, 1)

            def attention(st, its):
                it = its[0]
                for n in range(st.last):
                    if n < HU:
                        scores(it, n)
                    if n in st.quarters:
                        for w, tt, q in st.quarters[n]:
                            qkv(its[w], tt, [2 * q, 2 * q + 1], 1 if st.norm and w else None)
                    for tt, what in st.norm.get(n, ()):
                        if what[0] == "turn":
                            r = st.place["norm", tt, what[1]]
                            ring_free(st, r, its)
                            ln_half(1, tt, what[1], ps_t[r % 2])
                    if n in st.qk:
                        w, tt = st.qk[n]
                        r = st.place["qk", w, tt]
                        ring_free(st, r, its)
                        qk_transpose(its[w], tt, ps_t[r % 2])
                    if n >= 6 and (n - 6) % 4 == 0 and (n - 6) // 4 < NT:
                        values(it, (n - 6) // 4)
                    if 0 <= n - 2 < HU:
                        turn(st, its, n - 2)

            for k in range(FIRST_MOD):
                mod_chunk(k)
                if k:
                    mod_rows(k - 1)
            mod_rows(FIRST_MOD - 1)
            pe.wait_ge(mcol_ld, 32)
            pe.wait_ge(mod_rw, 4)
            pe.transpose(ps_pv[:, 0:4 * KT], mcol_rows[:, :], ident[0:4 * KT, 0:4 * KT]).then_inc(mcol_t, 1)

            def first_qk(tt):
                if tt >= 2:
                    pe.wait_ge(qk_lo, tt - 1)
                qk_transpose(0, tt, ps_t[tt % 2])

            for i in range(NT):
                for half in range(2):
                    if i:
                        pe.wait_ge(ln_tt[half], i)
                    ln_half(0, i, half, ps_s[1][:, half * BANK:(half + 1) * BANK])
                mod_chunk(FIRST_MOD + i)
                if i >= 1:
                    qkv(0, i - 1, list(range(KT)), 0)
                if i == 0:
                    pe.wait_ge(mcol, 1)
                mod_rows(FIRST_MOD + i)
                if i >= 2:
                    first_qk(i - 2)
            pe.wait_ge(mod_rw, MODC)
            for b in range(B):
                it0 = b * G
                pe.wait_ge(ln_hi, 2 * NT * (b + 1))
                pe.wait_ge(ln_lo, 2 * NT * (b + 1))
                with pe.Fori(0, G - 1) as g:
                    attention(INNER, (g + it0, g + (it0 + 1)))
                attention(FINAL if b else HANDOVER, (it0 + G - 1, it0 + G))
            phase_b_tensor(pe)

        @block.scalar
        def _(act):
            act.sem_inc(exp_ok, 2)
            act.sem_inc(ev["act"], 1)
            act.wait_ge(c_t, 1)
            act.activation(c_e[:, :], ps_pv[:, 0:B * KT], ACT.Exp, scale=-1.0).then_inc(c_ex, 1)

            def mod_out(k):
                act.wait_ge(mod_mm, k + 1)
                if k:
                    act.wait_ge(mod_sum, k)
                act.copy(mod_part, ps_s[0][:, 0:BANK]).then_inc(mod_ev, 1)

            def ln_split(b, tt, half):
                act.wait_ge(ln_tt[half], b * NT + tt + 1)
                act.copy(hT_hi[:, 4 * half:4 * half + 4, tt * P:(tt + 1) * P],
                         ht[b][:, half, :].rearrange("p (k t) -> p k t", k=4)).then_inc(ln_hi, 1)

            def ln_out(tt, bank):
                n = NT + tt
                act.wait_ge(ln_tr, 2 * n + 2)
                act.wait_ge(ln_lo, 2 * n)
                act.copy(ht[1][:, 1, :], bank[:, 0:BANK]).then_inc(ln_raw[1], 1)

            def ln_scale(tt):
                act.wait_ge(ln_raw[1], tt + 1)
                for kt in range(4):
                    h = ht[1][:, 1, kt * P:(kt + 1) * P]
                    o = act.activation(h, h, ACT.Identity, bias=modcol[:, 20 + kt:21 + kt], scale=modcol1[:, 28 + kt:29 + kt])
                o.then_inc(ln_tt[1], 1)

            def ln_mod(b, tt, bank):
                n = b * NT + tt
                act.wait_ge(ln_tr, 2 * n + 2)
                if n:
                    act.wait_ge(ln_lo, 2 * n)
                for j in range(4):
                    kt = 4 + j
                    o = act.activation(ht[b][:, 1, j * P:(j + 1) * P], bank[:, j * P:(j + 1) * P], ACT.Identity,
                                       bias=modcol[:, b * 16 + kt:b * 16 + kt + 1],
                                       scale=modcol1[:, b * 16 + 8 + kt:b * 16 + 9 + kt])
                o.then_inc(ln_tt[1], 1)

            def split_w(it, q):
                if q == 0:
                    act.wait_ge(w_ld, 48 * (it + 1))
                if not isinstance(it, int) or it:
                    if q < 3:
                        act.wait_ge(w_used, 3 * it - 2 + q)
                    else:
                        act.wait_ge(qkv_mm, 8 * it)
                act.copy(w_hi[:, 2 * q:2 * q + 2, :], w_raw[:, 2 * q:2 * q + 2, :, :].rearrange(
                    "p k j n -> p k (j n)")).then_inc(w_hi_ok, 1)

            def copy_qkv(it, tt):
                act.wait_ge(qkv_mm, 8 * it + tt + 1)
                if not isinstance(it, int) or 8 * it + tt >= 2:
                    act.wait_ge(v_cp, 8 * it + tt - 1)
                act.copy(qkv_sb[:, tt % 2, :], ps_qkv[:, 0:3 * P]).then_inc(qkv_cp, 1)

            def qk_split(it, tt, bank):
                act.wait_ge(qk_t, 8 * it + tt + 1)
                if not isinstance(it, int) or it:
                    if tt % 4 == 0:
                        for h in range(GH):
                            act.wait_ge(stacked[tt // 4][h], STACKING * it)
                act.copy(qkT[:, :, 0, tt * P:(tt + 1) * P].bitcast(F32R),
                         bank[:, 0:2 * P].rearrange("p (j t) -> p j t", j=2)).then_inc(qk_hi, 1)

            def softmax_exp(it, n):
                qt, h = n // GH, n % GH
                w = (qt + 1) * P
                act.wait_ge(max_ok, HU * it + n + 1)
                before = max((PLAN[k][2] + 1 for k in PLAN if k[0] <= n - GH), default=0)
                act.wait_ge(t_ok, TCHUNKS * it + before + 1)
                act.activation(probs[:, h, 0:w], ps_s[n % 2][:, 0:w], ACT.Exp, bias=nmax[:, n:n + 1], scale=1.0,
                               accum_out=sums[:, n:n + 1]).then_inc(exp_ok, 1)

            def evac(it, n, c, bank):
                eng, num, at, k0, m = PLAN[n, c]
                act.wait_ge(t_ok, TCHUNKS * it + at + 2)
                act.wait_ge(pv_ok, 8 * it + n // GH + 1)
                act.copy(probsT[:, k0:k0 + m, n % GH, :],
                         bank[:, 0:m * P].rearrange("p (k q) -> p k q", k=m)).then_inc(ev["act"], 1)

            def attention(st, its):
                it = its[0]
                for n in range(st.last):
                    if n in st.split:
                        split_w(its[1], st.split[n])
                    if n in st.ends:
                        w, tt = st.ends[n]
                        copy_qkv(its[w], tt)
                    if n < HU:
                        softmax_exp(it, n)
                    for tt, what in st.norm.get(n, ()):
                        if what == ("turn", 1):
                            ln_out(tt, ps_t[st.place["norm", tt, 1] % 2])
                        if what == ("scale", 1):
                            ln_scale(tt)
                        if what[0] == "split":
                            ln_split(1, tt, what[1])
                    if n in st.wo:
                        k = st.wo[n]
                        act.wait_ge(wo_ld[k % 3], 16 * (k // 3 + 1))
                        act.wait_ge(qkv_mm, 8 * B * G)
                        act.copy(wo_hi[:, k, :], wo_raw[k % 3]).then_inc(wo_hi_ok, 1)
                    if st.wo and n == HU - 2:
                        split_a(act, 0)
                    if n in st.qk:
                        w, tt = st.qk[n]
                        qk_split(its[w], tt, ps_t[st.place["qk", w, tt] % 2])
                    if n >= 6 and (n - 6) % 4 == 0 and (n - 6) // 4 < NT:
                        act.wait_ge(pv_ok, 8 * it + (n - 6) // 4 + 2)
                        act.copy(rinvT[:, :], ps_pv[:, P:2 * P]).then_inc(rinvT_ok, 1)
                    if 0 <= n - 2 < HU:
                        for c in range(len(chunks_of(n - 2))):
                            if PLAN[n - 2, c][0] == "act":
                                evac(it, n - 2, c, ps_t[st.place["probs", n - 2, c] % 2])

            for k in range(FIRST_MOD):
                mod_out(k)
            for q in range(4):
                split_w(0, q)
            act.wait_ge(mcol, 1)
            for i in range(NT):
                ln_split(0, i, 0)
                ln_mod(0, i, ps_s[1][:, BANK:2 * BANK])
                ln_split(0, i, 1)
                mod_out(FIRST_MOD + i)
                if i >= 1:
                    copy_qkv(0, i - 1)
                if i >= 2:
                    qk_split(0, i - 2, ps_t[i % 2])
            for b in range(B):
                it0 = b * G
                with act.Fori(0, G - 1) as g:
                    attention(INNER, (g + it0, g + (it0 + 1)))
                attention(FINAL if b else HANDOVER, (it0 + G - 1, it0 + G))
            phase_b_scalar(act)

        @block.vector
        def _(dve):
            dve.sem_inc(ev["dve"], 1)
            dve.sem_inc(at_ok, 1)
            dve.sem_inc(t_ok, 1)
            dve.sem_inc(pv_ok, 1)
            dve.sem_inc(at_st, 16)

            def then(ins):
                seq["dve"] += 1
                ins.then_inc(dve_seq, 1)
                dve.wait_ge(dve_seq, seq["dve"])

            dve.memset(c_pad[:, :, :], 0.0).then_inc(dve_seq, 1)
            seq["dve"] += 1
            dve.wait_ge(const_ld, 64)
            dve.tensor_copy(mask[:, :], rinvT[:, :])
            dve.tensor_copy(ident16[:, :], ident[:, :]).then_inc(c_done, 1)
            dve.wait_ge(c_ex, 1)
            then(dve.tensor_scalar(c_e1[:, :], c_e[:, :], 1.0, None, ALU.add))
            then(dve.reciprocal(c_sig[:, :], c_e1[:, :]))
            dve.tensor_tensor(c_pad[:, :, 0:B].rearrange("p k b -> p b k"),
                              ps_pv[:, 0:B * KT].rearrange("p (b k) -> p b k", b=B),
                              c_sig[:, :].rearrange("p (b k) -> p b k", b=B), ALU.mult).then_inc(c_done, 1)

            def mod_store(k):
                dve.wait_ge(mod_sum, k + 1)
                mod_row = mod_rows_sb[k]
                if k > FIRST_MOD:
                    dve.wait_ge(mod_st, 16 * k)
                row = dve.tensor_copy(mod_row, ps_pv[0:B, 0:BANK])
                if k in GATE_CHUNKS:
                    then(row)
                    then(dve.tensor_scalar(gate_sign, mod_row, 0.0, 2.0, ALU.is_ge, ALU.mult))
                    then(dve.scalar_tensor_tensor(mod_row, gate_sign, -1.0, mod_row, ALU.add, ALU.mult))
                    then(dve.tensor_scalar(gate_sign, gate_sign, -1.0, None, ALU.add))
                    row = dve.scalar_tensor_tensor(mod_row, mod_row, 0.25, gate_sign, ALU.max, ALU.mult)
                row.then_inc(mod_rw, 1)

            def ln_stats(b, tt):
                xt = xb[b][:, tt % 2, :]
                dve.wait_ge(ln_x[tt % 2], 16 * (b * NT // 2 + tt // 2 + 1))
                for i in range(2):
                    st = dve.bn_stats(stats[:, i, :], xt[:, i * BANK:(i + 1) * BANK])
                then(st)
                dve.bn_aggr(mv[:, :], stats[:, :, :].rearrange("p a s -> p (a s)")).then_inc(ln_st, 1)

            def ln_norm(b, tt):
                n = b * NT + tt
                xt = xb[b][:, tt % 2, :]
                dve.wait_ge(ln_st, n + 1)
                dve.wait_ge(ln_rs, n + 1)
                dve.tensor_scalar(xt, xt, mv[:, 0:1], rstd[:, 0:1], ALU.subtract, ALU.mult).then_inc(ln_xn, 1)

            def ln_out(tt, bank):
                n = NT + tt
                dve.wait_ge(ln_tr, 2 * n + 1)
                dve.wait_ge(ln_hi, 2 * n - 1)
                dve.wait_ge(ln_lo, 2 * n - 1)
                dve.tensor_copy(ht[1][:, 0, :], bank[:, 0:BANK]).then_inc(ln_raw[0], 1)

            def ln_scale(tt):
                dve.wait_ge(ln_raw[0], tt + 1)
                for kt in range(4):
                    h = ht[1][:, 0, kt * P:(kt + 1) * P]
                    o = dve.tensor_scalar(h, h, modcol1[:, 24 + kt:25 + kt], modcol[:, 16 + kt:17 + kt], ALU.mult, ALU.add)
                o.then_inc(ln_tt[0], 1)

            def ln_mod(b, tt, bank):
                n = b * NT + tt
                dve.wait_ge(ln_tr, 2 * n + 1)
                if n:
                    dve.wait_ge(ln_hi, 2 * n - 1)
                    dve.wait_ge(ln_lo, 2 * n - 1)
                for kt in range(4):
                    o = dve.tensor_scalar(ht[b][:, 0, kt * P:(kt + 1) * P], bank[:, kt * P:(kt + 1) * P],
                                          modcol1[:, b * 16 + 8 + kt:b * 16 + 9 + kt],
                                          modcol[:, b * 16 + kt:b * 16 + kt + 1], ALU.mult, ALU.add)
                o.then_inc(ln_tt[0], 1)

            def rest_w(it, q):
                dve.wait_ge(w_hi_ok, 4 * it + q + 1)
                ks = slice(2 * q, 2 * q + 2)
                dve.tensor_tensor(w_lo[:, ks, :], w_raw[:, ks, :, :].rearrange("p k j n -> p k (j n)"),
                                  w_hi[:, ks, :].bitcast(F32), ALU.subtract).then_inc(w_lo_ok, 1)

            def qk_rest(it, tt, bank):
                dve.wait_ge(qk_hi, 8 * it + tt + 1)
                dve.tensor_tensor(qkT[:, :, 1, tt * P:(tt + 1) * P].bitcast(F32R),
                                  bank[:, 0:2 * P].rearrange("p (j t) -> p j t", j=2),
                                  qkT[:, :, 0, tt * P:(tt + 1) * P], ALU.subtract).then_inc(qk_lo, 1)

            def rope_sin(it, tt):
                dve.wait_ge(qkv_cp, 8 * it + tt + 1)
                if not isinstance(it, int) or 8 * it + tt:
                    dve.wait_ge(roped, 16 * it + 2 * tt)
                for j in range(2):
                    tab = rope_tab[:, 1, tt, j, :].unsqueeze(1).broadcast_to([P, GH, HD])
                    o = dve.tensor_tensor(rope_b[:, j * P:(j + 1) * P].rearrange("p (h d) -> p h d", h=GH),
                                          qkv_sb[:, tt % 2, j * P:(j + 1) * P].rearrange("p (h d) -> p h d", h=GH),
                                          tab, ALU.mult)
                o.then_inc(rope_b_ok, 1)

            def row_max(it, n):
                w = (n // GH + 1) * P
                dve.wait_ge(s_ok, HU * it + n + 1)
                dve.tensor_reduce(nmax[:, n:n + 1], ps_s[n % 2][:, 0:w], AX_X, ALU.max, negate=True).then_inc(max_ok, 1)

            def evac(it, n, c, bank):
                eng, num, at, k0, m = PLAN[n, c]
                dve.wait_ge(t_ok, TCHUNKS * it + at + 2)
                dve.wait_ge(pv_ok, 8 * it + n // GH + 1)
                dve.tensor_copy(probsT[:, k0:k0 + m, n % GH, :],
                                bank[:, 0:m * P].rearrange("p (k q) -> p k q", k=m)).then_inc(ev["dve"], 1)

            def invert(it, u):
                dve.wait_ge(exp_ok, HU * it + GH * (u + 1) + 2)
                dve.reciprocal(rinv[:, :], sums[:, GH * u:GH * (u + 1)]).then_inc(inv_ok, 1)
                dve.wait_ge(inv_ok, 8 * it + u + 1)
                dve.wait_ge(pv_ok, 8 * it + u + 1)
                dve.tensor_copy(rinv_wide[:, :, :], rinv[:, :].unsqueeze(2).broadcast_to([P, GH, HD]))\
                   .then_inc(rinv_ok, 1)

            def normalise(it, u):
                dve.wait_ge(rinvT_ok, 8 * it + u + 1)
                if u == 0:
                    dve.wait_ge(at_st, 16 * it + 16)
                dve.tensor_tensor(attnT[:, u * P:(u + 1) * P], ps_pv[:, 0:P], rinvT[:, :], ALU.mult).then_inc(at_ok, 1)

            def place_v(it):
                dve.wait_ge(v_cp, 8 * it + EARLY - 1)
                dve.wait_ge(pv_ok, 8 * it + 1)
                dve.tensor_copy(v_now[:, 0:EARLY - 1, :], v_next[:, 0:EARLY - 1, :]).then_inc(v_ok, 1)

            def place_last_v(it):
                dve.wait_ge(v_cp, 8 * it + EARLY)
                dve.tensor_copy(v_now[:, EARLY - 1, :], v_next[:, EARLY - 1, :]).then_inc(v_ok, 1)

            def attention(st, its):
                it = its[0]
                for n in range(st.last):
                    if n == 5:
                        place_v(it)
                    if n == 9:
                        place_last_v(it)
                    if n < HU:
                        row_max(it, n)
                    if n in st.split:
                        rest_w(its[1], st.split[n])
                    for tt, what in st.norm.get(n, ()):
                        if what == "stats":
                            ln_stats(1, tt)
                        elif what == "norm":
                            ln_norm(1, tt)
                        elif what == ("turn", 0):
                            ln_out(tt, ps_t[st.place["norm", tt, 0] % 2])
                        elif what == ("scale", 0):
                            ln_scale(tt)
                    if n in st.qk:
                        w, tt = st.qk[n]
                        qk_rest(its[w], tt, ps_t[st.place["qk", w, tt] % 2])
                    if n >= 7 and (n - 7) % 4 == 0 and (n - 7) // 4 < NT:
                        normalise(it, (n - 7) // 4)
                    if n >= 5 and (n - 5) % 4 == 0 and (n - 5) // 4 < NT:
                        invert(it, (n - 5) // 4)
                    if 0 <= n - 2 < HU:
                        for c in range(len(chunks_of(n - 2))):
                            if PLAN[n - 2, c][0] == "dve":
                                evac(it, n - 2, c, ps_t[st.place["probs", n - 2, c] % 2])
                    if n in st.ends:
                        w, tt = st.ends[n]
                        rope_sin(its[w], tt)

            ln_stats(0, 0)
            for k in range(FIRST_MOD):
                mod_store(k)
            ln_norm(0, 0)
            dve.wait_ge(mcol_t, 1)
            dve.tensor_copy(modcol[:, :], ps_pv[:, 0:4 * KT])
            then(dve.tensor_scalar(modcol1[:, :], ps_pv[:, 0:4 * KT], 1.0, None, ALU.add))
            dve.sem_inc(mcol, 1)
            for q in range(4):
                rest_w(0, q)
            for i in range(NT):
                if i + 1 < NT:
                    ln_stats(0, i + 1)
                ln_mod(0, i, ps_s[1][:, 0:BANK])
                if i + 1 < NT:
                    ln_norm(0, i + 1)
                mod_store(FIRST_MOD + i)
                if i >= 2:
                    qk_rest(0, i - 2, ps_t[i % 2])
                if i == 1:
                    dve.wait_ge(rope_ld, 16)
                if i >= 1:
                    rope_sin(0, i - 1)
            dve.wait_ge(mod_mm, MODC)
            dve.wait_ge(mod_st, 16 * MODC)
            for b in range(B):
                it0 = b * G
                with dve.Fori(0, G - 1) as g:
                    attention(INNER, (g + it0, g + (it0 + 1)))
                attention(FINAL if b else HANDOVER, (it0 + G - 1, it0 + G))
            phase_b_vector(dve)

        @block.gpsimd
        def _(pool):
            pool.memset(eps[:, :], EPS)
            pool.memset(minus_half[:, :], -0.5).then_inc(pool_half, 1)
            pool.wait_ge(pool_half, 1)

            def ln_rstd(b, tt):
                n = b * NT + tt
                pool.wait_ge(ln_st, n + 1)
                pool.tensor_tensor(vareps[:, :], mv[:, 1:2], eps[:, :], ALU.add).then_inc(pool_ve, 1)
                pool.wait_ge(pool_ve, n + 1)
                pool.tensor_tensor(rstd[:, :], vareps[:, :], minus_half[:, :], ALU.pow).then_inc(ln_rs, 1)

            def ln_rest(b, tt, half):
                n = 2 * (b * NT + tt) + half
                pool.wait_ge(ln_hi, n + 1)
                hi = hT_hi[:, 4 * half:4 * half + 4, tt * P:(tt + 1) * P]
                pool.tensor_tensor(hT_lo[:, 4 * half:4 * half + 4, tt * P:(tt + 1) * P],
                                   ht[b][:, half, :].rearrange("p (k t) -> p k t", k=4), hi.bitcast(F32),
                                   ALU.subtract).then_inc(ln_lo, 1)

            def rotate(it, tt):
                if tt == 0 and (not isinstance(it, int) or it):
                    pool.wait_ge(v_ok, 2 * it)
                if tt == EARLY:
                    pool.wait_ge(pv_ok, 8 * it + 1)
                pool.wait_ge(qkv_cp, 8 * it + tt + 1)
                src = qkv_sb[:, tt % 2, :]
                pairs = src[:, 0:2 * P].rearrange("p (j h d) -> p j h d", j=2, h=GH)
                if not isinstance(it, int) or 8 * it + tt:
                    pool.wait_ge(roped, 16 * it + 2 * tt)
                for j in range(2):
                    tab = rope_tab[:, 0, tt, j, :].unsqueeze(1).broadcast_to([P, GH, HD])
                    pool.tensor_tensor(rope_a[:, j * P:(j + 1) * P].rearrange("p (h d) -> p h d", h=GH),
                                       pairs[:, j], tab, ALU.mult).then_inc(pool_seq, 1)
                pool.wait_ge(pool_seq, 2 * (8 * it + tt + 1))
                if not isinstance(it, int) or 8 * it + tt >= 2:
                    pool.wait_ge(qk_t, 8 * it + tt - 1)
                for i, (t, op) in enumerate(((rope_a, ALU.subtract), (rope_b, ALU.add))):
                    if i:
                        pool.wait_ge(rope_b_ok, 8 * it + tt + 1)
                    v = t[:, :].rearrange("p (g i e) -> p g i e", g=2 * GH, e=2)
                    dst = qk_rot[:, tt % 2, :].rearrange("p (g e i) -> p g e i", g=2 * GH, e=2)[:, :, i, :]
                    pool.tensor_tensor(dst, v[:, :, :, 0], v[:, :, :, 1], op).then_inc(roped, 1)
                v_to = v_next if tt < EARLY else v_now
                pool.tensor_copy(v_to[:, tt, :], src[:, 2 * P:3 * P]).then_inc(v_cp, 1)

            def attention(st, its):
                it = its[0]
                for n in range(st.last):
                    for tt, what in st.norm.get(n, ()):
                        if what == "stats":
                            ln_rstd(1, tt)
                    for tt, what in st.norm.get(n, ()):
                        if what[0] == "split":
                            ln_rest(1, tt, what[1])
                    if n in st.ends:
                        w, tt = st.ends[n]
                        rotate(its[w], tt)
                    if n in st.wo:
                        k = st.wo[n]
                        pool.wait_ge(wo_hi_ok, k + 1)
                        pool.tensor_tensor(wo_lo[:, k, :], wo_raw[k % 3], wo_hi[:, k, :].bitcast(F32),
                                           ALU.subtract).then_inc(wo_lo_ok, 1)

            ln_rstd(0, 0)
            for i in range(NT):
                if i + 1 < NT:
                    ln_rstd(0, i + 1)
                ln_rest(0, i, 0)
                ln_rest(0, i, 1)
                if i == 1:
                    pool.wait_ge(rope_ld, 16)
                if i >= 1:
                    rotate(0, i - 1)
            for b in range(B):
                it0 = b * G
                with pool.Fori(0, G - 1) as g:
                    attention(INNER, (g + it0, g + (it0 + 1)))
                attention(FINAL if b else HANDOVER, (it0 + G - 1, it0 + G))
            phase_b_gpsimd(pool)


_INS = ['L0_attn_x', 'L0_attn_wq', 'L0_attn_wk', 'L0_attn_wv', 'L0_attn_wo', 'L0_ffn_W_base', 'L0_ffn_b_base',
        'L0_ffn_W_gate', 'L0_ffn_W_thr', 'L0_ffn_b_thr', 'L0_ffn_A_w', 'L0_ffn_B_w', 'L0_c', 'L0_wmod']


def shape_constants():
    import numpy as np

    inv = 1.0 / 10000.0 ** (np.arange(0, HD, 2).astype(np.float32) / HD)
    f = np.outer(np.arange(S), inv).astype(np.float32)
    cos, sin = np.cos(f), np.sin(f)
    tabs = np.stack([np.stack([cos, sin], -1), np.stack([sin, cos], -1)]).reshape(2, NT, P, HD)
    scale = np.float32(1.0) / np.sqrt(np.float32(HD))
    rope = np.stack([tabs * scale, tabs], 3).transpose(2, 0, 1, 3, 4)
    q, k = np.arange(P)[:, None], np.arange(P)[None, :]
    return {
        "rope": np.ascontiguousarray(rope, np.float32),
        "ident": np.eye(P, dtype=np.float32),
        "mask": np.where(k > q, np.float32(MASKED), np.float32(0)),
        "sel": (np.arange(P)[:, None] % HD == np.arange(B)[None, :]).astype(np.float32),
    }


def kernel(**inputs):
    import numpy as np
    import concourse.bacc as bacc
    from concourse.bass_utils import run_bass_kernel_spmd

    nc = bacc.Bacc("TRN2", target_bir_lowering=False, num_devices=1)
    arrays, args = {}, []
    for name, a in [(n, inputs[n]) for n in _INS] + list(shape_constants().items()):
        a = np.ascontiguousarray(a)
        arrays[f"in_{name}_dram"] = a
        args.append(nc.dram_tensor(f"in_{name}_dram", a.shape, mybir.dt.from_np(a.dtype), kind="ExternalInput").ap())
    args.append(nc.dram_tensor("out_0_dram", (B, S, D), F32, kind="ExternalOutput").ap())
    adaln_block(nc, *args)
    r = run_bass_kernel_spmd(nc, [arrays], core_ids=[0])
    return r.results[0]["out_0_dram"]
```
